# Optimizing a Trainium2 kernel written in Bass

```python
import numpy as np
import jax
import jax.numpy as jnp

def _softmax(x, axis=-1):
    return jax.nn.softmax(x, axis=axis)

def _gelu(x):
    return jax.nn.gelu(x, approximate=True)

def _silu(x):
    return jax.nn.silu(x)

def _sigmoid(x):
    return jax.nn.sigmoid(x)

def _layernorm(x, axis=-1, eps=1e-05):
    m = jnp.mean(x, axis=axis, keepdims=True)
    v = jnp.var(x, axis=axis, keepdims=True)
    return (x - m) / jnp.sqrt(v + eps)

def _scatter_add(tgt, idx, src, axis=0):
    return tgt.at[idx].add(src)

def _segment_sum(src, seg, n):
    return jax.ops.segment_sum(src, seg, n)
kernel_name = 'mk_metaformer_d1_conv_nhwc256_r2_303303'

def setup_inputs(seed: int=0):
    np.random.seed(seed)
    _w = jnp.asarray

    def _rec_inputs():
        import jax
        import jax.numpy as jnp
        _gk = jax.random.key(seed)
        x = 7.22e-05 + 1 * jax.random.normal(jax.random.fold_in(_gk, 1), (1, 64, 128, 128), jnp.float32)
        return x
    x = _rec_inputs()

    def _L0_conv_setup():
        import jax, jax.numpy as jnp
        import numpy as np
        C_Z, H_Z, W_Z, NH, C = (64, 128, 128, 4, 32)
        EPS = 1e-05
        key = jax.random.key(seed)
        ks = jax.random.split(key, 8)
        s = 0.02
        return {'pair_rep': jax.random.normal(ks[0], (1, C_Z, H_Z, W_Z), jnp.float32), 'ln_w': jnp.ones((C_Z, H_Z, W_Z), jnp.float32), 'ln_b': jnp.zeros((C_Z, H_Z, W_Z), jnp.float32), 'wq': jax.random.normal(ks[1], (NH * C, C_Z), jnp.float32) * s, 'wk': jax.random.normal(ks[2], (NH * C, C_Z), jnp.float32) * s, 'wv': jax.random.normal(ks[3], (NH * C, C_Z), jnp.float32) * s, 'wb': jax.random.normal(ks[4], (NH, C_Z), jnp.float32) * s, 'wg_w': jax.random.normal(ks[5], (NH * C, C_Z), jnp.float32) * s, 'wg_b': jnp.zeros((NH * C,), jnp.float32), 'wrep_w': jax.random.normal(ks[6], (C_Z, NH * C), jnp.float32) * s, 'wrep_b': jnp.zeros((C_Z,), jnp.float32)}
    _L0_conv_all = _L0_conv_setup()
    _L0_conv_in = {k: v for k, v in _L0_conv_all.items() if k in ('ln_w', 'ln_b', 'wq', 'wk', 'wv', 'wb', 'wg_w', 'wg_b', 'wrep_w', 'wrep_b')}
    del _L0_conv_all

    def _L0_ffn_setup():
        import jax, jax.numpy as jnp
        import numpy as np
        TOP_K = 2
        key = jax.random.key(seed)
        ks = jax.random.split(key, 4)
        B, L, D, H, E = (8, 2048, 128, 512, 8)
        s = 0.02
        return {'x': jax.random.normal(ks[0], (B, L, D), jnp.float32), 'Wg': jax.random.normal(ks[1], (D, E), jnp.float32) * s, 'bg': jnp.zeros((E,), jnp.float32), 'W1': jax.random.normal(ks[2], (E, D, H), jnp.float32) * s, 'b1': jnp.zeros((E, H), jnp.float32), 'W2': jax.random.normal(ks[3], (E, H, D), jnp.float32) * s, 'b2': jnp.zeros((E, D), jnp.float32)}
    _L0_ffn_all = _L0_ffn_setup()
    _L0_ffn_in = {k: v for k, v in _L0_ffn_all.items() if k in ('Wg', 'bg', 'W1', 'b1', 'W2', 'b2')}
    del _L0_ffn_all
    return {'x': x, 'L0_conv_ln_w': _L0_conv_in['ln_w'], 'L0_conv_ln_b': _L0_conv_in['ln_b'], 'L0_conv_wq': _L0_conv_in['wq'], 'L0_conv_wk': _L0_conv_in['wk'], 'L0_conv_wv': _L0_conv_in['wv'], 'L0_conv_wb': _L0_conv_in['wb'], 'L0_conv_wg_w': _L0_conv_in['wg_w'], 'L0_conv_wg_b': _L0_conv_in['wg_b'], 'L0_conv_wrep_w': _L0_conv_in['wrep_w'], 'L0_conv_wrep_b': _L0_conv_in['wrep_b'], 'L0_ffn_Wg': _L0_ffn_in['Wg'], 'L0_ffn_bg': _L0_ffn_in['bg'], 'L0_ffn_W1': _L0_ffn_in['W1'], 'L0_ffn_b1': _L0_ffn_in['b1'], 'L0_ffn_W2': _L0_ffn_in['W2'], 'L0_ffn_b2': _L0_ffn_in['b2']}

def reference(x, L0_conv_ln_w, L0_conv_ln_b, L0_conv_wq, L0_conv_wk, L0_conv_wv, L0_conv_wb, L0_conv_wg_w, L0_conv_wg_b, L0_conv_wrep_w, L0_conv_wrep_b, L0_ffn_Wg, L0_ffn_bg, L0_ffn_W1, L0_ffn_b1, L0_ffn_W2, L0_ffn_b2):
    import jax
    import jax.numpy as jnp

    def _L0_conv_ref(pair_rep, ln_w, ln_b, wq, wk, wv, wb, wg_w, wg_b, wrep_w, wrep_b):
        import jax, jax.numpy as jnp
        import numpy as np
        C_Z, H_Z, W_Z, NH, C = (64, 128, 128, 4, 32)
        EPS = 1e-05
        B = pair_rep.shape[0]
        mu = jnp.mean(pair_rep, axis=(1, 2, 3), keepdims=True)
        var = jnp.var(pair_rep, axis=(1, 2, 3), keepdims=True)
        x = (pair_rep - mu) * jax.lax.rsqrt(var + EPS) * ln_w + ln_b

        def proj(w):
            y = jnp.einsum('oc,bcij->boij', w, x)
            return y.reshape(B, NH, C, H_Z, W_Z)
        q = proj(wq)
        k = proj(wk)
        v = proj(wv)
        g = jax.nn.sigmoid(proj(wg_w) + wg_b.reshape(1, NH, C, 1, 1))
        bias = jnp.einsum('hc,bcij->bhij', wb, x)
        scale = 1.0 / jnp.sqrt(jnp.float32(C))
        scores = jnp.einsum('bhcij,bhcik->bhijk', q, k) * scale + bias[:, :, None, :, :]
        a = jax.nn.softmax(scores, axis=-1)
        o = g * jnp.einsum('bhijk,bhcik->bhcij', a, v)
        o = o.transpose(0, 2, 1, 3, 4).reshape(B, C * NH, H_Z, W_Z)
        return jnp.einsum('oc,bcij->boij', wrep_w, o) + wrep_b.reshape(1, C_Z, 1, 1)

    def _L0_ffn_ref(x, Wg, bg, W1, b1, W2, b2):
        import jax, jax.numpy as jnp
        import numpy as np
        TOP_K = 2
        B, L, D = x.shape
        E = W1.shape[0]
        xf = x.reshape(-1, D)
        gate_logits = xf @ Wg + bg
        top_w, top_i = jax.lax.top_k(gate_logits, TOP_K)
        top_w = jax.nn.softmax(top_w, axis=-1)
        w_dense = jnp.sum(jax.nn.one_hot(top_i, E, dtype=xf.dtype) * top_w[..., None], axis=1)
        out = jnp.zeros_like(xf)
        for e in range(E):
            h = jax.nn.gelu(xf @ W1[e] + b1[e], approximate=False)
            out = out + w_dense[:, e:e + 1] * (h @ W2[e] + b2[e])
        return out.reshape(B, L, D)

    def _gn(v, G=32, eps=1e-05):
        B_, H_, W_, C_ = v.shape
        g = v.reshape(B_, H_, W_, G, C_ // G)
        m = jnp.mean(g, axis=(1, 2, 4), keepdims=True)
        s = jnp.var(g, axis=(1, 2, 4), keepdims=True)
        return ((g - m) / jnp.sqrt(s + eps)).reshape(v.shape)

    def _ln_c(v, eps=1e-06):
        m = jnp.mean(v, axis=-1, keepdims=True)
        s = jnp.var(v, axis=-1, keepdims=True)
        return (v - m) / jnp.sqrt(s + eps)

    def _ln_t(v, eps=1e-05):
        m = jnp.mean(v, axis=-1, keepdims=True)
        s = jnp.var(v, axis=-1, keepdims=True)
        return (v - m) / jnp.sqrt(s + eps)

    def _to_tokens(v):
        B_, H_, W_, C_ = v.shape
        return v.reshape(B_, H_ * W_, C_)

    def _from_tokens(t, like):
        return t.reshape(like.shape)
    x = x + _L0_conv_ref(_ln_c(x), L0_conv_ln_w, L0_conv_ln_b, L0_conv_wq, L0_conv_wk, L0_conv_wv, L0_conv_wb, L0_conv_wg_w, L0_conv_wg_b, L0_conv_wrep_w, L0_conv_wrep_b)
    t = _to_tokens(x)
    t = t + _L0_ffn_ref(_ln_t(t), L0_ffn_Wg, L0_ffn_bg, L0_ffn_W1, L0_ffn_b1, L0_ffn_W2, L0_ffn_b2)
    x = _from_tokens(t, x)
    return x

_drawn_inputs = setup_inputs


def setup_inputs(seed=0):
    import zlib

    import numpy as np

    out = dict(_drawn_inputs(seed))
    spreads = {'L0_conv_ln_w': (1.0, 0.6),
     'L0_conv_ln_b': (0.0, 0.8),
     'L0_conv_wg_b': (0.0, 0.8),
     'L0_conv_wrep_b': (0.0, 0.1),
     'L0_ffn_bg': (0.0, 0.268),
     'L0_ffn_b1': (0.0, 0.473),
     'L0_ffn_b2': (0.0, 0.1)}
    factors = {'L0_conv_wq': 8.0,
     'L0_conv_wk': 8.0,
     'L0_conv_wv': 8.0,
     'L0_conv_wb': 8.0,
     'L0_conv_wg_w': 8.0,
     'L0_conv_wrep_w': 8.0,
     'L0_ffn_W1': 2.858}
    for name, (base, spread) in spreads.items():
        noise = np.random.default_rng([zlib.crc32(name.encode()), seed]).standard_normal(out[name].shape)
        drawn = base * np.exp(spread * noise) if base else spread * noise
        out[name] = jnp.asarray(drawn.astype(out[name].dtype))
    for name, factor in factors.items():
        out[name] = (out[name] * factor).astype(out[name].dtype)
    return out
```

```python
from contextlib import ExitStack

import concourse.bass as bass
from concourse import mybir

P = 128
F32 = mybir.dt.float32
F32R = mybir.dt.float32r
F16 = mybir.dt.float16
I32 = mybir.dt.int32
ALU = mybir.AluOpType
ACT = mybir.ActivationFunctionType
AX_X = mybir.AxisListType.X

RSQRT_SEED = float(0x5F3759DF)
BIG = 3.0e38


class Chain:

    def __init__(self, engine, sem):
        self.engine, self.sem, self.count = engine, sem, 0

    def link(self, instruction):
        self.count += 1
        instruction.then_inc(self.sem, 1)
        self.engine.wait_ge(self.sem, self.count)


def wait(engine, sem, value):
    if isinstance(value, int) and value <= 0:
        return
    engine.wait_ge(sem, value)


def rsqrt(nc, chain, y, v, a, b):
    seed_bits = a.bitcast(I32)
    chain.link(nc.vector.tensor_scalar(seed_bits, v.bitcast(I32), 1, None, ALU.arith_shift_right))
    chain.link(nc.vector.tensor_scalar(y.bitcast(I32), seed_bits, -1.0, RSQRT_SEED, ALU.mult, ALU.add))
    for _ in range(3):
        chain.link(nc.vector.tensor_tensor(a, y, y, ALU.mult))
        chain.link(nc.vector.scalar_tensor_tensor(b, a, -0.5, v, ALU.mult, ALU.mult))
        chain.link(nc.vector.scalar_tensor_tensor(y, b, 1.5, y, ALU.add, ALU.mult))


def build(nc, x, ln_w, ln_b, wq, wk, wv, wb, wg_w, wg_b, wrep_w, wrep_b, Wg, bg, W1, b1, W2, b2, out):
    _, C, H, W = x.shape
    NH = wb.shape[0]
    HC = wq.shape[0]
    D = HC // NH
    HALF = H // 2
    R = 4
    UNITS = H // R
    NQ = R * W
    ROWSTATS = 6
    CH = 4
    CR = HALF // CH
    E, _, HID = W1.shape
    HB = HID // P
    TOKENS = C * H
    TILE = 256
    TILES = 2 * TOKENS // TILE + E - 1
    SLOTS = TILES * TILE
    ROW = W + 4
    NOWHERE = 1 << 20
    WPIECE = E * HID // UNITS
    assert W == P and H == P and 2 * C == P and HC == P and UNITS % 2 == 0

    with ExitStack() as ctx:
        def sb(name, shape, dt=F32):
            return ctx.enter_context(nc.sbuf_tensor(name, shape, dt))

        def psum(name, shape=(P, 512), dt=F32):
            return ctx.enter_context(nc.psum_tensor(name, list(shape), dt))

        def sem(name):
            return ctx.enter_context(nc.semaphore(name))

        xt = sb("xt", [P, HALF, W])
        lnw_sb = sb("lnw_sb", [P, 2, CR, W])
        lnb_sb = sb("lnb_sb", [P, 2, CR, W])
        identity = sb("identity", [P, P])
        ones = sb("ones", [P, P])
        ones_r = sb("ones_r", [P, P], F32R)
        rowstat = sb("rowstat", [P, HALF, ROWSTATS])
        mean = sb("mean", [P, HALF])
        var = sb("var", [P, HALF])
        rstd = sb("rstd", [P, HALF])
        tmp_a = sb("tmp_a", [P, HALF])
        tmp_b = sb("tmp_b", [P, HALF])
        sums = sb("sums", [P, 8])
        gstat = sb("gstat", [P, 8])
        xsq = sb("xsq", [P, 2 * CH])
        rstd2 = sb("rstd2", [P, HALF])
        gtmp = sb("gtmp", [P, 8])
        gtmp2 = sb("gtmp2", [P, 8])
        grstd = sb("grstd", [P, 1])
        ebits = sb("ebits", [P, 4], I32)
        ebits2 = sb("ebits2", [P, 4], I32)
        scales = sb("scales", [P, 4])
        inv_scales = sb("inv_scales", [P, 4])
        logit_scale = sb("logit_scale", [P, 1])
        bias_scale = sb("bias_scale", [P, 1])
        brep = sb("brep", [P, 1])
        bgrow = sb("bgrow", [1, HC])
        wb_sb = sb("wb_sb", [P, 2 * NH])
        w_raw = [lnw_sb, lnb_sb]
        b1_sb = sb("b1_sb", [P, E, HB])
        b2_row = sb("b2_row", [1, E * P])
        wg_sb = sb("wg_sb", [P, E])
        bgate_row = sb("bgate_row", [1, E])
        wsq = sb("wsq", [P, 2])
        hscale = sb("hscale", [P, 4])
        inv_hscale = sb("inv_hscale", [P, 4])
        y_scale = sb("y_scale", [P, 1])
        order8 = sb("order8", [P, E])
        before = sb("before", [P, P])
        counts = sb("counts", [P, 2 * E])
        tiles_i = sb("tiles_i", [P, E], I32)
        tiles_f = [sb(f"tiles_f{k}", [P, E]) for k in range(3)]
        token_id = sb("token_id", [P, HALF])
        tile_no = sb("tile_no", [1, TILES])
        tile_expert = sb("tile_expert", [1, TILES])
        tile_cmp = sb("tile_cmp", [1, TILES])
        tile_expert_i = sb("tile_expert_i", [1, TILES], I32)
        blank = sb("blank", [P, ROW])
        b1_flat = b1_sb[:].rearrange("p e b -> p (e b)")
        b1_sq = sb("b1_sq", [P, E * HB])
        b1_sum = sb("b1_sum", [P, 1])
        bgate_all = sb("bgate_all", [P, E])
        tiles_j = sb("tiles_j", [P, E], I32)
        first_row = sb("first_row", [P, E])
        first_row2 = sb("first_row2", [P, E])

        attention_memory = ExitStack()

        def sba(name, shape, dt=F32):
            return attention_memory.enter_context(nc.sbuf_tensor(name, shape, dt))

        x1 = sba("x1", [P, HALF, W])
        square_junk = sba("square_junk", [P, CR * W // 2])
        wraw = sba("wraw", [P, 4, 2, C])
        w4 = sba("w4", [P, 4, P])
        w4h = sba("w4h", [P, 4, P], F32R)
        w4l = sba("w4l", [P, 2, 4, P], F32R)
        wrep_raw = sba("wrep_raw", [C, HC])
        wrep_ordered = sba("wrep_ordered", [C, HC])
        wrepT = sba("wrepT", [P, P])
        wrep_h = sba("wrep_h", [P, P], F32R)
        wrep_l = sba("wrep_l", [P, P], F32R)
        bg_f = sba("bg_f", [P, HC])
        bg_h = sba("bg_h", [P, HC], F32R)
        bg_l = sba("bg_l", [P, HC], F32R)
        biasT = sba("biasT", [P, NH, P])
        biasN = sba("biasN", [P, NH, P])
        xf = sba("xf", [P, NQ])
        xs = [sba(f"xs{p}", [P, NQ], F32R) for p in range(2)]
        qk = [[[sba(f"{n}{part}{p}", [P, NQ], F16) for p in range(2)] for part in "hl"] for n in "qk"]
        L = [sba(f"L{p}", [P, NH, R, P]) for p in range(2)]
        lmin = [sba(f"lmin{p}", [P, NH * R]) for p in range(2)]
        ph = [sba(f"ph{p}", [P, NH * P], F16) for p in range(2)]
        pl = [sba(f"pl{p}", [P, NH * P], F16) for p in range(2)]
        vh = [sba(f"vh{p}", [P, R, NH, D + 1], F16) for p in range(2)]
        vl = [sba(f"vl{p}", [P, R, NH, D + 1], F16) for p in range(2)]
        gt = [sba(f"gt{p}", [P, R, HC]) for p in range(2)]
        turn = [sba(f"turn{k}", [P, 1]) for k in range(2)]
        rden = sba("rden", [P, 2, NH])
        on = sba("on", [P, 2, HC])
        og = [sba(f"og{p}", [P, R, HC]) for p in range(2)]
        ogT_h = sba("ogT_h", [P, NQ], F32R)
        ogT_l = sba("ogT_l", [P, NQ], F32R)
        attention_memory.close()

        def sbm(name, shape, dt=F32):
            return ctx.enter_context(nc.sbuf_tensor(name, shape, dt))

        pay = sbm("pay", [P, HALF, ROW])
        w_h = [sbm(f"w{n}_h", [P, E, HB, P], F16) for n in (1, 2)]
        w_l = [sbm(f"w{n}_l", [P, E, HB, P], F16) for n in (1, 2)]
        b2_scaled = sbm("b2_scaled", [1, E * P])
        b2_h = sbm("b2_h", [1, E * P], F32R)
        b2_l = sbm("b2_l", [1, E * P], F32R)
        ones_x = sbm("ones_x", [1, P], F32R)
        stage = [sbm(f"stage{p}", [P, R, P]) for p in range(2)]
        xnT = [sbm(f"xnT{p}", [P, R * P]) for p in range(2)]
        lg = sbm("lg", [P, HALF, E])
        r_a = sbm("r_a", [P, HALF, E])
        r_b = sbm("r_b", [P, HALF, E])
        oh = [sbm(f"oh{k}", [P, HALF, E]) for k in range(2)]
        picked = sbm("picked", [P, HALF, E])
        top = [sbm(f"top{k}", [P, HALF]) for k in range(2)]
        key = sbm("key", [P, HALF])
        gate_e = sbm("gate_e", [P, HALF])
        weight = [sbm(f"weight{k}", [P, HALF]) for k in range(2)]
        posf = sbm("posf", [P, HALF])
        pos = [sbm(f"pos{k}", [P, HALF], I32) for k in range(2)]
        rows_in = [sbm(f"rows_in{p}", [P, 2, ROW]) for p in range(2)]
        fx_h = [sbm(f"fx_h{p}", [P, TILE], F16) for p in range(2)]
        fx_l = [sbm(f"fx_l{p}", [P, TILE], F16) for p in range(2)]
        hf = [sbm(f"hf{p}", [P, HB, TILE]) for p in range(2)]
        hh = [sbm(f"hh{p}", [P, HB, TILE], F16) for p in range(2)]
        hl = [sbm(f"hl{p}", [P, HB, TILE], F16) for p in range(2)]
        meta = sbm("meta", [P, TILES, 2, 2])
        yidx = [sbm(f"yidx{p}", [P, 2], I32) for p in range(2)]
        yo = [sbm(f"yo{p}", [P, 2, P]) for p in range(2)]
        yin = w_raw

        routed = nc.dram_tensor("routed", [SLOTS, ROW], F32, kind="Internal").ap()
        expert_out = nc.dram_tensor("expert_out", [2 * TOKENS + TILES, W], F32, kind="Internal").ap()

        S = [psum(f"S{h}") for h in range(NH)]
        PT = [psum(f"PT{i}") for i in range(2)]
        A = psum("A")
        B = psum("B")
        AB = [A, B]

        x_in = [sem(f"x_in{c}") for c in range(CH)]
        lnw_in = [sem(f"lnw_in{c}") for c in range(2)]
        lnb_in = [sem(f"lnb_in{c}") for c in range(2)]
        w_in = sem("w_in")
        const_ready = sem("const_ready")
        pool_step = sem("pool_step")
        dve_step = sem("dve_step")
        act_step = sem("act_step")
        lnw_used = sem("lnw_used")
        x1_ready = sem("x1_ready")
        rowvar_ready = sem("rowvar_ready")
        rowvar_summed = sem("rowvar_summed")
        squares_ready = sem("squares_ready")
        squares_summed = sem("squares_summed")
        w_transposed = sem("w_transposed")
        bias_done = sem("bias_done")
        biasT_ready = sem("biasT_ready")
        bias_transposed = sem("bias_transposed")
        wrep_transposed = sem("wrep_transposed")
        wb_in = sem("wb_in")
        sums_ready = sem("sums_ready")
        wrep_reordered = sem("wrep_reordered")
        setup_done = sem("setup_done")
        xf_ready = sem("xf_ready")
        xs_high = sem("xs_high")
        xs_ready = sem("xs_ready")
        a_full = sem("a_full")
        a_high = sem("a_high")
        a_free = sem("a_free")
        tanh_done = sem("tanh_done")
        s_full = sem("s_full")
        logits_ready = sem("logits_ready")
        exp_done = sem("exp_done")
        pt_full = sem("pt_full")
        ph_ready = sem("ph_ready")
        pl_ready = sem("pl_ready")
        pv_done = sem("pv_done")
        b_free = sem("b_free")
        rden_ready = sem("rden_ready")
        on_ready = sem("on_ready")
        og_ready = sem("og_ready")
        ogt_full = sem("ogt_full")
        ogt_high = sem("ogt_high")
        oproj_done = sem("oproj_done")
        attention_done = sem("attention_done")
        ffn_in = sem("ffn_in")
        small_in = sem("small_in")
        wsq_ready = sem("wsq_ready")
        b1_summing = sem("b1_summing")
        b1_summed = sem("b1_summed")
        dve_step2 = sem("dve_step2")
        wsq_summed = sem("wsq_summed")
        hscale_ready = sem("hscale_ready")
        w_scaled = sem("w_scaled")
        w_split = sem("w_split")
        bgate_spread = sem("bgate_spread")
        b2_ready = sem("b2_ready")
        blanked = sem("blanked")
        xn_ready = sem("xn_ready")
        staged = sem("staged")
        stage_T = sem("stage_T")
        xnT_ready = sem("xnT_ready")
        lg_full = sem("lg_full")
        lg_ready = sem("lg_ready")
        gap_ready = sem("gap_ready")
        gate_exp = sem("gate_exp")
        totals_ready = sem("totals_ready")
        totals_summed = sem("totals_summed")
        meta_ready = sem("meta_ready")
        scattered = [sem(f"scattered{k}") for k in range(2)]
        table_ready = sem("table_ready")
        rows_loaded = [sem(f"rows_loaded{p}") for p in range(2)]
        fxT_full = sem("fxT_full")
        fx_high = sem("fx_high")
        fx_ready = sem("fx_ready")
        h_full = sem("h_full")
        gelu_done = sem("gelu_done")
        meta_kept = sem("meta_kept")
        hh_ready = sem("hh_ready")
        hl_ready = sem("hl_ready")
        y_full = sem("y_full")
        y_biased = sem("y_biased")
        y_ready = sem("y_ready")
        yidx_ready = sem("yidx_ready")
        y_sent = [sem(f"y_sent{p}") for p in range(2)]
        y_in = [sem(f"y_in{p}") for p in range(2)]
        y_added = sem("y_added")
        out_ready = sem("out_ready")
        stored = sem("stored")

        xv = x[0].rearrange("c (f i) j -> f c i j", f=2)
        lwv = ln_w.rearrange("c (f i) j -> f c i j", f=2)
        lbv = ln_b.rearrange("c (f i) j -> f c i j", f=2)
        outv = out[0].rearrange("c (f i) j -> f c i j", f=2)
        NWDMA = 17

        def chunk(c):
            return slice(c * CR, (c + 1) * CR)

        block = ctx.enter_context(nc.Block())

        def attention_steps(engine, step):
            step(0, 0)
            step(1, 1)
            with engine.Fori(1, UNITS // 2) as g:
                step(2 * g, 0)
                step(2 * g + 1, 1)
            step(UNITS, 0)
            step(UNITS + 1, 1)

        def stages(s):
            if not isinstance(s, int):
                return True, True, True
            return s < UNITS, 1 <= s <= UNITS, s >= 2

        def rows(u, p):
            if isinstance(u, int):
                return slice((u // 2) * R, (u // 2) * R + R)
            g0 = (u - p) * (R // 2)
            return bass.ds(g0, R)

        def tile_steps(engine, step):
            assert TILES % 4 == 3
            step(-1, 1)
            e = step(0, 0)
            for s in range(1, 6):
                e = step(s, s % 2, e)
            with engine.Fori(0, (TILES - 7) // 4) as g:
                e = step(4 * g + 6, 0)
                for k in range(1, 4):
                    e = step(4 * g + 6 + k, k % 2, e)
            e = step(TILES - 1, 0)
            step(TILES, 1, e)
            step(TILES + 1, 0)

        def tile_stages(s):
            if not isinstance(s, int):
                return True, True, True, True
            return s + 1 < TILES, 0 <= s < TILES, 1 <= s <= TILES, s >= 2

        def tile_at(t):
            return slice(t, t + 1) if isinstance(t, int) else bass.ds(t, 1)

        def expert_of(engine, t):
            at = slice(t, t + 1) if isinstance(t, int) else bass.ds(t, 1)
            return engine.value_load(tile_expert_i[0:1, at], min_val=0, max_val=E - 1)

        def pair_steps(engine, step):
            step(0, 0)
            step(1, 1)
            with engine.Fori(1, HALF // R // 2) as g:
                step(2 * g, 0)
                step(2 * g + 1, 1)

        def row_statistics(dve, chain, k, eps):
            for i in range(k.start, k.stop):
                last = nc.vector.bn_stats(rowstat[:, i, :], xt[:, i, :])
            chain.link(last)
            me, ve = rowstat[:, k, 1], rowstat[:, k, 2]
            mo, vo = rowstat[:, k, 4], rowstat[:, k, 5]
            chain.link(nc.vector.tensor_tensor(mean[:, k], me, mo, ALU.add))
            chain.link(nc.vector.tensor_scalar(mean[:, k], mean[:, k], 0.5, None, ALU.mult))
            chain.link(nc.vector.tensor_tensor(tmp_a[:, k], me, mo, ALU.subtract))
            chain.link(nc.vector.scalar_tensor_tensor(tmp_a[:, k], tmp_a[:, k], 0.25, tmp_a[:, k], ALU.mult, ALU.mult))
            chain.link(nc.vector.tensor_tensor(tmp_b[:, k], ve, vo, ALU.add))
            chain.link(nc.vector.scalar_tensor_tensor(var[:, k], tmp_b[:, k], 1.0 / W, tmp_a[:, k], ALU.mult, ALU.add))
            chain.link(nc.vector.tensor_scalar(rstd2[:, k], var[:, k], eps, None, ALU.add))
            rsqrt(nc, chain, rstd[:, k], rstd2[:, k], tmp_a[:, k], tmp_b[:, k])

        def power_of_two(chain, scale, square, bits, bits2):
            chain.link(nc.vector.tensor_scalar(bits, square.bitcast(I32), 23, None, ALU.arith_shift_right))
            chain.link(nc.vector.tensor_scalar(bits2, bits, -125.0, None, ALU.add))
            chain.link(nc.vector.tensor_scalar(bits, bits2, 1, None, ALU.arith_shift_right))
            chain.link(nc.vector.tensor_scalar(bits2, bits, -1.0, 141.0, ALU.mult, ALU.add))
            chain.link(nc.vector.tensor_scalar(scale.bitcast(I32), bits2, 23, None, ALU.arith_shift_left))

        @block.sync
        def _(sp):
            for c in range(CH):
                for f in range(2):
                    sp.dma_start(xt[f * C:(f + 1) * C, chunk(c), :], xv[f, :, chunk(c), :]).then_inc(x_in[c], 16)
                if c == 0:
                    for n, w in enumerate((wq, wk, wv, wg_w)):
                        for f in range(2):
                            sp.dma_start(wraw[:, n, f, :], w).then_inc(w_in, 16)
            for f in range(2):
                sp.dma_start(brep[f * C:(f + 1) * C, :], wrep_b.rearrange("(c o) -> c o", o=1)).then_inc(w_in, 16)
            sp.dma_start(wrep_raw[:], wrep_w).then_inc(w_in, 16)
            sp.dma_start(bgrow[:], wg_b.rearrange("(o c) -> o c", o=1)).then_inc(w_in, 16)
            sp.wait_ge(const_ready, 1)
            sp.dma_start(routed.rearrange("(n p) w -> p n w", p=P),
                         blank[:].unsqueeze(1).broadcast_to([P, SLOTS // P, ROW])).then_inc(blanked, 16)
            sp.wait_ge(x1_ready, CH)
            sp.dma_start(w_raw[0][:].rearrange("p a r w -> p (a r w)").rearrange("p (e h) -> p e h", e=E),
                         W1.rearrange("e d h -> d e h")).then_inc(ffn_in, 16)
            sp.dma_start(w_raw[1][:].rearrange("p a r w -> p (a r w)").rearrange("p (e b d) -> p e b d", e=E, b=HB),
                         W2.rearrange("e (b p) d -> p e b d", p=P)).then_inc(ffn_in, 16)
            for e in range(E):
                sp.dma_start(b1_sb[:, e, :], b1[e].rearrange("(b p) -> p b", p=P),
                             allow_slow_non_contiguous=True).then_inc(small_in, 16)
            sp.dma_start(b2_row[:], b2.rearrange("(o e) d -> o (e d)", o=1)).then_inc(small_in, 16)
            sp.dma_start(wg_sb[:], Wg).then_inc(small_in, 16)
            sp.dma_start(bgate_row[:], bg.rearrange("(o e) -> o e", o=1)).then_inc(small_in, 16)

            routed_v = routed.rearrange("(t k p) w -> t p k w", k=2, p=P)

            def load_rows(t, p):
                wait(sp, meta_kept, t - 1)
                sp.dma_start(rows_in[p][:], routed_v[t]).then_inc(rows_loaded[p], 16)

            for k in range(2):
                sp.wait_ge(scattered[k], 16 * HALF)
            load_rows(0, 0)
            load_rows(1, 1)
            with sp.Fori(1, (TILES - 1) // 2) as g:
                load_rows(2 * g, 0)
                load_rows(2 * g + 1, 1)
            load_rows(TILES - 1, 0)

            for p in range(2):
                sp.wait_ge(y_sent[p], 32 * ((TILES + 1 - p) // 2))
            ev = expert_out[0:2 * TOKENS].rearrange("(s c f i) w -> s f c i w", s=2, f=2, i=HALF)
            for c in range(CH):
                wait(sp, y_added, c - 1)
                for f in range(2):
                    for k in range(2):
                        sp.dma_start(yin[c % 2][f * C:(f + 1) * C, k], ev[k, f, :, chunk(c), :]).then_inc(y_in[c % 2], 16)
            for c in range(CH):
                sp.wait_ge(y_added, c + 1)
                for f in range(2):
                    sp.dma_start(outv[f, :, chunk(c), :], xt[f * C:(f + 1) * C, chunk(c), :]).then_inc(stored, 16)
            sp.wait_ge(stored, 32 * CH)

        @block.gpsimd
        def _(pool):
            chain = Chain(pool, pool_step)
            chain.link(nc.gpsimd.memset(identity[:], 0.0))
            chain.link(nc.gpsimd.affine_select(out=identity[:], in_=identity[:], compare_op=ALU.not_equal, fill=1.0,
                                               base=0, pattern=[[-1, P]], channel_multiplier=1))
            chain.link(nc.gpsimd.memset(wb_sb[:], 0.0))
            for f in range(2):
                pool.dma_start(wb_sb[f * C:(f + 1) * C, f * NH:(f + 1) * NH], wb.rearrange("h c -> c h"),
                               allow_slow_non_contiguous=True).then_inc(wb_in, 16)
            chain.link(nc.gpsimd.memset(ones[:], 1.0))
            chain.link(nc.gpsimd.memset(bg_f[:], 0.0))
            chain.link(nc.gpsimd.memset(w4l[:].bitcast(F32), 0.0))
            for p in range(2):
                chain.link(nc.gpsimd.memset(vh[p][:], 1.0))
                chain.link(nc.gpsimd.memset(vl[p][:], 0.0))
            for e in range(E):
                chain.link(nc.gpsimd.memset(order8[:, e:e + 1], float(E - e)))
            chain.link(nc.gpsimd.memset(before[:], 1.0))
            chain.link(nc.gpsimd.affine_select(out=before[:], in_=before[:], compare_op=ALU.is_gt, fill=0.0, base=0,
                                               pattern=[[1, P]], channel_multiplier=-1))
            for f in range(2):
                chain.link(nc.gpsimd.iota(token_id[f * C:(f + 1) * C, :], [[1, HALF]], base=f * HALF,
                                          channel_multiplier=H, allow_small_or_imprecise_dtypes=True))
            chain.link(nc.gpsimd.iota(tile_no[:], [[1, TILES]], base=0, channel_multiplier=0,
                                      allow_small_or_imprecise_dtypes=True))
            chain.link(nc.gpsimd.memset(blank[:], 0.0))
            nc.gpsimd.memset(blank[:, W + 1:W + 2], float(NOWHERE)).then_inc(const_ready, 1)

            def split_x1(s, p):
                one, _, _ = stages(s)
                if not one:
                    return
                if p == 0:
                    wait(pool, xs_ready, s)
                    nc.gpsimd.tensor_copy(xf[:].rearrange("p (r w) -> p r w", w=W), x1[:, rows(s, 0), :]).then_inc(xf_ready, 1)
                hi = slice(p * C, (p + 1) * C)
                lo = slice((1 - p) * C, (2 - p) * C)
                pool.wait_ge(xs_high, s + 1)
                nc.gpsimd.tensor_tensor(xs[p][lo], xf[hi], xs[p][hi], ALU.subtract).then_inc(xs_ready, 1)

            pool.wait_ge(x1_ready, CH)
            attention_steps(pool, split_x1)

            pool.wait_ge(hscale_ready, 1)
            for n in range(2):
                raw = w_raw[n][:].rearrange("p a r w -> p (a r w)")
                high, low = (t[:].rearrange("p e b d -> p (e b d)") for t in (w_h[n], w_l[n]))
                nc.gpsimd.tensor_scalar(raw, raw, hscale[:, n:n + 1], None, ALU.mult).then_inc(w_scaled, 1)
                pool.wait_ge(w_scaled, 2 * n + 1)
                nc.gpsimd.tensor_copy(high, raw).then_inc(w_scaled, 1)
                pool.wait_ge(w_scaled, 2 * n + 2)
                nc.gpsimd.tensor_tensor(low, raw, high, ALU.subtract).then_inc(w_split, 1)

            pool.wait_ge(blanked, 16)
            for k in range(2):
                pool.wait_ge(meta_ready, k + 1)
                for i in range(HALF):
                    pool.indirect_dma_start(routed, bass.IndirectOffsetOnAxis(ap=pos[k][:, i:i + 1], axis=0),
                                            pay[:, i, :], None).then_inc(scattered[k], 16)

            def send_rows(s, q, _=None):
                if isinstance(s, int) and s < 2:
                    return
                t, p = s - 2, q
                pool.wait_ge(yidx_ready, t + 1)
                pool.wait_ge(y_ready, t + 1)
                last_place = 2 * TOKENS - 1 + t
                for k in range(2):
                    pool.indirect_dma_start(
                        expert_out, bass.IndirectOffsetOnAxis(ap=yidx[p][:, k:k + 1], axis=0),
                        yo[p][:, k, :], None, bounds_check=last_place, oob_is_err=False).then_inc(y_sent[p], 16)

            tile_steps(pool, send_rows)

        @block.scalar
        def _(act):
            for c in range(CH):
                if c >= 2:
                    act.wait_ge(lnw_used, c - 1)
                for f in range(2):
                    act.dma_start(lnw_sb[f * C:(f + 1) * C, c % 2], lwv[f, :, chunk(c), :]).then_inc(lnw_in[c % 2], 16)
                if c < 2:
                    for f in range(2):
                        act.dma_start(lnb_sb[f * C:(f + 1) * C, c % 2], lbv[f, :, chunk(c), :]).then_inc(lnb_in[c % 2], 16)
            chain = Chain(act, act_step)
            act.wait_ge(w_in, 12 * 16)
            nc.scalar.activation(wrep_ordered[:].rearrange("o (h c) -> o h c", h=NH),
                                 wrep_raw[:].rearrange("o (c h) -> o h c", h=NH), ACT.Copy).then_inc(wrep_reordered, 1)
            for n in range(3):
                chain.link(nc.scalar.activation(square_junk[:, 0:C], wraw[:, n, 0, :], ACT.Square,
                                                accum_out=sums[:, n:n + 1]))
            for c in range(CH):
                act.wait_ge(x1_ready, c + 1)
                for k in range(2):
                    last = nc.scalar.activation(square_junk[:].rearrange("p (r w) -> p r w", w=W),
                                                x1[:, c * CR + k * CR // 2:c * CR + (k + 1) * CR // 2, :],
                                                ACT.Square, accum_out=xsq[:, 2 * c + k:2 * c + k + 1])
                    if c == CH - 1 and k == 1:
                        last.then_inc(squares_ready, 1)
                    else:
                        chain.link(last)
                if c + 2 < CH:
                    for f in range(2):
                        act.dma_start(lnb_sb[f * C:(f + 1) * C, c % 2], lbv[f, :, chunk(c + 2), :]).then_inc(lnb_in[c % 2], 16)

            def high_qk(u, p, n):
                act.wait_ge(a_full, 4 * u + n + 1)
                nc.scalar.activation(qk[n][0][p][:], A[:], ACT.Copy).then_inc(a_high, 1)

            def gate_and_high_v(u, p, half):
                act.wait_ge(a_full, 4 * u + 3 + half)
                if half == 0:
                    wait(act, og_ready, 2 * (u - 1))
                    wait(act, pv_done, 4 * (u - 1))
                av = A[:].rearrange("p (r s c) -> p r s c", r=2, s=2)
                nc.scalar.activation(gt[p][:, 2 * half:2 * half + 2, :], av[:, :, 1, :], ACT.Tanh,
                                     scale=0.5).then_inc(tanh_done, 1)
                for r in range(2):
                    last = nc.scalar.activation(vh[p][:, 2 * half + r, :, 0:D],
                                                av[:, r, 0, :].rearrange("p (h d) -> p h d", d=D), ACT.Copy)
                last.then_inc(a_high, 1)

            def high_p(u, i):
                n = 4 * u + i
                act.wait_ge(pt_full, n + 1)
                wait(act, pv_done, n - 1)
                nc.scalar.activation(ph[i % 2][:], PT[i % 2][:], ACT.Copy).then_inc(ph_ready, 1)

            def exponentials(u, p, pair):
                act.wait_ge(logits_ready, 2 * u + pair + 1)
                for h in (2 * pair, 2 * pair + 1):
                    for i in range(R):
                        last = nc.scalar.activation(L[p][:, h, i, :], L[p][:, h, i, :], ACT.Exp, scale=-1.0,
                                                    bias=lmin[p][:, h * R + i:h * R + i + 1])
                last.then_inc(exp_done, 1)

            def step(s, p):
                one, two, three = stages(s)
                if one:
                    act.wait_ge(xf_ready, s // 2 + 1 if isinstance(s, int) else (s - p) // 2 + 1)
                    wait(act, a_full, 4 * (s - 1))
                    hi = slice(p * C, (p + 1) * C)
                    nc.scalar.activation(xs[p][hi], xf[hi], ACT.Copy).then_inc(xs_high, 1)
                if three:
                    act.wait_ge(ogt_full, s - 1)
                    wait(act, oproj_done, s - 2)
                    nc.scalar.activation(ogT_h[:], B[:], ACT.Copy).then_inc(ogt_high, 1)
                if two:
                    high_p(s - 1, 0)
                    high_p(s - 1, 1)
                if one:
                    high_qk(s, p, 0)
                if two:
                    high_p(s - 1, 2)
                if one:
                    high_qk(s, p, 1)
                if two:
                    high_p(s - 1, 3)
                if one:
                    gate_and_high_v(s, p, 0)
                    exponentials(s, p, 0)
                    gate_and_high_v(s, p, 1)
                    exponentials(s, p, 1)

            attention_steps(act, step)

            act.wait_ge(ffn_in, 32)
            act.wait_ge(b_free, 4 * UNITS)
            for n in range(2):
                raw = w_raw[n][:].rearrange("p a r w -> p (a r w)")
                last = nc.scalar.activation(w_h[n][:].rearrange("p e b d -> p (e b d)"), raw, ACT.Square,
                                            accum_out=wsq[:, n:n + 1])
                if n == 0:
                    chain.link(last)
                else:
                    last.then_inc(wsq_ready, 1)

            def stage_rows(g, p):
                act.wait_ge(xn_ready, 1)
                wait(act, stage_T, g - 1)
                nc.scalar.activation(stage[p][:], pay[:, bass.ds(g * R, R), 0:W], ACT.Copy).then_inc(staged, 1)
                act.wait_ge(stage_T, g + 1)
                wait(act, lg_full, g - 1)
                nc.scalar.activation(xnT[p][:], PT[p][:], ACT.Copy).then_inc(xnT_ready, 1)

            pair_steps(act, stage_rows)
            act.wait_ge(gap_ready, 1)
            nc.scalar.activation(gate_e[:], key[:], ACT.Exp).then_inc(gate_exp, 1)

            def tile_step(s, q, _=None):
                tokens, first, second, weighting = tile_stages(s)
                if tokens:
                    t, p = s + 1, 1 - q
                    act.wait_ge(fxT_full, t + 1)
                    nc.scalar.activation(fx_h[p][:], AB[p][:, 0:TILE], ACT.Copy).then_inc(fx_high, 1)
                if first:
                    t, p = s, q
                    e = expert_of(act, s)
                    for pair in range(2):
                        act.wait_ge(h_full, 2 * t + pair + 1)
                        for k in range(2):
                            b = 2 * pair + k
                            last = nc.scalar.activation(hf[p][:, b, :], S[2 * p + pair][:, k * TILE:(k + 1) * TILE], ACT.Gelu,
                                                        scale=inv_hscale[:, 0:1], bias=b1_flat[:, bass.ds(e * HB + b, 1)])
                        last.then_inc(gelu_done, 1)
                if weighting:
                    t, p = s - 2, q
                    wait(act, y_sent[p], (t // 2) * 32 if isinstance(t, int) else (t - p) * 16)
                    act.wait_ge(y_full, t + 1)
                    for k in range(2):
                        last = nc.scalar.activation(yo[p][:, k, :], PT[p][:, k * P:(k + 1) * P], ACT.Copy,
                                                    scale=meta[:, tile_at(t), k, 0:1])
                    last.then_inc(y_ready, 1)

            act.wait_ge(table_ready, 1)
            act.wait_ge(small_in, 16 * (E + 3))
            tile_steps(act, tile_step)

        @block.vector
        def _(dve):
            chain = Chain(dve, dve_step)
            for c in range(CH):
                dve.wait_ge(x_in[c], 32)
                row_statistics(dve, chain, chunk(c), 1e-6)
                k = chunk(c)
                for i in range(c * CR, (c + 1) * CR):
                    last = nc.vector.tensor_scalar(x1[:, i, :], xt[:, i, :], mean[:, i:i + 1], rstd[:, i:i + 1],
                                                   ALU.subtract, ALU.mult)
                chain.link(last)
                dve.wait_ge(lnw_in[c % 2], 32 * (c // 2 + 1))
                nc.vector.tensor_tensor(x1[:, k, :], x1[:, k, :], lnw_sb[:, c % 2], ALU.mult).then_inc(lnw_used, 1)
            chain.link(nc.vector.tensor_tensor(tmp_a[:], rstd[:], rstd[:], ALU.mult))
            chain.link(nc.vector.tensor_tensor(tmp_b[:], tmp_a[:], var[:], ALU.mult))
            nc.vector.tensor_reduce(gstat[:, 0:1], tmp_b[:], AX_X, ALU.add).then_inc(rowvar_ready, 1)
            dve.wait_ge(const_ready, 1)
            dve.wait_ge(w_in, 12 * 16)
            chain.link(nc.vector.tensor_copy(bg_f[0:1, :], bgrow[:]))
            chain.link(nc.vector.tensor_copy(bg_h[:], bg_f[:]))
            chain.link(nc.vector.tensor_tensor(bg_l[:], bg_f[:], bg_h[:], ALU.subtract))
            chain.link(nc.vector.tensor_copy(ones_r[:], ones[:]))
            dve.wait_ge(rowvar_summed, 1)
            chain.link(nc.vector.tensor_scalar(gstat[:, 1:2], B[:, 0:1], 1.0 / (P * HALF), 1e-5, ALU.mult, ALU.add))
            rsqrt(nc, chain, grstd[:], gstat[:, 1:2], gtmp[:, 0:1], gtmp2[:, 0:1])
            dve.wait_ge(lnw_used, CH)
            for c in range(CH):
                k = chunk(c)
                dve.wait_ge(lnb_in[c % 2], 32 * (c // 2 + 1))
                nc.vector.scalar_tensor_tensor(x1[:, k, :], x1[:, k, :], grstd[:, 0:1], lnb_sb[:, c % 2],
                                               ALU.mult, ALU.add).then_inc(x1_ready, 1)
            dve.wait_ge(squares_ready, 1)
            nc.vector.tensor_reduce(sums[:, 3:4], xsq[:], AX_X, ALU.add).then_inc(sums_ready, 1)
            dve.wait_ge(squares_summed, 1)
            chain.link(nc.vector.tensor_copy(gstat[:, 0:4], B[:, 0:4]))
            chain.link(nc.vector.tensor_scalar(gstat[:, 4:7], gstat[:, 0:3], gstat[:, 3:4], 1e-30, ALU.mult, ALU.max))
            power_of_two(chain, scales[:, 0:3], gstat[:, 4:7], ebits[:, 0:3], ebits2[:, 0:3])
            chain.link(nc.vector.reciprocal(inv_scales[:, 0:3], scales[:, 0:3]))
            chain.link(nc.vector.tensor_scalar(bias_scale[:], scales[:, 0:1], scales[:, 1:2], float(D) ** 0.5, ALU.mult, ALU.mult))
            chain.link(nc.vector.tensor_scalar(logit_scale[:], inv_scales[:, 0:1], inv_scales[:, 1:2], -float(D) ** -0.5, ALU.mult, ALU.mult))
            dve.wait_ge(w_transposed, 1)
            for n in range(3):
                last = nc.vector.tensor_scalar(w4[:, n, :], PT[0][:, n * P:(n + 1) * P], scales[:, n:n + 1], None, ALU.mult)
            chain.link(nc.vector.tensor_copy(w4[:, 3, :], PT[0][:, 3 * P:4 * P]))
            chain.link(nc.vector.tensor_copy(w4h[:], w4[:]))
            for f in range(2):
                k = slice(f * C, (f + 1) * C)
                last = nc.vector.tensor_tensor(w4l[k, f], w4[k], w4h[k], ALU.subtract)
            chain.link(last)
            dve.wait_ge(wrep_transposed, 1)
            for f in range(2):
                last = nc.vector.tensor_scalar(wrepT[:, f * C:(f + 1) * C], PT[1][:, 0:C], inv_scales[:, 2:3], 0.5, ALU.mult, ALU.mult)
            chain.link(last)
            chain.link(nc.vector.tensor_copy(wrep_h[:], wrepT[:]))
            chain.link(nc.vector.tensor_tensor(wrep_l[:], wrepT[:], wrep_h[:], ALU.subtract))
            dve.wait_ge(bias_done, 1)
            nc.vector.tensor_scalar(biasT[:].rearrange("k h (f i) -> k f i h", f=2),
                                    A[:].rearrange("k (i f h) -> k f i h", f=2, h=NH), bias_scale[:, 0:1], None,
                                    ALU.mult).then_inc(biasT_ready, 1)
            dve.wait_ge(bias_transposed, 1)
            nc.vector.tensor_copy(biasN[:].rearrange("p h k -> p (h k)"), S[0][:]).then_inc(setup_done, 1)
            dve.wait_ge(setup_done, 1)

            def low_qk(u, p, n):
                dve.wait_ge(a_high, 4 * u + n + 1)
                nc.vector.tensor_tensor(qk[n][1][p][:], A[:], qk[n][0][p][:], ALU.subtract).then_inc(a_free, 1)

            def low_v(u, p, half):
                dve.wait_ge(a_high, 4 * u + 3 + half)
                av = A[:].rearrange("p (r s c) -> p r s c", r=2, s=2)
                for r in range(2):
                    last = nc.vector.tensor_tensor(vl[p][:, 2 * half + r, :, 0:D],
                                                   av[:, r, 0, :].rearrange("p (h d) -> p h d", d=D),
                                                   vh[p][:, 2 * half + r, :, 0:D], ALU.subtract)
                last.then_inc(a_free, 1)

            def low_p(u, i):
                n = 4 * u + i
                dve.wait_ge(ph_ready, n + 1)
                nc.vector.tensor_tensor(pl[i % 2][:], PT[i % 2][:], ph[i % 2][:], ALU.subtract).then_inc(pl_ready, 1)

            def logits(u, p, pair):
                dve.wait_ge(s_full, 2 * u + pair + 1)
                wait(dve, pt_full, 4 * (u - 1))
                nc.vector.memset(turn[pair][:], 0.0)
                for h in (2 * pair, 2 * pair + 1):
                    for i in range(R):
                        last = nc.vector.tensor_tensor_reduce(
                            out=L[p][:, h, i, :], in0=S[h][:, i * P:(i + 1) * P], in1=biasN[:, h, :],
                            scale=logit_scale[:, 0:1], scalar=BIG, op0=ALU.add, op1=ALU.min,
                            accum_out=lmin[p][:, h * R + i:h * R + i + 1])
                last.then_inc(logits_ready, 1)

            def normalise(u, p, half):
                dve.wait_ge(pv_done, 4 * u + 2 * half + 2)
                ov = B[:, 0:2 * NH * (D + 1)].rearrange("p (r h d) -> p r h d", r=2, h=NH)
                wait(dve, og_ready, 2 * u + half)
                nc.vector.reciprocal(rden[:], ov[:, :, :, D]).then_inc(rden_ready, 1)
                dve.wait_ge(rden_ready, 2 * u + half + 1)
                nc.vector.tensor_tensor(on[:].rearrange("p r (h d) -> p r h d", d=D), ov[:, :, :, 0:D],
                                        rden[:].unsqueeze(3).broadcast_to([P, 2, NH, D]), ALU.mult).then_inc(b_free, 1)
                dve.wait_ge(b_free, 4 * u + half + 1)
                if half == 0:
                    wait(dve, ogt_full, u - 1)
                nc.vector.scalar_tensor_tensor(og[p][:, 2 * half:2 * half + 2, :], gt[p][:, 2 * half:2 * half + 2, :], 1.0,
                                               on[:], ALU.add, ALU.mult).then_inc(og_ready, 1)

            def step(s, p):
                one, two, three = stages(s)
                if three:
                    dve.wait_ge(ogt_high, s - 1)
                    nc.vector.tensor_tensor(ogT_l[:], B[:], ogT_h[:], ALU.subtract).then_inc(b_free, 1)
                if two:
                    low_p(s - 1, 0)
                if three:
                    dve.wait_ge(oproj_done, s - 1)
                    k = slice(p * C, (p + 1) * C)
                    dst = xt[k, rows(s - 2, p), :].rearrange("p r w -> p (r w)")
                    nc.vector.scalar_tensor_tensor(dst, B[k, :], brep[k, 0:1], dst, ALU.add, ALU.add).then_inc(b_free, 1)
                if two:
                    low_p(s - 1, 1)
                if one:
                    low_qk(s, p, 0)
                if two:
                    low_p(s - 1, 2)
                if one:
                    low_qk(s, p, 1)
                if two:
                    normalise(s - 1, 1 - p, 0)
                    low_p(s - 1, 3)
                if one:
                    low_v(s, p, 0)
                    logits(s, p, 0)
                    logits(s, p, 1)
                    low_v(s, p, 1)
                if two:
                    normalise(s - 1, 1 - p, 1)

            attention_steps(dve, step)

            dve.wait_ge(b_free, 4 * UNITS)
            chain.count = 0
            chain.sem = dve_step2

            chain.link(nc.vector.memset(pay[:, :, W + 2:ROW], 0.0))
            row_statistics(dve, chain, slice(0, HALF), 1e-5)
            for i in range(HALF):
                last = nc.vector.tensor_scalar(pay[:, i, 0:W], xt[:, i, :], mean[:, i:i + 1], rstd[:, i:i + 1],
                                               ALU.subtract, ALU.mult)
            last.then_inc(xn_ready, 1)
            dve.wait_ge(wsq_summed, 1)
            chain.link(nc.vector.tensor_copy(gstat[:, 0:2], A[:, 0:2]))
            chain.link(nc.vector.tensor_scalar(gstat[:, 3:4], gstat[:, 0:1], float(4 * W), 1e-12, ALU.mult, ALU.add))
            chain.link(nc.vector.tensor_scalar(gstat[:, 4:6], gstat[:, 0:2], 1e-12, None, ALU.max))
            dve.wait_ge(small_in, 16 * (E + 3))
            chain.link(nc.vector.tensor_tensor(b1_sq[:], b1_sb[:].rearrange("p e b -> p (e b)"), b1_sb[:].rearrange("p e b -> p (e b)"), ALU.mult))
            nc.vector.tensor_reduce(b1_sum[:], b1_sq[:], AX_X, ALU.add).then_inc(b1_summing, 1)
            dve.wait_ge(b1_summed, 1)
            chain.link(nc.vector.scalar_tensor_tensor(gstat[:, 6:7], B[:, 0:1], 4.0, gstat[:, 3:4], ALU.mult, ALU.add))
            power_of_two(chain, hscale[:, 0:3], gstat[:, 4:7], ebits[:, 0:3], ebits2[:, 0:3])
            chain.link(nc.vector.reciprocal(inv_hscale[:, 0:3], hscale[:, 0:3]))
            nc.vector.tensor_scalar(y_scale[:], inv_hscale[:, 1:2], inv_hscale[:, 2:3], None, ALU.mult).then_inc(hscale_ready, 1)
            dve.wait_ge(hscale_ready, 1)
            chain.link(nc.vector.tensor_scalar(b2_scaled[:], b2_row[:], hscale[0:1, 1:2], hscale[0:1, 2:3], ALU.mult, ALU.mult))
            chain.link(nc.vector.tensor_copy(b2_h[:], b2_scaled[:]))
            chain.link(nc.vector.tensor_tensor(b2_l[:], b2_scaled[:], b2_h[:], ALU.subtract))
            chain.link(nc.vector.tensor_copy(ones_x[:], ones[0:1, :]))
            dve.wait_ge(bgate_spread, 1)
            chain.link(nc.vector.tensor_copy(bgate_all[:], B[:, E:2 * E]))

            def collect_logits(g, p):
                dve.wait_ge(lg_full, g + 1)
                nc.vector.tensor_copy(lg[:, bass.ds(g * R, R), :], S[2 + p][:, 0:R * E].rearrange("p (i e) -> p i e", e=E)).then_inc(lg_ready, 1)

            pair_steps(dve, collect_logits)

            dve.wait_ge(lg_ready, HALF // R)
            dve.wait_ge(const_ready, 1)
            rows_e = [P, HALF, E]
            spread = lambda v: v.unsqueeze(2).broadcast_to(rows_e)
            chain.link(nc.vector.tensor_tensor(lg[:], lg[:], bgate_all[:].unsqueeze(1).broadcast_to(rows_e), ALU.add))
            for k in range(2):
                chain.link(nc.vector.tensor_reduce(top[k][:], lg[:], AX_X, ALU.max))
                chain.link(nc.vector.tensor_tensor(r_a[:], lg[:], spread(top[k][:]), ALU.is_equal))
                chain.link(nc.vector.tensor_tensor(r_b[:], r_a[:], order8[:].unsqueeze(1).broadcast_to(rows_e), ALU.mult))
                chain.link(nc.vector.tensor_reduce(key[:], r_b[:], AX_X, ALU.max))
                chain.link(nc.vector.tensor_tensor(oh[k][:], r_b[:], spread(key[:]), ALU.is_equal))
                if k == 0:
                    chain.link(nc.vector.scalar_tensor_tensor(lg[:], oh[0][:], -BIG, lg[:], ALU.mult, ALU.add))
            chain.link(nc.vector.tensor_tensor(picked[:], oh[0][:], oh[1][:], ALU.add))
            nc.vector.tensor_tensor(key[:], top[1][:], top[0][:], ALU.subtract).then_inc(gap_ready, 1)
            chain.link(nc.vector.tensor_copy(r_a[:], picked[:]))
            src, dst = picked, r_b
            step_rows = 1
            while step_rows < HALF:
                nc.vector.tensor_copy(dst[:, 0:step_rows, :], src[:, 0:step_rows, :])
                chain.link(nc.vector.tensor_tensor(dst[:, step_rows:, :], src[:, step_rows:, :], src[:, 0:HALF - step_rows, :], ALU.add))
                src, dst = dst, src
                step_rows *= 2
            assert src is picked
            nc.vector.tensor_tensor(r_b[:], picked[:], r_a[:], ALU.subtract).then_inc(totals_ready, 1)
            dve.wait_ge(totals_ready, 1)
            dve.wait_ge(totals_summed, 2)
            chain.link(nc.vector.tensor_copy(counts[:], B[:, 0:2 * E]))
            tf, tg, th = tiles_f
            chain.link(nc.vector.tensor_scalar(tiles_i[:], counts[:, E:2 * E], float(TILE - 1), None, ALU.add))
            chain.link(nc.vector.tensor_scalar(tiles_j[:], tiles_i[:], TILE.bit_length() - 1, None, ALU.arith_shift_right))
            chain.link(nc.vector.tensor_copy(tf[:], tiles_j[:]))
            a, b = tf, tg
            for d in (1, 2, 4):
                nc.vector.tensor_copy(b[:, 0:d], a[:, 0:d])
                chain.link(nc.vector.tensor_tensor(b[:, d:], a[:, d:], a[:, 0:E - d], ALU.add))
                a, b = b, (th if a is tf else a)
            inclusive = a
            chain.link(nc.vector.tensor_tensor(first_row[:], inclusive[:], tf[:], ALU.subtract))
            chain.link(nc.vector.scalar_tensor_tensor(first_row2[:], first_row[:], float(TILE), counts[:, 0:E], ALU.mult, ALU.add))
            chain.link(nc.vector.memset(tile_expert[:], 0.0))
            for e in range(E - 1):
                chain.link(nc.vector.tensor_scalar(tile_cmp[:], tile_no[:], inclusive[0:1, e:e + 1], None, ALU.is_ge))
                chain.link(nc.vector.tensor_tensor(tile_expert[:], tile_expert[:], tile_cmp[:], ALU.add))
            nc.vector.tensor_copy(tile_expert_i[:], tile_expert[:]).then_inc(table_ready, 1)
            chain.link(nc.vector.tensor_tensor(r_b[:], r_b[:], first_row2[:].unsqueeze(1).broadcast_to(rows_e), ALU.add))
            for k in range(2):
                chain.link(nc.vector.tensor_tensor(r_a[:], r_b[:], oh[k][:], ALU.mult))
                chain.link(nc.vector.tensor_reduce(posf[:], r_a[:], AX_X, ALU.add))
                chain.link(nc.vector.tensor_copy(pos[k][:], posf[:]))
            dve.wait_ge(gate_exp, 1)
            chain.link(nc.vector.tensor_scalar(key[:], gate_e[:], 1.0, None, ALU.add))
            chain.link(nc.vector.reciprocal(weight[0][:], key[:]))
            chain.link(nc.vector.tensor_tensor(weight[1][:], gate_e[:], weight[0][:], ALU.mult))
            for k in range(2):
                if k:
                    dve.wait_ge(scattered[0], 16 * HALF)
                chain.link(nc.vector.tensor_scalar(pay[:, :, W], weight[k][:], y_scale[:, 0:1], None, ALU.mult))
                nc.vector.tensor_scalar(pay[:, :, W + 1], token_id[:], float(k * TOKENS), None,
                                        ALU.add).then_inc(meta_ready, 1)

            def tile_step(s, q, _=None):
                tokens, first, second, weighting = tile_stages(s)
                if tokens:
                    t, p = s + 1, 1 - q
                    dve.wait_ge(fx_high, t + 1)
                    nc.vector.tensor_tensor(fx_l[p][:], AB[p][:, 0:TILE], fx_h[p][:], ALU.subtract).then_inc(fx_ready, 1)
                    nc.vector.tensor_copy(meta[:, tile_at(t), :, :], rows_in[p][:, :, W:W + 2].unsqueeze(1)).then_inc(meta_kept, 1)
                if weighting:
                    t, p = s - 2, q
                    wait(dve, y_sent[p], (t // 2) * 32 if isinstance(t, int) else (t - p) * 16)
                    dve.wait_ge(meta_kept, t + 1)
                    nc.vector.tensor_copy(yidx[p][:].unsqueeze(1), meta[:, tile_at(t), :, 1]).then_inc(yidx_ready, 1)
                if first:
                    t, p = s, q
                    for pair in range(2):
                        b = slice(2 * pair, 2 * pair + 2)
                        dve.wait_ge(gelu_done, 2 * t + pair + 1)
                        nc.vector.tensor_scalar(hh[p][:, b, :], hf[p][:, b, :], hscale[:, 2:3], None, ALU.mult).then_inc(hh_ready, 1)
                        dve.wait_ge(hh_ready, 2 * t + pair + 1)
                        nc.vector.scalar_tensor_tensor(hl[p][:, b, :], hf[p][:, b, :], hscale[:, 2:3], hh[p][:, b, :],
                                                       ALU.mult, ALU.subtract).then_inc(hl_ready, 1)

            dve.wait_ge(table_ready, 1)
            tile_steps(dve, tile_step)

            for c in range(CH):
                dve.wait_ge(y_in[c % 2], 64 * (c // 2 + 1))
                for k in range(2):
                    chain.link(nc.vector.tensor_tensor(xt[:, chunk(c), :], xt[:, chunk(c), :], yin[c % 2][:, k], ALU.add)) if k == 0 else \
                        nc.vector.tensor_tensor(xt[:, chunk(c), :], xt[:, chunk(c), :], yin[c % 2][:, k], ALU.add).then_inc(y_added, 1)

        @block.tensor
        def _(pe):
            pe.wait_ge(const_ready, 1)
            pe.wait_ge(w_in, 12 * 16)
            for n in range(4):
                last = nc.tensor.transpose(PT[0][:, n * P:(n + 1) * P], wraw[:, n].rearrange("o f c -> o (f c)"), identity[:])
            last.then_inc(w_transposed, 1)
            pe.wait_ge(wrep_reordered, 1)
            nc.tensor.transpose(PT[1][:, 0:C], wrep_ordered[:], identity[0:C, 0:C]).then_inc(wrep_transposed, 1)
            pe.wait_ge(rowvar_ready, 1)
            nc.tensor.matmul(B[:, 0:1], ones[:], gstat[:, 0:1], start=True, stop=True).then_inc(rowvar_summed, 1)
            pe.wait_ge(wb_in, 32)
            for i in range(HALF):
                if i % CR == 0:
                    pe.wait_ge(x1_ready, i // CR + 1)
                last = nc.tensor.matmul(A[:, i * 2 * NH:(i + 1) * 2 * NH], x1[:, i, :], wb_sb[:], start=True, stop=True)
            last.then_inc(bias_done, 1)
            pe.wait_ge(sums_ready, 1)
            nc.tensor.matmul(B[:, 0:4], ones[:], sums[:, 0:4], start=True, stop=True).then_inc(squares_summed, 1)
            pe.wait_ge(biasT_ready, 1)
            for h in range(NH):
                last = nc.tensor.transpose(S[0][:, h * P:(h + 1) * P], biasT[:, h, :], identity[:])
            last.then_inc(bias_transposed, 1)
            pe.wait_ge(setup_done, 1)

            def project_qk(u, p, n):
                wait(pe, a_free, 4 * u + n)
                if n == 0:
                    pe.wait_ge(xs_ready, u + 1)
                nc.tensor.matmul(A[:], w4h[:, n, :], xs[p][:], start=True, stop=False)
                nc.tensor.matmul(A[:], w4l[:, p, n, :], xs[p][:], start=False, stop=True).then_inc(a_full, 1)

            def project_vg(u, p, half):
                pe.wait_ge(a_free, 4 * u + 2 + half)
                av = A[:].rearrange("p (r s c) -> p r s c", r=2, s=2)
                flags = dict(skip_group_check=True)
                for r in range(2):
                    i = 2 * half + r
                    xi = xs[p][:, i * P:(i + 1) * P]
                    nc.tensor.matmul(A[:, r * 256:(r + 1) * 256], xi, w4h[:, 2:4, :], start=r == 0, stop=False, **flags)
                    nc.tensor.matmul(A[:, r * 256:(r + 1) * 256], xi, w4l[:, p, 2:4, :], start=False, stop=False, **flags)
                for part in (bg_h, bg_l):
                    last = nc.tensor.matmul(av[:, :, 1, :], ones_r[:], part[:].unsqueeze(1).broadcast_to([P, 2, P]),
                                            start=False, stop=part is bg_l, **flags)
                last.then_inc(a_full, 1)

            def scores(u, p, pair):
                if pair == 0:
                    pe.wait_ge(a_free, 4 * u + 2)
                wait(pe, logits_ready, 2 * (u - 1) + pair + 1)
                (q_h, q_l), (k_h, k_l) = ([part[p] for part in qk[n]] for n in range(2))
                for i in range(R):
                    c = slice(i * P, (i + 1) * P)
                    for m, (a, b) in enumerate(((q_h, k_h), (q_h, k_l), (q_l, k_h))):
                        for h in (2 * pair, 2 * pair + 1):
                            d = slice(h * D, (h + 1) * D)
                            last = nc.tensor.matmul(S[h][:, c], a[d, c], b[d, c], start=m == 0, stop=m == 2)
                last.then_inc(s_full, 1)

            def transpose_p(u, p, i):
                n = 4 * u + i
                if i == 0:
                    pe.wait_ge(exp_done, 2 * u + 2)
                wait(pe, pl_ready, n - 1)
                for h in range(NH):
                    last = nc.tensor.transpose(PT[i % 2][:, h * P:(h + 1) * P], L[p][:, h, i, :], identity[:])
                last.then_inc(pt_full, 1)

            def values(u, p, i):
                n = 4 * u + i
                pe.wait_ge(pl_ready, n + 1)
                if i == 0:
                    pe.wait_ge(a_free, 4 * u + 4)
                if i % 2 == 0:
                    wait(pe, b_free, 4 * u + i // 2)
                for h in range(NH):
                    k = slice(h * P, (h + 1) * P)
                    o = ((i % 2) * NH + h) * (D + 1)
                    dst = B[:, o:o + D + 1]
                    nc.tensor.matmul(dst, ph[i % 2][:, k], vh[p][:, i, h, :], start=True, stop=False)
                    nc.tensor.matmul(dst, ph[i % 2][:, k], vl[p][:, i, h, :], start=False, stop=False)
                    last = nc.tensor.matmul(dst, pl[i % 2][:, k], vh[p][:, i, h, :], start=False, stop=True)
                last.then_inc(pv_done, 1)

            def step(s, p):
                one, two, three = stages(s)
                if three:
                    pe.wait_ge(og_ready, 2 * (s - 1))
                    for i in range(R):
                        last = nc.tensor.transpose(B[:, i * P:(i + 1) * P], og[p][:, i, :], identity[:])
                    last.then_inc(ogt_full, 1)
                if two:
                    transpose_p(s - 1, 1 - p, 0)
                if three:
                    pe.wait_ge(b_free, 4 * (s - 2) + 3)
                    nc.tensor.matmul(B[:], wrep_h[:], ogT_h[:], start=True, stop=False)
                    nc.tensor.matmul(B[:], wrep_h[:], ogT_l[:], start=False, stop=False)
                    nc.tensor.matmul(B[:], wrep_l[:], ogT_h[:], start=False, stop=True).then_inc(oproj_done, 1)
                if two:
                    transpose_p(s - 1, 1 - p, 1)
                if one:
                    project_qk(s, p, 0)
                if two:
                    values(s - 1, 1 - p, 0)
                    transpose_p(s - 1, 1 - p, 2)
                if one:
                    project_qk(s, p, 1)
                if two:
                    values(s - 1, 1 - p, 1)
                    transpose_p(s - 1, 1 - p, 3)
                if one:
                    project_vg(s, p, 0)
                    scores(s, p, 0)
                    project_vg(s, p, 1)
                    scores(s, p, 1)
                if two:
                    values(s - 1, 1 - p, 2)
                    values(s - 1, 1 - p, 3)

            attention_steps(pe, step)

            pe.wait_ge(b_free, 4 * UNITS)
            pe.wait_ge(wsq_ready, 1)
            nc.tensor.matmul(A[:, 0:2], ones[:], wsq[:], start=True, stop=True).then_inc(wsq_summed, 1)
            pe.wait_ge(small_in, 16 * (E + 3))
            nc.tensor.matmul(B[:, E:2 * E], ones[0:1, :], bgate_row[:], start=True, stop=True).then_inc(bgate_spread, 1)
            pe.wait_ge(b1_summing, 1)
            nc.tensor.matmul(B[:, 0:1], ones[:], b1_sum[:], start=True, stop=True).then_inc(b1_summed, 1)

            def gate_logits(g, p):
                pe.wait_ge(staged, g + 1)
                wait(pe, xnT_ready, g - 1)
                for i in range(R):
                    last = nc.tensor.transpose(PT[p][:, i * P:(i + 1) * P], stage[p][:, i, :], identity[:])
                last.then_inc(stage_T, 1)
                pe.wait_ge(xnT_ready, g + 1)
                wait(pe, lg_ready, g - 1)
                for i in range(R):
                    last = nc.tensor.matmul(S[2 + p][:, i * E:(i + 1) * E], xnT[p][:, i * P:(i + 1) * P], wg_sb[:], start=True, stop=True)
                last.then_inc(lg_full, 1)

            pair_steps(pe, gate_logits)
            pe.wait_ge(totals_ready, 1)
            nc.tensor.matmul(B[:, 0:E], before[:], picked[:, HALF - 1, :], start=True, stop=True).then_inc(totals_summed, 1)
            nc.tensor.matmul(B[:, E:2 * E], ones[:], picked[:, HALF - 1, :], start=True, stop=True).then_inc(totals_summed, 1)

            w1_h, w1_l, w2_h, w2_l = (w[:].rearrange("p e b d -> p (e b d)") for w in (w_h[0], w_l[0], w_h[1], w_l[1]))

            def tile_step(s, q, e_second=None):
                tokens, first, second, weighting = tile_stages(s)
                e_first = None
                if tokens:
                    t, p = s + 1, 1 - q
                    pe.wait_ge(rows_loaded[p], 16 * (t // 2 + 1) if isinstance(t, int) else (t - p) * 8 + 16)
                    wait(pe, fx_ready, t - 1)
                    for k in range(2):
                        last = nc.tensor.transpose(AB[p][:, k * P:(k + 1) * P], rows_in[p][:, k, 0:W], identity[:])
                    last.then_inc(fxT_full, 1)
                if first:
                    t, p = s, q
                    e_first = expert_of(pe, s)
                    pe.wait_ge(fx_ready, t + 1)
                    for pair in range(2):
                        for k in range(2):
                            dst = S[2 * p + pair][:, k * TILE:(k + 1) * TILE]
                            block_at = bass.ds(e_first * HID + (2 * pair + k) * P, P)
                            nc.tensor.matmul(dst, w1_h[:, block_at], fx_h[p][:], start=True, stop=False)
                            nc.tensor.matmul(dst, w1_h[:, block_at], fx_l[p][:], start=False, stop=False)
                            last = nc.tensor.matmul(dst, w1_l[:, block_at], fx_h[p][:], start=False, stop=True)
                        last.then_inc(h_full, 1)
                if second:
                    t, p = s - 1, 1 - q
                    if e_second is None:
                        e_second = expert_of(pe, s - 1)
                    e_at = bass.ds(e_second * P, P)
                    wait(pe, y_ready, t - 1)
                    for part in (b2_h, b2_l):
                        nc.tensor.matmul(PT[p][:, 0:2 * P].rearrange("p (k d) -> p k d", k=2), ones_x[:],
                                         part[0:1, e_at].unsqueeze(1).broadcast_to([1, 2, P]),
                                         start=part is b2_h, stop=False, skip_group_check=True)
                    pe.wait_ge(hl_ready, 2 * t + 2)
                    for b in range(HB):
                        block_at = bass.ds(e_second * HID + b * P, P)
                        for h_part, w_part in ((hh, w2_h), (hl, w2_h), (hh, w2_l)):
                            for k in range(2):
                                last = nc.tensor.matmul(PT[p][:, k * P:(k + 1) * P], h_part[p][:, b, k * P:(k + 1) * P],
                                                        w_part[:, block_at], start=False,
                                                        stop=b == HB - 1 and w_part is w2_l, skip_group_check=True)
                    last.then_inc(y_full, 1)
                return e_first

            pe.wait_ge(table_ready, 1)
            pe.wait_ge(w_split, 2)
            tile_steps(pe, tile_step)


INPUTS = ["x", "L0_conv_ln_w", "L0_conv_ln_b", "L0_conv_wq", "L0_conv_wk", "L0_conv_wv", "L0_conv_wb", "L0_conv_wg_w",
          "L0_conv_wg_b", "L0_conv_wrep_w", "L0_conv_wrep_b", "L0_ffn_Wg", "L0_ffn_bg", "L0_ffn_W1", "L0_ffn_b1",
          "L0_ffn_W2", "L0_ffn_b2"]


def kernel(**inputs):
    import numpy as np
    import concourse.bacc as bacc
    from concourse.bass_utils import run_bass_kernel_spmd

    nc = bacc.Bacc("TRN2", target_bir_lowering=False, num_devices=1)
    arrays, args = {}, []
    for name in INPUTS:
        a = np.ascontiguousarray(inputs[name])
        arrays[f"in_{name}"] = a
        args.append(nc.dram_tensor(f"in_{name}", a.shape, mybir.dt.from_np(a.dtype), kind="ExternalInput").ap())
    out = nc.dram_tensor("out", list(inputs["x"].shape), F32, kind="ExternalOutput").ap()
    build(nc, *args, out)
    r = run_bass_kernel_spmd(nc, [arrays], core_ids=[0])
    return r.results[0]["out"]
```

```python
from contextlib import ExitStack

import concourse.bass as bass
from concourse import mybir

P = 128
F32 = mybir.dt.float32
F32R = mybir.dt.float32r
F16 = mybir.dt.float16
I32 = mybir.dt.int32
ALU = mybir.AluOpType
ACT = mybir.ActivationFunctionType
AX_X = mybir.AxisListType.X

RSQRT_SEED = float(0x5F3759DF)
BIG = 3.0e38


class Chain:

    def __init__(self, engine, sem):
        self.engine, self.sem, self.count = engine, sem, 0

    def link(self, instruction):
        self.count += 1
        instruction.then_inc(self.sem, 1)
        self.engine.wait_ge(self.sem, self.count)


def wait(engine, sem, value):
    if isinstance(value, int) and value <= 0:
        return
    engine.wait_ge(sem, value)


def rsqrt(nc, chain, y, v, a, b):
    seed_bits = a.bitcast(I32)
    chain.link(nc.vector.tensor_scalar(seed_bits, v.bitcast(I32), 1, None, ALU.arith_shift_right))
    chain.link(nc.vector.tensor_scalar(y.bitcast(I32), seed_bits, -1.0, RSQRT_SEED, ALU.mult, ALU.add))
    for _ in range(3):
        chain.link(nc.vector.tensor_tensor(a, y, y, ALU.mult))
        chain.link(nc.vector.scalar_tensor_tensor(b, a, -0.5, v, ALU.mult, ALU.mult))
        chain.link(nc.vector.scalar_tensor_tensor(y, b, 1.5, y, ALU.add, ALU.mult))


def build(nc, x, ln_w, ln_b, wq, wk, wv, wb, wg_w, wg_b, wrep_w, wrep_b, Wg, bg, W1, b1, W2, b2, out):
    _, C, H, W = x.shape
    NH = wb.shape[0]
    HC = wq.shape[0]
    D = HC // NH
    HALF = H // 2
    R = 4
    UNITS = H // R
    NQ = R * W
    ROWSTATS = 6
    CH = 4
    CR = HALF // CH
    E, _, HID = W1.shape
    HB = HID // P
    TOKENS = C * H
    TILE = 256
    TILES = 2 * TOKENS // TILE + E - 1
    SLOTS = TILES * TILE
    ROW = W + 4
    NOWHERE = 1 << 20
    WPIECE = E * HID // UNITS
    assert W == P and H == P and 2 * C == P and HC == P and UNITS % 2 == 0

    with ExitStack() as ctx:
        def sb(name, shape, dt=F32):
            return ctx.enter_context(nc.sbuf_tensor(name, shape, dt))

        def psum(name, shape=(P, 512), dt=F32):
            return ctx.enter_context(nc.psum_tensor(name, list(shape), dt))

        def sem(name):
            return ctx.enter_context(nc.semaphore(name))

        xt = sb("xt", [P, HALF, W])
        lnw_sb = sb("lnw_sb", [P, 2, CR, W])
        lnb_sb = sb("lnb_sb", [P, 2, CR, W])
        identity = sb("identity", [P, P])
        ones = sb("ones", [P, P])
        ones_r = sb("ones_r", [P, P], F32R)
        rowstat = sb("rowstat", [P, HALF, ROWSTATS])
        mean = sb("mean", [P, HALF])
        var = sb("var", [P, HALF])
        rstd = sb("rstd", [P, HALF])
        tmp_a = sb("tmp_a", [P, HALF])
        tmp_b = sb("tmp_b", [P, HALF])
        sums = sb("sums", [P, 8])
        gstat = sb("gstat", [P, 8])
        xsq = sb("xsq", [P, 2 * CH])
        rstd2 = sb("rstd2", [P, HALF])
        gtmp = sb("gtmp", [P, 8])
        gtmp2 = sb("gtmp2", [P, 8])
        grstd = sb("grstd", [P, 1])
        ebits = sb("ebits", [P, 4], I32)
        ebits2 = sb("ebits2", [P, 4], I32)
        scales = sb("scales", [P, 4])
        inv_scales = sb("inv_scales", [P, 4])
        logit_scale = sb("logit_scale", [P, 1])
        bias_scale = sb("bias_scale", [P, 1])
        brep = sb("brep", [P, 1])
        bgrow = sb("bgrow", [1, HC])
        wb_sb = sb("wb_sb", [P, 2 * NH])
        w_raw = [lnw_sb, lnb_sb]
        b1_sb = sb("b1_sb", [P, E, HB])
        b2_row = sb("b2_row", [1, E * P])
        wg_sb = sb("wg_sb", [P, E])
        bgate_row = sb("bgate_row", [1, E])
        wsq = sb("wsq", [P, 2])
        hscale = sb("hscale", [P, 4])
        inv_hscale = sb("inv_hscale", [P, 4])
        y_scale = sb("y_scale", [P, 1])
        order8 = sb("order8", [P, E])
        before = sb("before", [P, P])
        counts = sb("counts", [P, 2 * E])
        tiles_i = sb("tiles_i", [P, E], I32)
        tiles_f = [sb(f"tiles_f{k}", [P, E]) for k in range(3)]
        token_id = sb("token_id", [P, HALF])
        tile_no = sb("tile_no", [1, TILES])
        tile_expert = sb("tile_expert", [1, TILES])
        tile_cmp = sb("tile_cmp", [1, TILES])
        w_at = sb("w_at", [1, TILES], I32)
        b1_at = sb("b1_at", [1, TILES], I32)
        blank = sb("blank", [P, ROW])
        b1_flat = b1_sb[:].rearrange("p e b -> p (e b)")
        b1_sq = sb("b1_sq", [P, E * HB])
        b1_sum = sb("b1_sum", [P, 1])
        bgate_all = sb("bgate_all", [P, E])
        tiles_j = sb("tiles_j", [P, E], I32)
        first_row = sb("first_row", [P, E])
        first_row2 = sb("first_row2", [P, E])

        attention_memory = ExitStack()

        def sba(name, shape, dt=F32):
            return attention_memory.enter_context(nc.sbuf_tensor(name, shape, dt))

        x1 = sba("x1", [P, HALF, W])
        wraw = sba("wraw", [P, 4, 2, C])
        w4h = sba("w4h", [P, 4, P], F32R)
        w4l = sba("w4l", [P, 2, 4, P], F32R)
        wrep_raw = sba("wrep_raw", [C, HC])
        wrep_ordered = sba("wrep_ordered", [C, HC])
        wrepT = sba("wrepT", [P, P])
        wrep_h = sba("wrep_h", [P, P], F32R)
        wrep_l = sba("wrep_l", [P, P], F32R)
        bg_f = sba("bg_f", [P, HC])
        bg_h = sba("bg_h", [P, HC], F32R)
        bg_l = sba("bg_l", [P, HC], F32R)
        bias_rows = sba("bias_rows", [2 * NH, HALF * W])
        biasN = sba("biasN", [P, NH, P])
        xf = sba("xf", [P, NQ])
        xs = [sba(f"xs{p}", [P, NQ], F32R) for p in range(2)]
        qk = [[[sba(f"{n}{part}{p}", [P, NQ], F16) for p in range(2)] for part in "hl"] for n in "qk"]
        L = [sba(f"L{p}", [P, NH, R, P]) for p in range(2)]
        square_junk = L[0][:].rearrange("p h i k -> p (h i k)")[:, 0:CR * W // 2]
        lmin = [sba(f"lmin{p}", [P, NH * R]) for p in range(2)]
        ph = [sba(f"ph{p}", [P, NH * P], F16) for p in range(2)]
        pl = [sba(f"pl{p}", [P, NH * P], F16) for p in range(2)]
        vh = [sba(f"vh{p}", [P, R, NH, D + 1], F16) for p in range(2)]
        vl = [sba(f"vl{p}", [P, R, NH, D + 1], F16) for p in range(2)]
        gt = [sba(f"gt{p}", [P, R, HC]) for p in range(2)]
        turn = [sba(f"turn{k}", [P, 1]) for k in range(2)]
        rden = [sba(f"rden{k}", [P, 2, NH]) for k in range(2)]
        on = [sba(f"on{k}", [P, 2, HC]) for k in range(2)]
        og = [sba(f"og{p}", [P, R, HC]) for p in range(2)]
        w4 = og[0]
        ogT_h = sba("ogT_h", [P, NQ], F32R)
        ogT_l = sba("ogT_l", [P, NQ], F32R)
        attention_memory.close()

        def sbm(name, shape, dt=F32):
            return ctx.enter_context(nc.sbuf_tensor(name, shape, dt))

        pay = sbm("pay", [P, HALF, ROW])
        w_h = [sbm(f"w{n}_h", [P, E, HB, P], F16) for n in (1, 2)]
        w_l = [sbm(f"w{n}_l", [P, E, HB, P], F16) for n in (1, 2)]
        b2_parts = sbm("b2_parts", [1, E, HB, P], F32R)
        ones_x = sbm("ones_x", [1, P], F32R)
        stage = [sbm(f"stage{p}", [P, R, P]) for p in range(2)]
        xnT = [sbm(f"xnT{p}", [P, R * P]) for p in range(2)]
        lg = sbm("lg", [P, HALF, E])
        r_a = sbm("r_a", [P, HALF, E])
        r_b = sbm("r_b", [P, HALF, E])
        oh = [sbm(f"oh{k}", [P, HALF, E]) for k in range(2)]
        picked = sbm("picked", [P, HALF, E])
        top = [sbm(f"top{k}", [P, HALF]) for k in range(2)]
        key = sbm("key", [P, HALF])
        gate_e = sbm("gate_e", [P, HALF])
        weight = [sbm(f"weight{k}", [P, HALF]) for k in range(2)]
        posf = sbm("posf", [P, HALF])
        pos = [sbm(f"pos{k}", [P, HALF], I32) for k in range(2)]
        rows_in = [sbm(f"rows_in{p}", [P, 2, ROW]) for p in range(2)]
        fx_h = [sbm(f"fx_h{p}", [P, TILE], F16) for p in range(2)]
        fx_l = [sbm(f"fx_l{p}", [P, TILE], F16) for p in range(2)]
        hf = [sbm(f"hf{p}", [P, HB, TILE]) for p in range(2)]
        hh = [sbm(f"hh{p}", [P, HB, TILE], F16) for p in range(2)]
        hl = [sbm(f"hl{p}", [P, HB, TILE], F16) for p in range(2)]
        meta = sbm("meta", [P, TILES, 2, 2])
        yidx = [sbm(f"yidx{p}", [P, 2], I32) for p in range(2)]
        yo = [sbm(f"yo{p}", [P, 2, P]) for p in range(2)]
        yin = w_raw

        routed = nc.dram_tensor("routed", [SLOTS, ROW], F32, kind="Internal").ap()
        expert_out = nc.dram_tensor("expert_out", [2 * TOKENS + TILES, W], F32, kind="Internal").ap()

        S = [psum(f"S{h}") for h in range(NH)]
        PT = [psum(f"PT{i}") for i in range(2)]
        A = psum("A")
        B = psum("B")
        AB = [A, B]

        x_in = [sem(f"x_in{c}") for c in range(CH)]
        lnw_in = [sem(f"lnw_in{c}") for c in range(2)]
        lnb_in = [sem(f"lnb_in{c}") for c in range(2)]
        w_in = sem("w_in")
        const_ready = sem("const_ready")
        pool_step = sem("pool_step")
        dve_step = sem("dve_step")
        act_step = sem("act_step")
        lnw_used = sem("lnw_used")
        x1_ready = sem("x1_ready")
        rowvar_ready = sem("rowvar_ready")
        rowvar_summed = sem("rowvar_summed")
        squares_ready = sem("squares_ready")
        squares_summed = sem("squares_summed")
        w_transposed = sem("w_transposed")
        bias_done = sem("bias_done")
        bias_copied = sem("bias_copied")
        bias_in = sem("bias_in")
        wrep_transposed = sem("wrep_transposed")
        wb_in = sem("wb_in")
        sums_ready = sem("sums_ready")
        wrep_reordered = sem("wrep_reordered")
        weights_ready = sem("weights_ready")
        xf_ready = sem("xf_ready")
        xs_high = sem("xs_high")
        xs_ready = sem("xs_ready")
        s_full = sem("s_full")
        qk_full = sem("qk_full")
        qk_high = sem("qk_high")
        qk_low = sem("qk_low")
        vg_full = sem("vg_full")
        vg_high = sem("vg_high")
        vg_low = sem("vg_low")
        norm_done = sem("norm_done")
        og_part = sem("og_part")
        ogt_low = sem("ogt_low")
        res_done = sem("res_done")
        logits_ready = sem("logits_ready")
        exp_done = sem("exp_done")
        pt_full = sem("pt_full")
        ph_ready = sem("ph_ready")
        pl_ready = sem("pl_ready")
        pv_done = sem("pv_done")
        rden_ready = sem("rden_ready")
        og_ready = sem("og_ready")
        ogt_full = sem("ogt_full")
        ogt_high = sem("ogt_high")
        oproj_done = sem("oproj_done")
        attention_done = sem("attention_done")
        ffn_in = sem("ffn_in")
        small_in = sem("small_in")
        wsq_ready = sem("wsq_ready")
        b1_summing = sem("b1_summing")
        b1_summed = sem("b1_summed")
        dve_step2 = sem("dve_step2")
        wsq_summed = sem("wsq_summed")
        hscale_ready = sem("hscale_ready")
        w_high = sem("w_high")
        w_split = sem("w_split")
        bgate_spread = sem("bgate_spread")
        b2_ready = sem("b2_ready")
        blanked = sem("blanked")
        xn_ready = sem("xn_ready")
        staged = sem("staged")
        stage_T = sem("stage_T")
        xnT_ready = sem("xnT_ready")
        lg_full = sem("lg_full")
        gap_ready = sem("gap_ready")
        gate_exp = sem("gate_exp")
        totals_ready = sem("totals_ready")
        totals_summed = sem("totals_summed")
        meta_ready = sem("meta_ready")
        scattered = [sem(f"scattered{k}") for k in range(2)]
        table_ready = sem("table_ready")
        rows_loaded = [sem(f"rows_loaded{p}") for p in range(2)]
        fxT_full = sem("fxT_full")
        fx_high = sem("fx_high")
        fx_ready = sem("fx_ready")
        h_full = sem("h_full")
        gelu_done = sem("gelu_done")
        meta_kept = sem("meta_kept")
        hh_ready = sem("hh_ready")
        hl_ready = sem("hl_ready")
        y_full = sem("y_full")
        y_biased = sem("y_biased")
        y_ready = sem("y_ready")
        yidx_ready = sem("yidx_ready")
        y_sent = [sem(f"y_sent{p}") for p in range(2)]
        y_in = [sem(f"y_in{p}") for p in range(2)]
        y_added = sem("y_added")
        out_ready = sem("out_ready")
        stored = sem("stored")

        xv = x[0].rearrange("c (f i) j -> f c i j", f=2)
        lwv = ln_w.rearrange("c (f i) j -> f c i j", f=2)
        lbv = ln_b.rearrange("c (f i) j -> f c i j", f=2)
        outv = out[0].rearrange("c (f i) j -> f c i j", f=2)
        NWDMA = 17

        def chunk(c):
            return slice(c * CR, (c + 1) * CR)

        block = ctx.enter_context(nc.Block())

        FIRST = 6
        LAST = UNITS + 3

        def attention_steps(step, engine):
            for s in range(FIRST):
                step(s, s % 2)
            with engine.Fori(FIRST // 2, UNITS // 2) as g:
                step(2 * g, 0)
                step(2 * g + 1, 1)
            for s in range(UNITS, LAST):
                step(s, s % 2)

        def unit(s, p, delay, operation, *args):
            u = s - delay
            if not isinstance(u, int) or 0 <= u < UNITS:
                operation(u, (p + delay) % 2, *args)

        def rows(u, p):
            if isinstance(u, int):
                return slice((u // 2) * R, (u // 2) * R + R)
            g0 = (u - p) * (R // 2)
            return bass.ds(g0, R)

        BODY = 8

        def tile_steps(engine, step):
            assert (TILES - 7) % BODY == 0
            step(-1, 1)
            e = step(0, 0)
            for s in range(1, 6):
                e = step(s, s % 2, e)
            with engine.Fori(0, (TILES - 7) // BODY) as g:
                e = step(BODY * g + 6, 0)
                for k in range(1, BODY):
                    e = step(BODY * g + 6 + k, k % 2, e)
            e = step(TILES - 1, 0)
            step(TILES, 1, e)
            step(TILES + 1, 0)

        def tile_stages(s):
            if not isinstance(s, int):
                return True, True, True, True
            return s + 1 < TILES, 0 <= s < TILES, 1 <= s <= TILES, s >= 2

        def tile_at(t):
            return slice(t, t + 1) if isinstance(t, int) else bass.ds(t, 1)

        def expert_of(engine, table, t, step):
            return engine.value_load(table[0:1, tile_at(t)], min_val=0, max_val=(E - 1) * step)

        GROUPS = HALF // R

        def group_steps(engine, step):
            step(0, 0)
            step(1, 1)
            with engine.Fori(1, GROUPS // 2) as g:
                step(2 * g, 0)
                step(2 * g + 1, 1)
            step(GROUPS, 0)

        def row_statistics(first, stop):
            for i in range(first, stop):
                last = nc.vector.bn_stats(rowstat[:, i, :], xt[:, i, :])
            return last

        def row_scales(chain, k, eps):
            me, ve = rowstat[:, k, 1], rowstat[:, k, 2]
            mo, vo = rowstat[:, k, 4], rowstat[:, k, 5]
            chain.link(nc.vector.tensor_tensor(mean[:, k], me, mo, ALU.add))
            chain.link(nc.vector.tensor_scalar(mean[:, k], mean[:, k], 0.5, None, ALU.mult))
            chain.link(nc.vector.tensor_tensor(tmp_a[:, k], me, mo, ALU.subtract))
            chain.link(nc.vector.scalar_tensor_tensor(tmp_a[:, k], tmp_a[:, k], 0.25, tmp_a[:, k], ALU.mult, ALU.mult))
            chain.link(nc.vector.tensor_tensor(tmp_b[:, k], ve, vo, ALU.add))
            chain.link(nc.vector.scalar_tensor_tensor(var[:, k], tmp_b[:, k], 1.0 / W, tmp_a[:, k], ALU.mult, ALU.add))
            chain.link(nc.vector.tensor_scalar(rstd2[:, k], var[:, k], eps, None, ALU.add))
            rsqrt(nc, chain, rstd[:, k], rstd2[:, k], tmp_a[:, k], tmp_b[:, k])

        def power_of_two(chain, scale, square, bits, bits2):
            chain.link(nc.vector.tensor_scalar(bits, square.bitcast(I32), 23, None, ALU.arith_shift_right))
            chain.link(nc.vector.tensor_scalar(bits2, bits, -125.0, None, ALU.add))
            chain.link(nc.vector.tensor_scalar(bits, bits2, 1, None, ALU.arith_shift_right))
            chain.link(nc.vector.tensor_scalar(bits2, bits, -1.0, 141.0, ALU.mult, ALU.add))
            chain.link(nc.vector.tensor_scalar(scale.bitcast(I32), bits2, 23, None, ALU.arith_shift_left))

        @block.sync
        def _(sp):
            for c in range(CH):
                for f in range(2):
                    sp.dma_start(xt[f * C:(f + 1) * C, chunk(c), :], xv[f, :, chunk(c), :]).then_inc(x_in[c], 16)
                if c == 0:
                    for n, w in enumerate((wq, wk, wv, wg_w)):
                        for f in range(2):
                            sp.dma_start(wraw[:, n, f, :], w).then_inc(w_in, 16)
            for f in range(2):
                sp.dma_start(brep[f * C:(f + 1) * C, :], wrep_b.rearrange("(c o) -> c o", o=1)).then_inc(w_in, 16)
            sp.dma_start(wrep_raw[:], wrep_w).then_inc(w_in, 16)
            sp.dma_start(bgrow[:], wg_b.rearrange("(o c) -> o c", o=1)).then_inc(w_in, 16)
            sp.wait_ge(bias_copied, HALF // R)
            for f in range(2):
                for h in range(NH):
                    sp.dma_start(biasN[f * C:(f + 1) * C, h, :],
                                 bias_rows[f * NH + h:f * NH + h + 1, :].rearrange("o (i k) -> o i k", i=HALF)).then_inc(bias_in, 16)
            sp.wait_ge(x1_ready, CH)
            sp.dma_start(w_raw[0][:].rearrange("p a r w -> p (a r w)").rearrange("p (e h) -> p e h", e=E),
                         W1.rearrange("e d h -> d e h")).then_inc(ffn_in, 16)
            sp.dma_start(w_raw[1][:].rearrange("p a r w -> p (a r w)").rearrange("p (e b d) -> p e b d", e=E, b=HB),
                         W2.rearrange("e (b p) d -> p e b d", p=P)).then_inc(ffn_in, 16)
            for e in range(E):
                sp.dma_start(b1_sb[:, e, :], b1[e].rearrange("(b p) -> p b", p=P),
                             allow_slow_non_contiguous=True).then_inc(small_in, 16)
            sp.dma_start(b2_row[:], b2.rearrange("(o e) d -> o (e d)", o=1)).then_inc(small_in, 16)
            sp.dma_start(wg_sb[:], Wg).then_inc(small_in, 16)
            sp.dma_start(bgate_row[:], bg.rearrange("(o e) -> o e", o=1)).then_inc(small_in, 16)

            sp.wait_ge(const_ready, 1)
            sp.dma_start(routed.rearrange("(n p) w -> p n w", p=P),
                         blank[:].unsqueeze(1).broadcast_to([P, SLOTS // P, ROW])).then_inc(blanked, 16)

            routed_v = routed.rearrange("(t k p) w -> t p k w", k=2, p=P)

            def load_rows(t, p):
                wait(sp, meta_kept, t - 1)
                sp.dma_start(rows_in[p][:], routed_v[t]).then_inc(rows_loaded[p], 16)

            for k in range(2):
                sp.wait_ge(scattered[k], 16 * HALF)
            load_rows(0, 0)
            load_rows(1, 1)
            with sp.Fori(1, (TILES - 1) // 2) as g:
                load_rows(2 * g, 0)
                load_rows(2 * g + 1, 1)
            load_rows(TILES - 1, 0)

            for p in range(2):
                sp.wait_ge(y_sent[p], 32 * ((TILES + 1 - p) // 2))
            ev = expert_out[0:2 * TOKENS].rearrange("(s c f i) w -> s f c i w", s=2, f=2, i=HALF)
            for c in range(CH):
                wait(sp, y_added, c - 1)
                for f in range(2):
                    for k in range(2):
                        sp.dma_start(yin[c % 2][f * C:(f + 1) * C, k], ev[k, f, :, chunk(c), :]).then_inc(y_in[c % 2], 16)
            for c in range(CH):
                sp.wait_ge(y_added, c + 1)
                for f in range(2):
                    sp.dma_start(outv[f, :, chunk(c), :], xt[f * C:(f + 1) * C, chunk(c), :]).then_inc(stored, 16)
            sp.wait_ge(stored, 32 * CH)

        @block.gpsimd
        def _(pool):
            chain = Chain(pool, pool_step)
            chain.link(nc.gpsimd.memset(identity[:], 0.0))
            chain.link(nc.gpsimd.affine_select(out=identity[:], in_=identity[:], compare_op=ALU.not_equal, fill=1.0,
                                               base=0, pattern=[[-1, P]], channel_multiplier=1))
            chain.link(nc.gpsimd.memset(wb_sb[:], 0.0))
            for f in range(2):
                pool.dma_start(wb_sb[f * C:(f + 1) * C, f * NH:(f + 1) * NH], wb.rearrange("h c -> c h"),
                               allow_slow_non_contiguous=True).then_inc(wb_in, 16)
            chain.link(nc.gpsimd.memset(ones[:], 1.0))
            chain.link(nc.gpsimd.memset(bg_f[:], 0.0))
            chain.link(nc.gpsimd.memset(w4l[:].bitcast(F32), 0.0))
            for p in range(2):
                chain.link(nc.gpsimd.memset(vh[p][:], 1.0))
                chain.link(nc.gpsimd.memset(vl[p][:], 0.0))
            for e in range(E):
                chain.link(nc.gpsimd.memset(order8[:, e:e + 1], float(E - e)))
            chain.link(nc.gpsimd.memset(before[:], 1.0))
            chain.link(nc.gpsimd.affine_select(out=before[:], in_=before[:], compare_op=ALU.is_gt, fill=0.0, base=0,
                                               pattern=[[1, P]], channel_multiplier=-1))
            for f in range(2):
                chain.link(nc.gpsimd.iota(token_id[f * C:(f + 1) * C, :], [[1, HALF]], base=f * HALF,
                                          channel_multiplier=H, allow_small_or_imprecise_dtypes=True))
            chain.link(nc.gpsimd.iota(tile_no[:], [[1, TILES]], base=0, channel_multiplier=0,
                                      allow_small_or_imprecise_dtypes=True))
            chain.link(nc.gpsimd.memset(blank[:], 0.0))
            nc.gpsimd.memset(blank[:, W + 1:W + 2], float(NOWHERE)).then_inc(const_ready, 1)

            def copy_x1(u, p):
                if p == 0:
                    wait(pool, xs_ready, u)
                    nc.gpsimd.tensor_copy(xf[:].rearrange("p (r w) -> p r w", w=W), x1[:, rows(u, 0), :]).then_inc(xf_ready, 1)

            def low_x(u, p):
                hi = slice(p * C, (p + 1) * C)
                lo = slice((1 - p) * C, (2 - p) * C)
                pool.wait_ge(xs_high, u + 1)
                wait(pool, og_ready, 2 * (u - 2))
                nc.gpsimd.tensor_tensor(xs[p][lo], xf[hi], xs[p][hi], ALU.subtract).then_inc(xs_ready, 1)

            def gate(u, p, half):
                pool.wait_ge(norm_done, 2 * u + half + 1)
                if half == 0:
                    wait(pool, ogt_full, u - 1)
                    pool.wait_ge(xs_ready, min(u + 3, UNITS) if isinstance(u, int) else u + 3)
                k = slice(2 * half, 2 * half + 2)
                nc.gpsimd.tensor_tensor(og[p][:, k, :], gt[p][:, k, :], on[half][:], ALU.mult).then_inc(og_part, 1)
                pool.wait_ge(og_part, 2 * u + half + 1)
                nc.gpsimd.tensor_tensor(og[p][:, k, :], og[p][:, k, :], on[half][:], ALU.add).then_inc(og_ready, 1)

            def step(s, p):
                unit(s, p, 0, copy_x1)
                unit(s, p, 3, gate, 0)
                unit(s, p, 3, gate, 1)
                unit(s, p, 0, low_x)

            pool.wait_ge(x1_ready, CH)
            attention_steps(step, pool)

            pool.wait_ge(blanked, 16)
            for k in range(2):
                pool.wait_ge(meta_ready, k + 1)
                for i in range(HALF):
                    pool.indirect_dma_start(routed, bass.IndirectOffsetOnAxis(ap=pos[k][:, i:i + 1], axis=0),
                                            pay[:, i, :], None).then_inc(scattered[k], 16)

            def send_rows(s, q, _=None):
                if isinstance(s, int) and s < 2:
                    return
                t, p = s - 2, q
                pool.wait_ge(yidx_ready, t + 1)
                pool.wait_ge(y_ready, t + 1)
                last_place = 2 * TOKENS - 1 + t
                for k in range(2):
                    pool.indirect_dma_start(
                        expert_out, bass.IndirectOffsetOnAxis(ap=yidx[p][:, k:k + 1], axis=0),
                        yo[p][:, k, :], None, bounds_check=last_place, oob_is_err=False).then_inc(y_sent[p], 16)

            tile_steps(pool, send_rows)

        @block.scalar
        def _(act):
            for c in range(CH):
                if c >= 2:
                    act.wait_ge(lnw_used, c - 1)
                for f in range(2):
                    act.dma_start(lnw_sb[f * C:(f + 1) * C, c % 2], lwv[f, :, chunk(c), :]).then_inc(lnw_in[c % 2], 16)
                if c < 2:
                    for f in range(2):
                        act.dma_start(lnb_sb[f * C:(f + 1) * C, c % 2], lbv[f, :, chunk(c), :]).then_inc(lnb_in[c % 2], 16)
            chain = Chain(act, act_step)
            act.wait_ge(w_in, 12 * 16)
            nc.scalar.activation(wrep_ordered[:].rearrange("o (h c) -> o h c", h=NH),
                                 wrep_raw[:].rearrange("o (c h) -> o h c", h=NH), ACT.Copy).then_inc(wrep_reordered, 1)
            for n in range(3):
                chain.link(nc.scalar.activation(square_junk[:, 0:C], wraw[:, n, 0, :], ACT.Square,
                                                accum_out=sums[:, n:n + 1]))
            for c in range(CH):
                act.wait_ge(x1_ready, c + 1)
                if c + 2 < CH:
                    for f in range(2):
                        act.dma_start(lnb_sb[f * C:(f + 1) * C, c % 2], lbv[f, :, chunk(c + 2), :]).then_inc(lnb_in[c % 2], 16)
                for k in range(2):
                    last = nc.scalar.activation(square_junk.rearrange("p (r w) -> p r w", w=W),
                                                x1[:, c * CR + k * CR // 2:c * CR + (k + 1) * CR // 2, :],
                                                ACT.Square, accum_out=xsq[:, 2 * c + k:2 * c + k + 1])
                    if c == CH - 1 and k == 1:
                        last.then_inc(squares_ready, 1)
                    else:
                        chain.link(last)
                for n in range(c * (CR // R), (c + 1) * (CR // R)):
                    act.wait_ge(bias_done, n + 1)
                    nc.scalar.activation(bias_rows[:, n * NQ:(n + 1) * NQ], S[n % 4][0:2 * NH, :], ACT.Copy).then_inc(bias_copied, 1)

            def high_x(u, p):
                act.wait_ge(xf_ready, (u - p) // 2 + 1)
                wait(act, vg_full, 2 * (u - 1))
                hi = slice(p * C, (p + 1) * C)
                nc.scalar.activation(xs[p][hi], xf[hi], ACT.Copy).then_inc(xs_high, 1)

            def high_qk(u, p, n):
                act.wait_ge(qk_full, 2 * u + n + 1)
                if n == 0:
                    wait(act, s_full, 2 * (u - 1))
                nc.scalar.activation(qk[n][0][p][:], A[:], ACT.Copy).then_inc(qk_high, 1)

            def gate_and_high_v(u, p, half):
                act.wait_ge(vg_full, 2 * u + half + 1)
                wait(act, og_ready, 2 * (u - 2) + half + 1)
                av = A[:].rearrange("p (r s c) -> p r s c", r=2, s=2)
                nc.scalar.activation(gt[p][:, 2 * half:2 * half + 2, :], av[:, :, 1, :], ACT.Tanh, scale=0.5)
                nc.scalar.activation(vh[p][:, 2 * half:2 * half + 2, :, 0:D],
                                     av[:, :, 0, :].rearrange("p r (h d) -> p r h d", d=D), ACT.Copy).then_inc(vg_high, 1)

            def high_p(u, p, i):
                act.wait_ge(pt_full, 4 * u + i + 1)
                wait(act, pv_done, 4 * u + i - 1)
                nc.scalar.activation(ph[i % 2][:], PT[i % 2][:], ACT.Copy).then_inc(ph_ready, 1)

            def exponentials(u, p, h):
                act.wait_ge(logits_ready, 4 * u + h + 1)
                for i in range(R):
                    last = nc.scalar.activation(L[p][:, h, i, :], L[p][:, h, i, :], ACT.Exp, scale=-1.0,
                                                bias=lmin[p][:, h * R + i:h * R + i + 1])
                last.then_inc(exp_done, 1)

            def high_og(u, p):
                act.wait_ge(ogt_full, u + 1)
                wait(act, oproj_done, u)
                nc.scalar.activation(ogT_h[:], B[:], ACT.Copy).then_inc(ogt_high, 1)

            def step(s, p):
                unit(s, p, 2, exponentials, 3)
                unit(s, p, 1, gate_and_high_v, 0)
                unit(s, p, 2, high_p, 0)
                unit(s, p, 0, high_x)
                unit(s, p, 2, high_p, 1)
                unit(s, p, 1, gate_and_high_v, 1)
                unit(s, p, 3, high_og)
                unit(s, p, 1, exponentials, 0)
                unit(s, p, 0, high_qk, 0)
                unit(s, p, 1, exponentials, 1)
                unit(s, p, 0, high_qk, 1)
                unit(s, p, 2, high_p, 2)
                unit(s, p, 2, high_p, 3)
                unit(s, p, 1, exponentials, 2)

            attention_steps(step, act)

            def stage_rows(g, p):
                act.wait_ge(xn_ready, g + 1)
                wait(act, stage_T, g - 1)
                nc.scalar.activation(stage[p][:], pay[:, bass.ds(g * R, R), 0:W], ACT.Copy).then_inc(staged, 1)

            def copy_transposed(g, p):
                act.wait_ge(stage_T, g + 1)
                wait(act, lg_full, g - 1)
                nc.scalar.activation(xnT[p][:], PT[p][:], ACT.Copy).then_inc(xnT_ready, 1)

            def step(s, p):
                if not isinstance(s, int) or s < GROUPS:
                    stage_rows(s, p)
                if not isinstance(s, int) or s >= 1:
                    copy_transposed(s - 1, 1 - p)

            group_steps(act, step)
            act.wait_ge(gap_ready, 1)
            nc.scalar.activation(gate_e[:], key[:], ACT.Exp).then_inc(gate_exp, 1)

            act.wait_ge(ffn_in, 32)
            act.wait_ge(res_done, UNITS)
            for n in range(2):
                raw = w_raw[n][:].rearrange("p a r w -> p (a r w)")
                last = nc.scalar.activation(w_h[n][:].rearrange("p e b d -> p (e b d)"), raw, ACT.Square,
                                            accum_out=wsq[:, n:n + 1])
                if n == 0:
                    chain.link(last)
                else:
                    last.then_inc(wsq_ready, 1)

            act.wait_ge(hscale_ready, 1)
            for n in range(2):
                nc.scalar.activation(w_h[n][:].rearrange("p e b d -> p (e b d)"), w_raw[n][:].rearrange("p a r w -> p (a r w)"),
                                     ACT.Copy, scale=hscale[:, n:n + 1]).then_inc(w_high, 1)

            def tile_step(s, q, _=None):
                tokens, first, second, weighting = tile_stages(s)
                if tokens:
                    t, p = s + 1, 1 - q
                    act.wait_ge(fxT_full, t + 1)
                    nc.scalar.activation(fx_h[p][:], AB[p][:, 0:TILE], ACT.Copy).then_inc(fx_high, 1)
                if first:
                    t, p = s, q
                    e = expert_of(act, b1_at, s, HB)
                    for pair in range(2):
                        act.wait_ge(h_full, 2 * t + pair + 1)
                        for k in range(2):
                            b = 2 * pair + k
                            last = nc.scalar.activation(hf[p][:, b, :], S[2 * p + pair][:, k * TILE:(k + 1) * TILE], ACT.Gelu,
                                                        scale=inv_hscale[:, 0:1], bias=b1_flat[:, bass.ds(e + b, 1)])
                        last.then_inc(gelu_done, 1)
                if weighting:
                    t, p = s - 2, q
                    wait(act, y_sent[p], (t // 2) * 32 if isinstance(t, int) else (t - p) * 16)
                    act.wait_ge(y_full, t + 1)
                    for k in range(2):
                        last = nc.scalar.activation(yo[p][:, k, :], PT[p][:, k * P:(k + 1) * P], ACT.Copy,
                                                    scale=meta[:, tile_at(t), k, 0:1])
                    last.then_inc(y_ready, 1)

            act.wait_ge(table_ready, 1)
            act.wait_ge(small_in, 16 * (E + 3))
            tile_steps(act, tile_step)

        @block.vector
        def _(dve):
            chain = Chain(dve, dve_step)
            for c in range(CH):
                dve.wait_ge(x_in[c], 32)
                chain.link(row_statistics(c * CR, (c + 1) * CR))
                row_scales(chain, chunk(c), 1e-6)
                k = chunk(c)
                for i in range(c * CR, (c + 1) * CR):
                    last = nc.vector.tensor_scalar(x1[:, i, :], xt[:, i, :], mean[:, i:i + 1], rstd[:, i:i + 1],
                                                   ALU.subtract, ALU.mult)
                chain.link(last)
                dve.wait_ge(lnw_in[c % 2], 32 * (c // 2 + 1))
                nc.vector.tensor_tensor(x1[:, k, :], x1[:, k, :], lnw_sb[:, c % 2], ALU.mult).then_inc(lnw_used, 1)
            chain.link(nc.vector.tensor_tensor(tmp_a[:], rstd[:], rstd[:], ALU.mult))
            chain.link(nc.vector.tensor_tensor(tmp_b[:], tmp_a[:], var[:], ALU.mult))
            nc.vector.tensor_reduce(gstat[:, 0:1], tmp_b[:], AX_X, ALU.add).then_inc(rowvar_ready, 1)
            dve.wait_ge(const_ready, 1)
            dve.wait_ge(w_in, 12 * 16)
            chain.link(nc.vector.tensor_copy(bg_f[0:1, :], bgrow[:]))
            chain.link(nc.vector.tensor_copy(bg_h[:], bg_f[:]))
            chain.link(nc.vector.tensor_tensor(bg_l[:], bg_f[:], bg_h[:], ALU.subtract))
            chain.link(nc.vector.tensor_copy(ones_r[:], ones[:]))
            dve.wait_ge(rowvar_summed, 1)
            chain.link(nc.vector.tensor_scalar(gstat[:, 1:2], B[:, 0:1], 1.0 / (P * HALF), 1e-5, ALU.mult, ALU.add))
            rsqrt(nc, chain, grstd[:], gstat[:, 1:2], gtmp[:, 0:1], gtmp2[:, 0:1])
            dve.wait_ge(lnw_used, CH)
            for c in range(CH):
                k = chunk(c)
                dve.wait_ge(lnb_in[c % 2], 32 * (c // 2 + 1))
                nc.vector.scalar_tensor_tensor(x1[:, k, :], x1[:, k, :], grstd[:, 0:1], lnb_sb[:, c % 2],
                                               ALU.mult, ALU.add).then_inc(x1_ready, 1)
            dve.wait_ge(squares_ready, 1)
            nc.vector.tensor_reduce(sums[:, 3:4], xsq[:], AX_X, ALU.add).then_inc(sums_ready, 1)
            dve.wait_ge(squares_summed, 1)
            chain.link(nc.vector.tensor_copy(gstat[:, 0:4], B[:, 0:4]))
            chain.link(nc.vector.tensor_scalar(gstat[:, 4:7], gstat[:, 0:3], gstat[:, 3:4], 1e-30, ALU.mult, ALU.max))
            power_of_two(chain, scales[:, 0:3], gstat[:, 4:7], ebits[:, 0:3], ebits2[:, 0:3])
            chain.link(nc.vector.reciprocal(inv_scales[:, 0:3], scales[:, 0:3]))
            chain.link(nc.vector.tensor_scalar(bias_scale[:], scales[:, 0:1], scales[:, 1:2], float(D) ** 0.5, ALU.mult, ALU.mult))
            chain.link(nc.vector.tensor_scalar(logit_scale[:], inv_scales[:, 0:1], inv_scales[:, 1:2], -float(D) ** -0.5, ALU.mult, ALU.mult))
            dve.wait_ge(w_transposed, 1)
            for n in range(3):
                last = nc.vector.tensor_scalar(w4[:, n, :], PT[0][:, n * P:(n + 1) * P], scales[:, n:n + 1], None, ALU.mult)
            chain.link(nc.vector.tensor_copy(w4[:, 3, :], PT[0][:, 3 * P:4 * P]))
            chain.link(nc.vector.tensor_copy(w4h[:], w4[:]))
            for f in range(2):
                k = slice(f * C, (f + 1) * C)
                last = nc.vector.tensor_tensor(w4l[k, f], w4[k], w4h[k], ALU.subtract)
            chain.link(last)
            dve.wait_ge(wrep_transposed, 1)
            for f in range(2):
                last = nc.vector.tensor_scalar(wrepT[:, f * C:(f + 1) * C], PT[1][:, 0:C], inv_scales[:, 2:3], 0.5, ALU.mult, ALU.mult)
            chain.link(last)
            chain.link(nc.vector.tensor_copy(wrep_h[:], wrepT[:]))
            chain.link(nc.vector.tensor_tensor(wrep_l[:], wrepT[:], wrep_h[:], ALU.subtract))
            nc.vector.tensor_copy(turn[0][:], scales[:, 0:1]).then_inc(weights_ready, 1)
            dve.wait_ge(bias_in, 2 * NH * 16)
            chain.link(nc.vector.tensor_scalar(biasN[:], biasN[:], bias_scale[:, 0:1], None, ALU.mult))

            def low_qk(u, p, n):
                dve.wait_ge(qk_high, 2 * u + n + 1)
                nc.vector.tensor_tensor(qk[n][1][p][:], A[:], qk[n][0][p][:], ALU.subtract).then_inc(qk_low, 1)

            def low_v(u, p, half):
                dve.wait_ge(vg_high, 2 * u + half + 1)
                av = A[:].rearrange("p (r s c) -> p r s c", r=2, s=2)
                nc.vector.tensor_tensor(vl[p][:, 2 * half:2 * half + 2, :, 0:D],
                                        av[:, :, 0, :].rearrange("p r (h d) -> p r h d", d=D),
                                        vh[p][:, 2 * half:2 * half + 2, :, 0:D], ALU.subtract).then_inc(vg_low, 1)

            def low_p(u, p, i):
                dve.wait_ge(ph_ready, 4 * u + i + 1)
                nc.vector.tensor_tensor(pl[i % 2][:], PT[i % 2][:], ph[i % 2][:], ALU.subtract).then_inc(pl_ready, 1)

            def logits(u, p, h):
                if h % 2 == 0:
                    dve.wait_ge(s_full, 2 * u + h // 2 + 1)
                    if h == 0:
                        wait(dve, pt_full, 4 * (u - 1))
                    nc.vector.memset(turn[h // 2][:], 0.0)
                for i in range(R):
                    last = nc.vector.tensor_tensor_reduce(
                        out=L[p][:, h, i, :], in0=S[h][:, i * P:(i + 1) * P], in1=biasN[:, h, :],
                        scale=logit_scale[:, 0:1], scalar=BIG, op0=ALU.add, op1=ALU.min,
                        accum_out=lmin[p][:, h * R + i:h * R + i + 1])
                last.then_inc(logits_ready, 1)

            def normalise(u, p, half):
                dve.wait_ge(pv_done, 4 * u + 2 * half + 2)
                ov = B[:, 0:2 * NH * (D + 1)].rearrange("p (r h d) -> p r h d", r=2, h=NH)
                wait(dve, og_ready, 2 * u + half - 1)
                nc.vector.reciprocal(rden[half][:], ov[:, :, :, D]).then_inc(rden_ready, 1)
                dve.wait_ge(rden_ready, 2 * u + half + 1)
                nc.vector.tensor_tensor(on[half][:].rearrange("p r (h d) -> p r h d", d=D), ov[:, :, :, 0:D],
                                        rden[half][:].unsqueeze(3).broadcast_to([P, 2, NH, D]), ALU.mult).then_inc(norm_done, 1)

            def low_og(u, p):
                dve.wait_ge(ogt_high, u + 1)
                nc.vector.tensor_tensor(ogT_l[:], B[:], ogT_h[:], ALU.subtract).then_inc(ogt_low, 1)

            def residual(u, p):
                dve.wait_ge(oproj_done, u + 1)
                k = slice(p * C, (p + 1) * C)
                dst = xt[k, rows(u, p), :].rearrange("p r w -> p (r w)")
                nc.vector.scalar_tensor_tensor(dst, B[k, :], brep[k, 0:1], dst, ALU.add, ALU.add).then_inc(res_done, 1)

            def step(s, p):
                unit(s, p, 1, logits, 1)
                unit(s, p, 2, low_p, 0)
                unit(s, p, 2, low_p, 1)
                unit(s, p, 1, low_v, 1)
                unit(s, p, 3, low_og)
                unit(s, p, 1, logits, 2)
                unit(s, p, 0, low_qk, 0)
                unit(s, p, 3, residual)
                unit(s, p, 1, logits, 3)
                unit(s, p, 0, low_qk, 1)
                unit(s, p, 2, normalise, 0)
                unit(s, p, 2, low_p, 2)
                unit(s, p, 2, low_p, 3)
                unit(s, p, 0, logits, 0)
                unit(s, p, 2, normalise, 1)
                unit(s, p, 0, low_v, 0)

            def step_and_statistics(s, p):
                step(s, p)
                if isinstance(s, int) and UNITS <= s <= UNITS + 1:
                    complete = (s - 3 + 1) // 2 * R
                    dve.wait_ge(res_done, s - 2)
                    row_statistics(24 * (s - UNITS), min(24 * (s - UNITS + 1), complete))

            attention_steps(step_and_statistics, dve)
            row_statistics(48, HALF - R)
            dve.wait_ge(res_done, UNITS)
            chain.count = 0
            chain.sem = dve_step2

            chain.link(nc.vector.memset(pay[:, :, W + 2:ROW], 0.0))
            chain.link(row_statistics(HALF - R, HALF))
            row_scales(chain, slice(0, HALF), 1e-5)
            for i in range(HALF):
                last = nc.vector.tensor_scalar(pay[:, i, 0:W], xt[:, i, :], mean[:, i:i + 1], rstd[:, i:i + 1],
                                               ALU.subtract, ALU.mult)
                if i % R == R - 1:
                    last.then_inc(xn_ready, 1)
            dve.wait_ge(bgate_spread, 1)
            chain.link(nc.vector.tensor_copy(bgate_all[:], B[:, E:2 * E]))
            dve.wait_ge(lg_full, GROUPS)
            dve.wait_ge(const_ready, 1)
            rows_e = [P, HALF, E]
            spread = lambda v: v.unsqueeze(2).broadcast_to(rows_e)
            chain.link(nc.vector.tensor_tensor(lg[:], S[0][:].rearrange("p (i e) -> p i e", e=E), bgate_all[:].unsqueeze(1).broadcast_to(rows_e), ALU.add))
            for k in range(2):
                chain.link(nc.vector.tensor_reduce(top[k][:], lg[:], AX_X, ALU.max))
                chain.link(nc.vector.tensor_tensor(r_a[:], lg[:], spread(top[k][:]), ALU.is_equal))
                chain.link(nc.vector.tensor_tensor(r_b[:], r_a[:], order8[:].unsqueeze(1).broadcast_to(rows_e), ALU.mult))
                chain.link(nc.vector.tensor_reduce(key[:], r_b[:], AX_X, ALU.max))
                chain.link(nc.vector.tensor_tensor(oh[k][:], r_b[:], spread(key[:]), ALU.is_equal))
                if k == 0:
                    chain.link(nc.vector.scalar_tensor_tensor(lg[:], oh[0][:], -BIG, lg[:], ALU.mult, ALU.add))
            chain.link(nc.vector.tensor_tensor(picked[:], oh[0][:], oh[1][:], ALU.add))
            nc.vector.tensor_tensor(key[:], top[1][:], top[0][:], ALU.subtract).then_inc(gap_ready, 1)
            chain.link(nc.vector.tensor_copy(r_a[:], picked[:]))
            src, dst = picked, r_b
            step_rows = 1
            while step_rows < HALF:
                nc.vector.tensor_copy(dst[:, 0:step_rows, :], src[:, 0:step_rows, :])
                chain.link(nc.vector.tensor_tensor(dst[:, step_rows:, :], src[:, step_rows:, :], src[:, 0:HALF - step_rows, :], ALU.add))
                src, dst = dst, src
                step_rows *= 2
            assert src is picked
            nc.vector.tensor_tensor(r_b[:], picked[:], r_a[:], ALU.subtract).then_inc(totals_ready, 1)
            dve.wait_ge(totals_ready, 1)
            dve.wait_ge(totals_summed, 2)
            chain.link(nc.vector.tensor_copy(counts[:], B[:, 0:2 * E]))
            tf, tg, th = tiles_f
            chain.link(nc.vector.tensor_scalar(tiles_i[:], counts[:, E:2 * E], float(TILE - 1), None, ALU.add))
            chain.link(nc.vector.tensor_scalar(tiles_j[:], tiles_i[:], TILE.bit_length() - 1, None, ALU.arith_shift_right))
            chain.link(nc.vector.tensor_copy(tf[:], tiles_j[:]))
            a, b = tf, tg
            for d in (1, 2, 4):
                nc.vector.tensor_copy(b[:, 0:d], a[:, 0:d])
                chain.link(nc.vector.tensor_tensor(b[:, d:], a[:, d:], a[:, 0:E - d], ALU.add))
                a, b = b, (th if a is tf else a)
            inclusive = a
            chain.link(nc.vector.tensor_tensor(first_row[:], inclusive[:], tf[:], ALU.subtract))
            chain.link(nc.vector.scalar_tensor_tensor(first_row2[:], first_row[:], float(TILE), counts[:, 0:E], ALU.mult, ALU.add))
            chain.link(nc.vector.memset(tile_expert[:], 0.0))
            for e in range(E - 1):
                chain.link(nc.vector.tensor_scalar(tile_cmp[:], tile_no[:], inclusive[0:1, e:e + 1], None, ALU.is_ge))
                chain.link(nc.vector.tensor_tensor(tile_expert[:], tile_expert[:], tile_cmp[:], ALU.add))
            chain.link(nc.vector.tensor_scalar(w_at[:], tile_expert[:], float(HID), None, ALU.mult))
            nc.vector.tensor_scalar(b1_at[:], tile_expert[:], float(HB), None, ALU.mult).then_inc(table_ready, 1)
            def prepare_weights():
                dve.wait_ge(wsq_summed, 1)
                chain.link(nc.vector.tensor_copy(gstat[:, 0:2], A[:, 0:2]))
                chain.link(nc.vector.tensor_scalar(gstat[:, 3:4], gstat[:, 0:1], float(4 * W), 1e-12, ALU.mult, ALU.add))
                chain.link(nc.vector.tensor_scalar(gstat[:, 4:6], gstat[:, 0:2], 1e-12, None, ALU.max))
                dve.wait_ge(small_in, 16 * (E + 3))
                chain.link(nc.vector.tensor_tensor(b1_sq[:], b1_sb[:].rearrange("p e b -> p (e b)"), b1_sb[:].rearrange("p e b -> p (e b)"), ALU.mult))
                nc.vector.tensor_reduce(b1_sum[:], b1_sq[:], AX_X, ALU.add).then_inc(b1_summing, 1)
                dve.wait_ge(b1_summed, 1)
                chain.link(nc.vector.scalar_tensor_tensor(gstat[:, 6:7], B[:, 0:1], 4.0, gstat[:, 3:4], ALU.mult, ALU.add))
                power_of_two(chain, hscale[:, 0:3], gstat[:, 4:7], ebits[:, 0:3], ebits2[:, 0:3])
                chain.link(nc.vector.reciprocal(inv_hscale[:, 0:3], hscale[:, 0:3]))
                nc.vector.tensor_scalar(y_scale[:], inv_hscale[:, 1:2], inv_hscale[:, 2:3], None, ALU.mult).then_inc(hscale_ready, 1)
                dve.wait_ge(hscale_ready, 1)
                chain.link(nc.vector.tensor_scalar(b2_row[:], b2_row[:], hscale[0:1, 1:2], hscale[0:1, 2:3], ALU.mult, ALU.mult))
                b2_e = b2_row[:].rearrange("o (e d) -> o e d", e=E)
                chain.link(nc.vector.tensor_copy(b2_parts[:, :, 0, :], b2_e))
                chain.link(nc.vector.tensor_tensor(b2_parts[:, :, 1, :], b2_e, b2_parts[:, :, 0, :], ALU.subtract))
                chain.link(nc.vector.tensor_copy(ones_x[:], ones[0:1, :]))
                for n in range(2):
                    dve.wait_ge(w_high, n + 1)
                    nc.vector.scalar_tensor_tensor(w_l[n][:].rearrange("p e b d -> p (e b d)"),
                                                   w_raw[n][:].rearrange("p a r w -> p (a r w)"), hscale[:, n:n + 1],
                                                   w_h[n][:].rearrange("p e b d -> p (e b d)"), ALU.mult, ALU.subtract).then_inc(w_split, 1)

            chain.link(nc.vector.tensor_tensor(r_b[:], r_b[:], first_row2[:].unsqueeze(1).broadcast_to(rows_e), ALU.add))
            for k in range(2):
                chain.link(nc.vector.tensor_tensor(r_a[:], r_b[:], oh[k][:], ALU.mult))
                chain.link(nc.vector.tensor_reduce(posf[:], r_a[:], AX_X, ALU.add))
                chain.link(nc.vector.tensor_copy(pos[k][:], posf[:]))
            dve.wait_ge(gate_exp, 1)
            chain.link(nc.vector.tensor_scalar(key[:], gate_e[:], 1.0, None, ALU.add))
            chain.link(nc.vector.reciprocal(weight[0][:], key[:]))
            chain.link(nc.vector.tensor_tensor(weight[1][:], gate_e[:], weight[0][:], ALU.mult))
            for k in range(2):
                if k:
                    prepare_weights()
                    dve.wait_ge(scattered[0], 16 * HALF)
                chain.link(nc.vector.tensor_copy(pay[:, :, W], weight[k][:]))
                nc.vector.tensor_scalar(pay[:, :, W + 1], token_id[:], float(k * TOKENS), None,
                                        ALU.add).then_inc(meta_ready, 1)

            def tile_step(s, q, _=None):
                tokens, first, second, weighting = tile_stages(s)
                if tokens:
                    t, p = s + 1, 1 - q
                    dve.wait_ge(fx_high, t + 1)
                    nc.vector.tensor_tensor(fx_l[p][:], AB[p][:, 0:TILE], fx_h[p][:], ALU.subtract).then_inc(fx_ready, 1)
                    nc.vector.tensor_copy(meta[:, tile_at(t), :, :], rows_in[p][:, :, W:W + 2].unsqueeze(1)).then_inc(meta_kept, 1)
                if weighting:
                    t, p = s - 2, q
                    wait(dve, y_sent[p], (t // 2) * 32 if isinstance(t, int) else (t - p) * 16)
                    dve.wait_ge(meta_kept, t + 1)
                    nc.vector.tensor_copy(yidx[p][:].unsqueeze(1), meta[:, tile_at(t), :, 1]).then_inc(yidx_ready, 1)
                if first:
                    t, p = s, q
                    for pair in range(2):
                        b = slice(2 * pair, 2 * pair + 2)
                        dve.wait_ge(gelu_done, 2 * t + pair + 1)
                        nc.vector.tensor_scalar(hh[p][:, b, :], hf[p][:, b, :], hscale[:, 2:3], None, ALU.mult).then_inc(hh_ready, 1)
                        dve.wait_ge(hh_ready, 2 * t + pair + 1)
                        nc.vector.scalar_tensor_tensor(hl[p][:, b, :], hf[p][:, b, :], hscale[:, 2:3], hh[p][:, b, :],
                                                       ALU.mult, ALU.subtract).then_inc(hl_ready, 1)

            dve.wait_ge(table_ready, 1)
            tile_steps(dve, tile_step)

            for c in range(CH):
                dve.wait_ge(y_in[c % 2], 64 * (c // 2 + 1))
                for k in range(2):
                    last = nc.vector.scalar_tensor_tensor(xt[:, chunk(c), :], yin[c % 2][:, k], y_scale[:, 0:1], xt[:, chunk(c), :],
                                                          ALU.mult, ALU.add)
                    if k == 0:
                        chain.link(last)
                last.then_inc(y_added, 1)

        @block.tensor
        def _(pe):
            pe.wait_ge(const_ready, 1)
            pe.wait_ge(w_in, 12 * 16)
            for n in range(4):
                last = nc.tensor.transpose(PT[0][:, n * P:(n + 1) * P], wraw[:, n].rearrange("o f c -> o (f c)"), identity[:])
            last.then_inc(w_transposed, 1)
            pe.wait_ge(wrep_reordered, 1)
            nc.tensor.transpose(PT[1][:, 0:C], wrep_ordered[:], identity[0:C, 0:C]).then_inc(wrep_transposed, 1)
            pe.wait_ge(rowvar_ready, 1)
            nc.tensor.matmul(B[:, 0:1], ones[:], gstat[:, 0:1], start=True, stop=True).then_inc(rowvar_summed, 1)
            pe.wait_ge(wb_in, 32)
            for n in range(HALF // R):
                if n % (CR // R) == 0:
                    pe.wait_ge(x1_ready, n // (CR // R) + 1)
                wait(pe, bias_copied, n - 3)
                nc.tensor.matmul(S[n % 4][0:2 * NH, :], wb_sb[:], x1[:, n * R:(n + 1) * R, :].rearrange("p r w -> p (r w)"),
                                 start=True, stop=True).then_inc(bias_done, 1)
            pe.wait_ge(sums_ready, 1)
            nc.tensor.matmul(B[:, 0:4], ones[:], sums[:, 0:4], start=True, stop=True).then_inc(squares_summed, 1)
            pe.wait_ge(weights_ready, 1)

            def project_qk(u, p, n):
                if n == 0:
                    wait(pe, vg_low, 2 * u)
                    pe.wait_ge(xs_ready, u + 1)
                else:
                    pe.wait_ge(qk_low, 2 * u + 1)
                nc.tensor.matmul(A[:], w4h[:, n, :], xs[p][:], start=True, stop=False)
                nc.tensor.matmul(A[:], w4l[:, p, n, :], xs[p][:], start=False, stop=True).then_inc(qk_full, 1)

            def project_vg(u, p, half):
                if half == 0:
                    pe.wait_ge(qk_low, 2 * u + 2)
                else:
                    pe.wait_ge(vg_low, 2 * u + 1)
                av = A[:].rearrange("p (r s c) -> p r s c", r=2, s=2)
                flags = dict(skip_group_check=True)
                for r in range(2):
                    i = 2 * half + r
                    xi = xs[p][:, i * P:(i + 1) * P]
                    nc.tensor.matmul(A[:, r * 256:(r + 1) * 256], xi, w4h[:, 2:4, :], start=r == 0, stop=False, **flags)
                    nc.tensor.matmul(A[:, r * 256:(r + 1) * 256], xi, w4l[:, p, 2:4, :], start=False, stop=False, **flags)
                for part in (bg_h, bg_l):
                    last = nc.tensor.matmul(av[:, :, 1, :], ones_r[:], part[:].unsqueeze(1).broadcast_to([P, 2, P]),
                                            start=False, stop=part is bg_l, **flags)
                last.then_inc(vg_full, 1)

            def scores(u, p, pair):
                if pair == 0:
                    pe.wait_ge(qk_low, 2 * u + 2)
                wait(pe, logits_ready, 4 * (u - 1) + 2 * pair + 2)
                (q_h, q_l), (k_h, k_l) = ([part[p] for part in qk[n]] for n in range(2))
                for i in range(R):
                    c = slice(i * P, (i + 1) * P)
                    for m, (a, b) in enumerate(((q_h, k_h), (q_h, k_l), (q_l, k_h))):
                        for h in (2 * pair, 2 * pair + 1):
                            d = slice(h * D, (h + 1) * D)
                            last = nc.tensor.matmul(S[h][:, c], a[d, c], b[d, c], start=m == 0, stop=m == 2)
                last.then_inc(s_full, 1)

            def transpose_p(u, p, i):
                if i == 0:
                    pe.wait_ge(exp_done, 4 * u + 4)
                wait(pe, pl_ready, 4 * u + i - 1)
                for h in range(NH):
                    last = nc.tensor.transpose(PT[i % 2][:, h * P:(h + 1) * P], L[p][:, h, i, :], identity[:])
                last.then_inc(pt_full, 1)

            def values(u, p, i):
                pe.wait_ge(pl_ready, 4 * u + i + 1)
                if i % 2 == 0:
                    pe.wait_ge(vg_low, 2 * u + i // 2 + 1)
                if i == 0:
                    wait(pe, res_done, u)
                if i == 2:
                    pe.wait_ge(norm_done, 2 * u + 1)
                for h in range(NH):
                    k = slice(h * P, (h + 1) * P)
                    o = ((i % 2) * NH + h) * (D + 1)
                    dst = B[:, o:o + D + 1]
                    nc.tensor.matmul(dst, ph[i % 2][:, k], vh[p][:, i, h, :], start=True, stop=False)
                    nc.tensor.matmul(dst, ph[i % 2][:, k], vl[p][:, i, h, :], start=False, stop=False)
                    last = nc.tensor.matmul(dst, pl[i % 2][:, k], vh[p][:, i, h, :], start=False, stop=True)
                last.then_inc(pv_done, 1)

            def transpose_og(u, p):
                pe.wait_ge(og_ready, 2 * u + 2)
                for i in range(R):
                    last = nc.tensor.transpose(B[:, i * P:(i + 1) * P], og[p][:, i, :], identity[:])
                last.then_inc(ogt_full, 1)

            def project_out(u, p):
                pe.wait_ge(ogt_low, u + 1)
                nc.tensor.matmul(B[:], wrep_h[:], ogT_h[:], start=True, stop=False)
                nc.tensor.matmul(B[:], wrep_h[:], ogT_l[:], start=False, stop=False)
                nc.tensor.matmul(B[:], wrep_l[:], ogT_h[:], start=False, stop=True).then_inc(oproj_done, 1)

            def step(s, p):
                unit(s, p, 0, project_qk, 0)
                unit(s, p, 2, transpose_p, 2)
                unit(s, p, 3, project_out)
                unit(s, p, 0, project_qk, 1)
                unit(s, p, 2, transpose_p, 3)
                unit(s, p, 2, values, 0)
                unit(s, p, 2, values, 1)
                unit(s, p, 0, scores, 0)
                unit(s, p, 2, values, 2)
                unit(s, p, 0, project_vg, 0)
                unit(s, p, 2, values, 3)
                unit(s, p, 1, transpose_p, 0)
                unit(s, p, 1, transpose_p, 1)
                unit(s, p, 0, project_vg, 1)
                unit(s, p, 2, transpose_og)
                unit(s, p, 0, scores, 1)

            attention_steps(step, pe)

            pe.wait_ge(res_done, UNITS)
            pe.wait_ge(small_in, 16 * (E + 3))
            nc.tensor.matmul(B[:, E:2 * E], ones[0:1, :], bgate_row[:], start=True, stop=True).then_inc(bgate_spread, 1)
            def transpose_rows(g, p):
                pe.wait_ge(staged, g + 1)
                wait(pe, xnT_ready, g - 1)
                for i in range(R):
                    last = nc.tensor.transpose(PT[p][:, i * P:(i + 1) * P], stage[p][:, i, :], identity[:])
                last.then_inc(stage_T, 1)

            def gate_logits(g, p):
                pe.wait_ge(xnT_ready, g + 1)
                for i in range(R):
                    last = nc.tensor.matmul(S[0][:, bass.ds(g * (R * E) + i * E, E)], xnT[p][:, i * P:(i + 1) * P], wg_sb[:],
                                            start=True, stop=True)
                last.then_inc(lg_full, 1)

            def step(s, p):
                if not isinstance(s, int) or s < GROUPS:
                    transpose_rows(s, p)
                if not isinstance(s, int) or s >= 1:
                    gate_logits(s - 1, 1 - p)

            group_steps(pe, step)
            pe.wait_ge(totals_ready, 1)
            nc.tensor.matmul(B[:, 0:E], before[:], picked[:, HALF - 1, :], start=True, stop=True).then_inc(totals_summed, 1)
            nc.tensor.matmul(B[:, E:2 * E], ones[:], picked[:, HALF - 1, :], start=True, stop=True).then_inc(totals_summed, 1)

            pe.wait_ge(wsq_ready, 1)
            nc.tensor.matmul(A[:, 0:2], ones[:], wsq[:], start=True, stop=True).then_inc(wsq_summed, 1)
            pe.wait_ge(b1_summing, 1)
            nc.tensor.matmul(B[:, 0:1], ones[:], b1_sum[:], start=True, stop=True).then_inc(b1_summed, 1)

            b2_flat = b2_parts[:].rearrange("o e b d -> o (e b d)")
            w1_h, w1_l, w2_h, w2_l = (w[:].rearrange("p e b d -> p (e b d)") for w in (w_h[0], w_l[0], w_h[1], w_l[1]))

            def tile_step(s, q, e_second=None):
                tokens, first, second, weighting = tile_stages(s)
                e_first = None
                if tokens:
                    t, p = s + 1, 1 - q
                    pe.wait_ge(rows_loaded[p], 16 * (t // 2 + 1) if isinstance(t, int) else (t - p) * 8 + 16)
                    for k in range(2):
                        last = nc.tensor.transpose(AB[p][:, k * P:(k + 1) * P], rows_in[p][:, k, 0:W], identity[:])
                    last.then_inc(fxT_full, 1)
                if first:
                    t, p = s, q
                    e_first = expert_of(pe, w_at, s, HID)
                    pe.wait_ge(fx_ready, t + 1)
                    for pair in range(2):
                        for k in range(2):
                            dst = S[2 * p + pair][:, k * TILE:(k + 1) * TILE]
                            block_at = bass.ds(e_first + (2 * pair + k) * P, P)
                            nc.tensor.matmul(dst, w1_h[:, block_at], fx_h[p][:], start=True, stop=False)
                            nc.tensor.matmul(dst, w1_h[:, block_at], fx_l[p][:], start=False, stop=False)
                            last = nc.tensor.matmul(dst, w1_l[:, block_at], fx_h[p][:], start=False, stop=True)
                        last.then_inc(h_full, 1)
                if second:
                    t, p = s - 1, 1 - q
                    if e_second is None:
                        e_second = expert_of(pe, w_at, s - 1, HID)
                    wait(pe, y_ready, t - 1)
                    for k in range(2):
                        nc.tensor.matmul(PT[p][:, 0:2 * P].rearrange("p (k d) -> p k d", k=2), ones_x[:],
                                         b2_flat[0:1, bass.ds(e_second + k * P, P)].unsqueeze(1).broadcast_to([1, 2, P]),
                                         start=k == 0, stop=False, skip_group_check=True)
                    pe.wait_ge(hl_ready, 2 * t + 2)
                    for b in range(HB):
                        block_at = bass.ds(e_second + b * P, P)
                        for h_part, w_part in ((hh, w2_h), (hl, w2_h), (hh, w2_l)):
                            for k in range(2):
                                last = nc.tensor.matmul(PT[p][:, k * P:(k + 1) * P], h_part[p][:, b, k * P:(k + 1) * P],
                                                        w_part[:, block_at], start=False,
                                                        stop=b == HB - 1 and w_part is w2_l, skip_group_check=True)
                    last.then_inc(y_full, 1)
                return e_first

            pe.wait_ge(table_ready, 1)
            pe.wait_ge(w_split, 2)
            tile_steps(pe, tile_step)


INPUTS = ["x", "L0_conv_ln_w", "L0_conv_ln_b", "L0_conv_wq", "L0_conv_wk", "L0_conv_wv", "L0_conv_wb", "L0_conv_wg_w",
          "L0_conv_wg_b", "L0_conv_wrep_w", "L0_conv_wrep_b", "L0_ffn_Wg", "L0_ffn_bg", "L0_ffn_W1", "L0_ffn_b1",
          "L0_ffn_W2", "L0_ffn_b2"]


def kernel(**inputs):
    import numpy as np
    import concourse.bacc as bacc
    from concourse.bass_utils import run_bass_kernel_spmd

    nc = bacc.Bacc("TRN2", target_bir_lowering=False, num_devices=1)
    arrays, args = {}, []
    for name in INPUTS:
        a = np.ascontiguousarray(inputs[name])
        arrays[f"in_{name}"] = a
        args.append(nc.dram_tensor(f"in_{name}", a.shape, mybir.dt.from_np(a.dtype), kind="ExternalInput").ap())
    out = nc.dram_tensor("out", list(inputs["x"].shape), F32, kind="ExternalOutput").ap()
    build(nc, *args, out)
    r = run_bass_kernel_spmd(nc, [arrays], core_ids=[0])
    return r.results[0]["out"]
```

```python
from contextlib import ExitStack

import concourse.bass as bass
from concourse import mybir

P = 128
F32 = mybir.dt.float32
F32R = mybir.dt.float32r
F16 = mybir.dt.float16
I32 = mybir.dt.int32
ALU = mybir.AluOpType
ACT = mybir.ActivationFunctionType
AX_X = mybir.AxisListType.X

RSQRT_SEED = float(0x5F3759DF)
BIG = 3.0e38


class Chain:

    def __init__(self, engine, sem):
        self.engine, self.sem, self.count = engine, sem, 0

    def link(self, instruction):
        self.count += 1
        instruction.then_inc(self.sem, 1)
        self.engine.wait_ge(self.sem, self.count)


def wait(engine, sem, value):
    if isinstance(value, int) and value <= 0:
        return
    engine.wait_ge(sem, value)


def rsqrt(nc, chain, y, v, a, b):
    seed_bits = a.bitcast(I32)
    chain.link(nc.vector.tensor_scalar(seed_bits, v.bitcast(I32), 1, None, ALU.arith_shift_right))
    chain.link(nc.vector.tensor_scalar(y.bitcast(I32), seed_bits, -1.0, RSQRT_SEED, ALU.mult, ALU.add))
    for _ in range(3):
        chain.link(nc.vector.tensor_tensor(a, y, y, ALU.mult))
        chain.link(nc.vector.scalar_tensor_tensor(b, a, -0.5, v, ALU.mult, ALU.mult))
        chain.link(nc.vector.scalar_tensor_tensor(y, b, 1.5, y, ALU.add, ALU.mult))


def build(nc, x, ln_w, ln_b, wq, wk, wv, wb, wg_w, wg_b, wrep_w, wrep_b, Wg, bg, W1, b1, W2, b2, out):
    _, C, H, W = x.shape
    NH = wb.shape[0]
    HC = wq.shape[0]
    D = HC // NH
    HALF = H // 2
    R = 4
    UNITS = H // R
    NQ = R * W
    ROWSTATS = 6
    CH = 4
    CR = HALF // CH
    E, _, HID = W1.shape
    HB = HID // P
    TOKENS = C * H
    TILE = 256
    SLOT_TILES = TOKENS // TILE + E - 1
    TILES = 2 * SLOT_TILES
    ROW = W + 4
    NOWHERE = 1 << 20
    WPIECE = E * HID // UNITS
    assert W == P and H == P and 2 * C == P and HC == P and UNITS % 2 == 0

    with ExitStack() as ctx:
        def sb(name, shape, dt=F32):
            return ctx.enter_context(nc.sbuf_tensor(name, shape, dt))

        def psum(name, shape=(P, 512), dt=F32):
            return ctx.enter_context(nc.psum_tensor(name, list(shape), dt))

        def sem(name):
            return ctx.enter_context(nc.semaphore(name))

        xt = sb("xt", [P, HALF, W])
        shared = sb("shared", [P, HALF, W])
        lnw_sb, lnb_sb = (shared[:, n * 2 * CR:(n + 1) * 2 * CR, :].rearrange("p (a r) w -> p a r w", a=2) for n in range(2))
        lnb_at = [lnb_sb[:, 0], lnb_sb[:, 1], lnw_sb[:, 0], lnw_sb[:, 1]]
        identity = sb("identity", [P, P])
        ones = sb("ones", [P, P])
        ones_r = sb("ones_r", [P, P], F32R)
        rowstat = sb("rowstat", [P, HALF, ROWSTATS])
        mean = sb("mean", [P, HALF])
        var = sb("var", [P, HALF])
        rstd = sb("rstd", [P, HALF])
        tmp_a = sb("tmp_a", [P, HALF])
        tmp_b = sb("tmp_b", [P, HALF])
        sums = sb("sums", [P, 8])
        gstat = sb("gstat", [P, 8])
        xsq = sb("xsq", [P, 2 * CH])
        rstd2 = sb("rstd2", [P, HALF])
        gtmp = sb("gtmp", [P, 8])
        gtmp2 = sb("gtmp2", [P, 8])
        grstd = sb("grstd", [P, 1])
        ebits = sb("ebits", [P, 4], I32)
        ebits2 = sb("ebits2", [P, 4], I32)
        scales = sb("scales", [P, 4])
        inv_scales = sb("inv_scales", [P, 4])
        logit_scale = sb("logit_scale", [P, 1])
        bias_scale = sb("bias_scale", [P, 1])
        brep = sb("brep", [P, 1])
        bgrow = sb("bgrow", [1, HC])
        wb_sb = sb("wb_sb", [P, 2 * NH])
        w_raw = [lnw_sb, lnb_sb]
        b1_sb = sb("b1_sb", [P, E, HB])
        b2_row = sb("b2_row", [1, E * P])
        wg_sb = sb("wg_sb", [P, E])
        bgate_row = sb("bgate_row", [1, E])
        wsq = sb("wsq", [P, 2])
        hscale = sb("hscale", [P, 4])
        inv_hscale = sb("inv_hscale", [P, 4])
        y_scale = sb("y_scale", [P, 1])
        order8 = sb("order8", [P, E])
        before = sb("before", [P, P])
        counts = sb("counts", [P, 2 * E])
        tiles_i = sb("tiles_i", [P, E], I32)
        tiles_f = [sb(f"tiles_f{k}", [P, E]) for k in range(3)]
        token_id = sb("token_id", [P, HALF])
        tile_no = sb("tile_no", [1, SLOT_TILES])
        tile_expert = sb("tile_expert", [1, SLOT_TILES])
        tile_cmp = sb("tile_cmp", [1, SLOT_TILES])
        w_at = sb("w_at", [1, TILES], I32)
        b1_at = sb("b1_at", [1, TILES], I32)
        blank = sb("blank", [P, ROW])
        b1_flat = b1_sb[:].rearrange("p e b -> p (e b)")
        b1_sq = sb("b1_sq", [P, E * HB])
        b1_sum = sb("b1_sum", [P, 1])
        bgate_all = sb("bgate_all", [P, E])
        tiles_j = sb("tiles_j", [P, E], I32)
        first_row = sb("first_row", [P, E])
        first_row2 = sb("first_row2", [P, E])

        attention_memory = ExitStack()

        def sba(name, shape, dt=F32):
            return attention_memory.enter_context(nc.sbuf_tensor(name, shape, dt))

        x1 = sba("x1", [P, HALF, W])
        wraw = sba("wraw", [P, 4, 2, C])
        w4h = sba("w4h", [P, 4, P], F32R)
        w4l = sba("w4l", [P, 2, 4, P], F32R)
        wrep_raw = sba("wrep_raw", [C, HC])
        wrep_ordered = sba("wrep_ordered", [C, HC])
        wrepT = sba("wrepT", [P, P])
        wrep_h = sba("wrep_h", [P, P], F32R)
        wrep_l = sba("wrep_l", [P, P], F32R)
        bg_f = sba("bg_f", [P, HC])
        bg_h = sba("bg_h", [P, HC], F32R)
        bg_l = sba("bg_l", [P, HC], F32R)
        bias_rows = sba("bias_rows", [2 * NH, HALF * W])
        biasN = sba("biasN", [P, NH, P])
        xf = sba("xf", [P, NQ])
        xs = [sba(f"xs{p}", [P, NQ], F32R) for p in range(2)]
        qk = [[[sba(f"{n}{part}{p}", [P, NQ], F16) for p in range(2)] for part in "hl"] for n in "qk"]
        L = [sba(f"L{p}", [P, NH, R, P]) for p in range(2)]
        dve_square_junk = L[1][:].rearrange("p h i k -> p (h i k)")[:, 0:CR * W // 2]
        square_junk = L[0][:].rearrange("p h i k -> p (h i k)")[:, 0:CR * W // 2]
        lmin = [sba(f"lmin{p}", [P, NH * R]) for p in range(2)]
        ph = [sba(f"ph{p}", [P, NH * P], F16) for p in range(2)]
        pl = [sba(f"pl{p}", [P, NH * P], F16) for p in range(2)]
        vh = [sba(f"vh{p}", [P, R, NH, D + 1], F16) for p in range(2)]
        vl = [sba(f"vl{p}", [P, R, NH, D + 1], F16) for p in range(2)]
        gt = [sba(f"gt{p}", [P, R, HC]) for p in range(2)]
        turn = [sba(f"turn{k}", [P, 1]) for k in range(2)]
        rden = [sba(f"rden{k}", [P, 2, NH]) for k in range(2)]
        on = [sba(f"on{k}", [P, 2, HC]) for k in range(2)]
        og = [sba(f"og{p}", [P, R, HC]) for p in range(2)]
        w4 = og[0]
        ogT_h = sba("ogT_h", [P, NQ], F32R)
        ogT_l = sba("ogT_l", [P, NQ], F32R)
        attention_memory.close()

        def sbm(name, shape, dt=F32):
            return ctx.enter_context(nc.sbuf_tensor(name, shape, dt))

        pay = sbm("pay", [P, HALF, ROW])
        w_h = [sbm(f"w{n}_h", [P, E, HB, P], F16) for n in (1, 2)]
        w_l = [sbm(f"w{n}_l", [P, E, HB, P], F16) for n in (1, 2)]
        b2_parts = sbm("b2_parts", [1, E, HB, P], F32R)
        ones_x = sbm("ones_x", [1, P], F32R)
        stage = [sbm(f"stage{p}", [P, R, P]) for p in range(2)]
        xnT = [sbm(f"xnT{p}", [P, R * P]) for p in range(2)]
        hf = [sbm(f"hf{p}", [P, HB, TILE]) for p in range(2)]
        lgT = [hf[p][0:E].rearrange("p b t -> p (b t)")[:, 0:R * P] for p in range(2)]
        lg = sbm("lg", [P, HALF, E])
        r_a = sbm("r_a", [P, HALF, E])
        r_b = sbm("r_b", [P, HALF, E])
        oh = [sbm(f"oh{k}", [P, HALF, E]) for k in range(2)]
        picked = sbm("picked", [P, HALF, E])
        top = [sbm(f"top{k}", [P, HALF]) for k in range(2)]
        key = sbm("key", [P, HALF])
        gate_e = sbm("gate_e", [P, HALF])
        weight = [sbm(f"weight{k}", [P, HALF]) for k in range(2)]
        posf = sbm("posf", [P, HALF])
        pos = [sbm(f"pos{k}", [P, HALF], I32) for k in range(2)]
        rows_in = [sbm(f"rows_in{p}", [P, 2, ROW]) for p in range(2)]
        fx_h = [sbm(f"fx_h{p}", [P, TILE], F16) for p in range(2)]
        fx_l = [sbm(f"fx_l{p}", [P, TILE], F16) for p in range(2)]
        hh = [sbm(f"hh{p}", [P, HB, TILE], F16) for p in range(2)]
        hl = [sbm(f"hl{p}", [P, HB, TILE], F16) for p in range(2)]
        meta = sbm("meta", [P, TILES, 2, 2])
        yidx = [sbm(f"yidx{p}", [P, 2], I32) for p in range(2)]
        yo = [sbm(f"yo{p}", [P, 2, P]) for p in range(2)]

        routed = [nc.dram_tensor(f"routed{k}", [SLOT_TILES * TILE, ROW], F32, kind="Internal").ap() for k in range(2)]
        expert_out = [nc.dram_tensor(f"expert_out{k}", [TOKENS + TILES, W], F32, kind="Internal").ap() for k in range(2)]

        S = [psum(f"S{h}") for h in range(NH)]
        PT = [psum(f"PT{i}") for i in range(2)]
        A = psum("A")
        B = psum("B")
        AB = [A, B]

        x_in = [sem(f"x_in{c}") for c in range(CH)]
        lnw_in = [sem(f"lnw_in{c}") for c in range(2)]
        lnb_in = [sem(f"lnb_in{c}") for c in range(2)]
        w_in = sem("w_in")
        const_ready = sem("const_ready")
        pool_step = sem("pool_step")
        dve_step = sem("dve_step")
        act_step = sem("act_step")
        lnw_used = sem("lnw_used")
        x1_ready = sem("x1_ready")
        rowvar_ready = sem("rowvar_ready")
        rowvar_summed = sem("rowvar_summed")
        squares_ready = sem("squares_ready")
        squares_summed = sem("squares_summed")
        w_transposed = sem("w_transposed")
        bias_done = sem("bias_done")
        bias_copied = sem("bias_copied")
        bias_in = sem("bias_in")
        wrep_transposed = sem("wrep_transposed")
        wb_in = sem("wb_in")
        sums_ready = sem("sums_ready")
        wrep_reordered = sem("wrep_reordered")
        weights_ready = sem("weights_ready")
        xf_ready = sem("xf_ready")
        xs_high = sem("xs_high")
        xs_ready = sem("xs_ready")
        s_full = sem("s_full")
        qk_full = sem("qk_full")
        qk_high = sem("qk_high")
        qk_low = sem("qk_low")
        vg_full = sem("vg_full")
        vg_high = sem("vg_high")
        vg_low = sem("vg_low")
        norm_done = sem("norm_done")
        og_part = sem("og_part")
        ogt_low = sem("ogt_low")
        res_done = sem("res_done")
        logits_ready = sem("logits_ready")
        exp_done = sem("exp_done")
        pt_full = sem("pt_full")
        ph_ready = sem("ph_ready")
        pl_ready = sem("pl_ready")
        pv_done = sem("pv_done")
        rden_ready = sem("rden_ready")
        og_ready = sem("og_ready")
        ogt_full = sem("ogt_full")
        ogt_high = sem("ogt_high")
        oproj_done = sem("oproj_done")
        ffn_in = sem("ffn_in")
        small_in = sem("small_in")
        wsq_ready = sem("wsq_ready")
        b1_summing = sem("b1_summing")
        b1_summed = sem("b1_summed")
        dve_step2 = sem("dve_step2")
        wsq_summed = sem("wsq_summed")
        hscale_ready = sem("hscale_ready")
        w_high = sem("w_high")
        w_split = sem("w_split")
        bgate_spread = sem("bgate_spread")
        blanked = sem("blanked")
        xn_ready = sem("xn_ready")
        staged = sem("staged")
        stage_T = sem("stage_T")
        xnT_ready = sem("xnT_ready")
        lg_full = sem("lg_full")
        lgT_ready = sem("lgT_ready")
        lg_T = sem("lg_T")
        gap_ready = sem("gap_ready")
        gate_exp = sem("gate_exp")
        totals_ready = sem("totals_ready")
        totals_summed = sem("totals_summed")
        meta_ready = sem("meta_ready")
        scattered = [sem(f"scattered{k}") for k in range(2)]
        table_ready = sem("table_ready")
        rows_loaded = [sem(f"rows_loaded{p}") for p in range(2)]
        fxT_full = sem("fxT_full")
        fx_high = sem("fx_high")
        fx_ready = sem("fx_ready")
        h_full = sem("h_full")
        gelu_done = sem("gelu_done")
        meta_kept = sem("meta_kept")
        hh_ready = sem("hh_ready")
        hl_ready = sem("hl_ready")
        y_full = sem("y_full")
        y_ready = sem("y_ready")
        yidx_ready = sem("yidx_ready")
        y_sent = [sem(f"y_sent{p}") for p in range(2)]
        y0_in = sem("y0_in")
        y0_added = sem("y0_added")
        y_in = [sem(f"y_in{c}") for c in range(CH)]
        y_added = sem("y_added")
        stored = sem("stored")

        xv = x[0].rearrange("c (f i) j -> f c i j", f=2)
        lwv = ln_w.rearrange("c (f i) j -> f c i j", f=2)
        lbv = ln_b.rearrange("c (f i) j -> f c i j", f=2)
        outv = out[0].rearrange("c (f i) j -> f c i j", f=2)

        LEAD = 8

        def chunk(c):
            return slice(c * CR, (c + 1) * CR)

        block = ctx.enter_context(nc.Block())

        FIRST = 6
        LAST = UNITS + 3

        def attention_steps(step, engine):
            for s in range(FIRST):
                step(s, s % 2)
            with engine.Fori(FIRST // 2, UNITS // 2) as g:
                step(2 * g, 0)
                step(2 * g + 1, 1)
            for s in range(UNITS, LAST):
                step(s, s % 2)

        def unit(s, p, delay, operation, *args):
            u = s - delay
            if not isinstance(u, int) or 0 <= u < UNITS:
                operation(u, (p + delay) % 2, *args)

        def rows(u, p):
            if isinstance(u, int):
                return slice((u // 2) * R, (u // 2) * R + R)
            g0 = (u - p) * (R // 2)
            return bass.ds(g0, R)

        BODY = 8
        LOOPS = (5, 45, 77)

        def tile_steps(engine, step, extra=None):
            assert LOOPS[2] == TILES - 1 and all((b - a) % BODY == 0 for a, b in zip(LOOPS, LOOPS[1:]))
            e = None
            for s in range(-1, LOOPS[0]):
                e = step(s, s % 2, e)
            for n in range(2):
                with engine.Fori(0, (LOOPS[n + 1] - LOOPS[n]) // BODY) as g:
                    e = None
                    for k in range(BODY):
                        e = step(BODY * g + LOOPS[n] + k, (LOOPS[n] + k) % 2, e)
                        if n == 1 and extra and k % 2:
                            extra(g, k // 2)
            e = None
            for s in range(LOOPS[2], TILES + 2):
                e = step(s, s % 2, e)

        def tile_stages(s):
            if not isinstance(s, int):
                return True, True, True, True
            return s + 1 < TILES, 0 <= s < TILES, 1 <= s <= TILES, s >= 2

        def tile_at(t):
            return slice(t, t + 1) if isinstance(t, int) else bass.ds(t, 1)

        def expert_of(engine, table, t, step):
            return engine.value_load(table[0:1, tile_at(t)], min_val=0, max_val=(E - 1) * step)

        GROUPS = HALF // R

        def group_steps(engine, step):
            for s in range(4):
                step(s, s % 2)
            with engine.Fori(2, GROUPS // 2) as g:
                step(2 * g, 0)
                step(2 * g + 1, 1)
            for s in range(GROUPS, GROUPS + 2):
                step(s, s % 2)

        def group(s, p, delay, operation):
            g = s - delay
            if not isinstance(g, int) or 0 <= g < GROUPS:
                operation(g, (p + delay) % 2)

        def row_statistics(first, stop):
            for i in range(first, stop):
                last = nc.vector.bn_stats(rowstat[:, i, :], xt[:, i, :])
            return last

        def row_scales(chain, k, eps):
            me, ve = rowstat[:, k, 1], rowstat[:, k, 2]
            mo, vo = rowstat[:, k, 4], rowstat[:, k, 5]
            chain.link(nc.vector.tensor_tensor(mean[:, k], me, mo, ALU.add))
            chain.link(nc.vector.tensor_scalar(mean[:, k], mean[:, k], 0.5, None, ALU.mult))
            chain.link(nc.vector.tensor_tensor(tmp_a[:, k], me, mo, ALU.subtract))
            chain.link(nc.vector.scalar_tensor_tensor(tmp_a[:, k], tmp_a[:, k], 0.25, tmp_a[:, k], ALU.mult, ALU.mult))
            chain.link(nc.vector.tensor_tensor(tmp_b[:, k], ve, vo, ALU.add))
            chain.link(nc.vector.scalar_tensor_tensor(var[:, k], tmp_b[:, k], 1.0 / W, tmp_a[:, k], ALU.mult, ALU.add))
            chain.link(nc.vector.tensor_scalar(rstd2[:, k], var[:, k], eps, None, ALU.add))
            rsqrt(nc, chain, rstd[:, k], rstd2[:, k], tmp_a[:, k], tmp_b[:, k])

        def power_of_two(chain, scale, square, bits, bits2):
            chain.link(nc.vector.tensor_scalar(bits, square.bitcast(I32), 23, None, ALU.arith_shift_right))
            chain.link(nc.vector.tensor_scalar(bits2, bits, -125.0, None, ALU.add))
            chain.link(nc.vector.tensor_scalar(bits, bits2, 1, None, ALU.arith_shift_right))
            chain.link(nc.vector.tensor_scalar(bits2, bits, -1.0, 141.0, ALU.mult, ALU.add))
            chain.link(nc.vector.tensor_scalar(scale.bitcast(I32), bits2, 23, None, ALU.arith_shift_left))

        @block.sync
        def _(sp):
            for c in range(CH):
                for f in range(2):
                    sp.dma_start(xt[f * C:(f + 1) * C, chunk(c), :], xv[f, :, chunk(c), :]).then_inc(x_in[c], 16)
                if c == 0:
                    for n, w in enumerate((wq, wk, wv, wg_w)):
                        for f in range(2):
                            sp.dma_start(wraw[:, n, f, :], w).then_inc(w_in, 16)
            for f in range(2):
                sp.dma_start(brep[f * C:(f + 1) * C, :], wrep_b.rearrange("(c o) -> c o", o=1)).then_inc(w_in, 16)
            sp.dma_start(wrep_raw[:], wrep_w).then_inc(w_in, 16)
            sp.dma_start(bgrow[:], wg_b.rearrange("(o c) -> o c", o=1)).then_inc(w_in, 16)
            for n in range(2):
                sp.wait_ge(bias_copied, (n + 1) * HALF // R // 2)
                some = slice(n * HALF // 2, (n + 1) * HALF // 2)
                for f in range(2):
                    for h in range(NH):
                        sp.dma_start(biasN[f * C + some.start:f * C + some.stop, h, :],
                                     bias_rows[f * NH + h:f * NH + h + 1, :].rearrange(
                                         "o (i k) -> o i k", i=HALF)[:, some, :]).then_inc(bias_in, 16)
            sp.wait_ge(x1_ready, CH)
            sp.dma_start(w_raw[0][:].rearrange("p a r w -> p (a r w)").rearrange("p (e h) -> p e h", e=E),
                         W1.rearrange("e d h -> d e h")).then_inc(ffn_in, 16)
            sp.dma_start(w_raw[1][:].rearrange("p a r w -> p (a r w)").rearrange("p (e b d) -> p e b d", e=E, b=HB),
                         W2.rearrange("e (b p) d -> p e b d", p=P)).then_inc(ffn_in, 16)
            for e in range(E):
                sp.dma_start(b1_sb[:, e, :], b1[e].rearrange("(b p) -> p b", p=P),
                             allow_slow_non_contiguous=True).then_inc(small_in, 16)
            sp.dma_start(b2_row[:], b2.rearrange("(o e) d -> o (e d)", o=1)).then_inc(small_in, 16)
            sp.dma_start(wg_sb[:], Wg).then_inc(small_in, 16)
            sp.dma_start(bgate_row[:], bg.rearrange("(o e) -> o e", o=1)).then_inc(small_in, 16)

            sp.wait_ge(const_ready, 1)
            for k in range(2):
                sp.dma_start(routed[k].rearrange("(n p) w -> p n w", p=P),
                             blank[:].unsqueeze(1).broadcast_to([P, SLOT_TILES * TILE // P, ROW])).then_inc(blanked, 16)

            routed_v = [r.rearrange("(t k p) w -> t p k w", k=2, p=P) for r in routed]
            outputs_v = [e[0:TOKENS].rearrange("(c f i) w -> f c i w", f=2, i=HALF) for e in expert_out]

            def load_rows(t, p, slot):
                wait(sp, meta_kept, t - 1)
                sp.dma_start(rows_in[p][:], routed_v[slot][t - slot * SLOT_TILES]).then_inc(rows_loaded[p], 16)

            def load_pairs(first, stop, slot):
                with sp.Fori(first // 2, stop // 2) as g:
                    load_rows(2 * g, 0, slot)
                    load_rows(2 * g + 1, 1, slot)

            assert SLOT_TILES % 2 == 1
            LATER = SLOT_TILES + 7
            sp.wait_ge(scattered[0], 16 * HALF)
            load_rows(0, 0, 0)
            load_rows(1, 1, 0)
            load_pairs(2, SLOT_TILES - 1, 0)
            load_rows(SLOT_TILES - 1, 0, 0)
            sp.wait_ge(scattered[1], 16 * HALF)
            load_rows(SLOT_TILES, 1, 1)
            load_pairs(SLOT_TILES + 1, LATER, 1)
            for p in range(2):
                sp.wait_ge(y_sent[p], 32 * ((SLOT_TILES + 1 - p) // 2))
            for n in range(2 * CH):
                c, f = divmod(n, 2)
                sp.dma_start(shared[f * C:(f + 1) * C, chunk(c), :], outputs_v[0][f, :, chunk(c), :]).then_inc(y0_in, 16)
                load_rows(LATER + n, n % 2, 1)
            load_pairs(LATER + 2 * CH, TILES, 1)

            for p in range(2):
                sp.wait_ge(y_sent[p], 32 * (TILES // 2))
            sp.wait_ge(y0_added, HALF // R)
            for c in range(CH):
                for f in range(2):
                    sp.dma_start(shared[f * C:(f + 1) * C, chunk(c), :], outputs_v[1][f, :, chunk(c), :]).then_inc(y_in[c], 16)
            for c in range(CH):
                sp.wait_ge(y_added, c + 1)
                for f in range(2):
                    sp.dma_start(outv[f, :, chunk(c), :], xt[f * C:(f + 1) * C, chunk(c), :]).then_inc(stored, 16)
            sp.wait_ge(stored, 32 * CH)

        @block.gpsimd
        def _(pool):
            chain = Chain(pool, pool_step)
            chain.link(nc.gpsimd.memset(identity[:], 0.0))
            chain.link(nc.gpsimd.affine_select(out=identity[:], in_=identity[:], compare_op=ALU.not_equal, fill=1.0,
                                               base=0, pattern=[[-1, P]], channel_multiplier=1))
            chain.link(nc.gpsimd.memset(wb_sb[:], 0.0))
            for f in range(2):
                pool.dma_start(wb_sb[f * C:(f + 1) * C, f * NH:(f + 1) * NH], wb.rearrange("h c -> c h"),
                               allow_slow_non_contiguous=True).then_inc(wb_in, 16)
            chain.link(nc.gpsimd.memset(ones[:], 1.0))
            chain.link(nc.gpsimd.memset(bg_f[:], 0.0))
            chain.link(nc.gpsimd.memset(w4l[:].bitcast(F32), 0.0))
            for p in range(2):
                chain.link(nc.gpsimd.memset(vh[p][:], 1.0))
                chain.link(nc.gpsimd.memset(vl[p][:], 0.0))
            for e in range(E):
                chain.link(nc.gpsimd.memset(order8[:, e:e + 1], float(E - e)))
            chain.link(nc.gpsimd.memset(before[:], 1.0))
            chain.link(nc.gpsimd.affine_select(out=before[:], in_=before[:], compare_op=ALU.is_gt, fill=0.0, base=0,
                                               pattern=[[1, P]], channel_multiplier=-1))
            for f in range(2):
                chain.link(nc.gpsimd.iota(token_id[f * C:(f + 1) * C, :], [[1, HALF]], base=f * HALF,
                                          channel_multiplier=H, allow_small_or_imprecise_dtypes=True))
            chain.link(nc.gpsimd.iota(tile_no[:], [[1, SLOT_TILES]], base=0, channel_multiplier=0,
                                      allow_small_or_imprecise_dtypes=True))
            chain.link(nc.gpsimd.memset(blank[:], 0.0))
            nc.gpsimd.memset(blank[:, W + 1:W + 2], float(NOWHERE)).then_inc(const_ready, 1)

            def copy_x1(u, p):
                if p == 0:
                    wait(pool, xs_ready, u)
                    nc.gpsimd.tensor_copy(xf[:].rearrange("p (r w) -> p r w", w=W), x1[:, rows(u, 0), :]).then_inc(xf_ready, 1)

            def low_x(u, p):
                hi = slice(p * C, (p + 1) * C)
                lo = slice((1 - p) * C, (2 - p) * C)
                pool.wait_ge(xs_high, u + 1)
                wait(pool, og_ready, 2 * (u - 2))
                nc.gpsimd.tensor_tensor(xs[p][lo], xf[hi], xs[p][hi], ALU.subtract).then_inc(xs_ready, 1)

            def gate(u, p, half):
                pool.wait_ge(norm_done, 2 * u + half + 1)
                if half == 0:
                    wait(pool, ogt_full, u - 1)
                    pool.wait_ge(xs_ready, min(u + 3, UNITS) if isinstance(u, int) else u + 3)
                k = slice(2 * half, 2 * half + 2)
                nc.gpsimd.tensor_tensor(og[p][:, k, :], gt[p][:, k, :], on[half][:], ALU.mult).then_inc(og_part, 1)
                pool.wait_ge(og_part, 2 * u + half + 1)
                nc.gpsimd.tensor_tensor(og[p][:, k, :], og[p][:, k, :], on[half][:], ALU.add).then_inc(og_ready, 1)

            def step(s, p):
                unit(s, p, 0, copy_x1)
                unit(s, p, 3, gate, 0)
                unit(s, p, 3, gate, 1)
                unit(s, p, 0, low_x)

            pool.wait_ge(x1_ready, CH)
            attention_steps(step, pool)

            pool.wait_ge(blanked, 32)

            def scatter_rows(k, i):
                pool.indirect_dma_start(routed[k], bass.IndirectOffsetOnAxis(ap=pos[k][:, i:i + 1], axis=0),
                                        pay[:, i, :], None).then_inc(scattered[k], 16)

            def send_rows(t, p, slot):
                pool.wait_ge(yidx_ready, t + 1)
                pool.wait_ge(y_ready, t + 1)
                last_place = TOKENS - 1 + t
                for k in range(2):
                    pool.indirect_dma_start(
                        expert_out[slot], bass.IndirectOffsetOnAxis(ap=yidx[p][:, k:k + 1], axis=0),
                        yo[p][:, k, :], None, bounds_check=last_place, oob_is_err=False).then_inc(y_sent[p], 16)

            pool.wait_ge(meta_ready, 1)
            for i in range(HALF):
                scatter_rows(0, i)
            pool.wait_ge(meta_ready, 2)
            due = [LEAD + (HALF - LEAD) * t // (SLOT_TILES - 8) for t in range(SLOT_TILES)]
            for t in range(SLOT_TILES):
                for i in range(due[t - 1] if t else 0, min(HALF, due[t])):
                    scatter_rows(1, i)
                send_rows(t, t % 2, 0)
            send_rows(SLOT_TILES, 1, 1)
            with pool.Fori((SLOT_TILES + 1) // 2, SLOT_TILES) as g:
                send_rows(2 * g, 0, 1)
                send_rows(2 * g + 1, 1, 1)

        @block.scalar
        def _(act):
            for c in range(CH):
                if c >= 2:
                    act.wait_ge(lnw_used, c - 1)
                for f in range(2):
                    act.dma_start(lnw_sb[f * C:(f + 1) * C, c % 2], lwv[f, :, chunk(c), :]).then_inc(lnw_in[c % 2], 16)
                if c < 2:
                    for f in range(2):
                        act.dma_start(lnb_sb[f * C:(f + 1) * C, c % 2], lbv[f, :, chunk(c), :]).then_inc(lnb_in[c % 2], 16)
            chain = Chain(act, act_step)
            act.wait_ge(w_in, 12 * 16)
            nc.scalar.activation(wrep_ordered[:].rearrange("o (h c) -> o h c", h=NH),
                                 wrep_raw[:].rearrange("o (c h) -> o h c", h=NH), ACT.Copy).then_inc(wrep_reordered, 1)
            for n in range(3):
                chain.link(nc.scalar.activation(square_junk[:, 0:C], wraw[:, n, 0, :], ACT.Square,
                                                accum_out=sums[:, n:n + 1]))
            for c in range(2, CH):
                act.wait_ge(lnw_used, c + 1)
                for f in range(2):
                    act.dma_start(lnb_at[c][f * C:(f + 1) * C], lbv[f, :, chunk(c), :]).then_inc(lnb_in[c % 2], 16)
            for c in range(CH):
                act.wait_ge(x1_ready, c + 1)
                for k in range(2 if c < CH // 2 else 0):
                    last = nc.scalar.activation(square_junk.rearrange("p (r w) -> p r w", w=W),
                                                x1[:, c * CR + k * CR // 2:c * CR + (k + 1) * CR // 2, :],
                                                ACT.Square, accum_out=xsq[:, 2 * c + k:2 * c + k + 1])
                    if c == CH // 2 - 1 and k == 1:
                        last.then_inc(squares_ready, 1)
                    else:
                        chain.link(last)
                for n in range(c * (CR // R), (c + 1) * (CR // R)):
                    act.wait_ge(bias_done, n + 1)
                    nc.scalar.activation(bias_rows[:, n * NQ:(n + 1) * NQ], S[n % 4][0:2 * NH, :], ACT.Copy).then_inc(bias_copied, 1)

            def high_x(u, p):
                act.wait_ge(xf_ready, (u - p) // 2 + 1)
                wait(act, vg_full, 2 * (u - 1))
                hi = slice(p * C, (p + 1) * C)
                nc.scalar.activation(xs[p][hi], xf[hi], ACT.Copy).then_inc(xs_high, 1)

            def high_qk(u, p, n):
                act.wait_ge(qk_full, 2 * u + n + 1)
                if n == 0:
                    wait(act, s_full, 2 * (u - 1))
                nc.scalar.activation(qk[n][0][p][:], A[:], ACT.Copy).then_inc(qk_high, 1)

            def gate_and_high_v(u, p, half):
                act.wait_ge(vg_full, 2 * u + half + 1)
                wait(act, og_ready, 2 * (u - 2) + half + 1)
                av = A[:].rearrange("p (r s c) -> p r s c", r=2, s=2)
                nc.scalar.activation(gt[p][:, 2 * half:2 * half + 2, :], av[:, :, 1, :], ACT.Tanh, scale=0.5)
                nc.scalar.activation(vh[p][:, 2 * half:2 * half + 2, :, 0:D],
                                     av[:, :, 0, :].rearrange("p r (h d) -> p r h d", d=D), ACT.Copy).then_inc(vg_high, 1)

            def high_p(u, p, i):
                act.wait_ge(pt_full, 4 * u + i + 1)
                wait(act, pv_done, 4 * u + i - 1)
                nc.scalar.activation(ph[i % 2][:], PT[i % 2][:], ACT.Copy).then_inc(ph_ready, 1)

            def exponentials(u, p, h):
                act.wait_ge(logits_ready, 4 * u + h + 1)
                for i in range(R):
                    last = nc.scalar.activation(L[p][:, h, i, :], L[p][:, h, i, :], ACT.Exp, scale=-1.0,
                                                bias=lmin[p][:, h * R + i:h * R + i + 1])
                last.then_inc(exp_done, 1)

            def high_og(u, p):
                act.wait_ge(ogt_full, u + 1)
                wait(act, oproj_done, u)
                nc.scalar.activation(ogT_h[:], B[:], ACT.Copy).then_inc(ogt_high, 1)

            def step(s, p):
                unit(s, p, 2, exponentials, 3)
                unit(s, p, 1, gate_and_high_v, 0)
                unit(s, p, 2, high_p, 0)
                unit(s, p, 0, high_x)
                unit(s, p, 2, high_p, 1)
                unit(s, p, 1, gate_and_high_v, 1)
                unit(s, p, 3, high_og)
                unit(s, p, 1, exponentials, 0)
                unit(s, p, 0, high_qk, 0)
                unit(s, p, 1, exponentials, 1)
                unit(s, p, 0, high_qk, 1)
                unit(s, p, 2, high_p, 2)
                unit(s, p, 2, high_p, 3)
                unit(s, p, 1, exponentials, 2)

            attention_steps(step, act)

            def stage_rows(g, p):
                act.wait_ge(xn_ready, g + 1)
                wait(act, stage_T, g - 1)
                nc.scalar.activation(stage[p][:], pay[:, bass.ds(g * R, R), 0:W], ACT.Copy).then_inc(staged, 1)

            def copy_transposed(g, p):
                act.wait_ge(stage_T, g + 1)
                wait(act, lg_full, g - 1)
                nc.scalar.activation(xnT[p][:], PT[p][:], ACT.Copy).then_inc(xnT_ready, 1)

            def copy_logits(g, p):
                act.wait_ge(lg_full, g + 1)
                wait(act, lg_T, g - 1)
                nc.scalar.activation(lgT[p], S[p][0:E, :], ACT.Copy).then_inc(lgT_ready, 1)

            def step(s, p):
                group(s, p, 0, stage_rows)
                group(s, p, 1, copy_transposed)
                group(s, p, 2, copy_logits)

            group_steps(act, step)
            act.wait_ge(gap_ready, 1)
            nc.scalar.activation(gate_e[:], key[:], ACT.Exp).then_inc(gate_exp, 1)

            act.wait_ge(ffn_in, 32)
            act.wait_ge(res_done, UNITS)
            for n in range(2):
                raw = w_raw[n][:].rearrange("p a r w -> p (a r w)")
                last = nc.scalar.activation(w_h[n][:].rearrange("p e b d -> p (e b d)"), raw, ACT.Square,
                                            accum_out=wsq[:, n:n + 1])
                if n == 0:
                    chain.link(last)
                else:
                    last.then_inc(wsq_ready, 1)

            act.wait_ge(hscale_ready, 1)
            for n in range(2):
                nc.scalar.activation(w_h[n][:].rearrange("p e b d -> p (e b d)"), w_raw[n][:].rearrange("p a r w -> p (a r w)"),
                                     ACT.Copy, scale=hscale[:, n:n + 1]).then_inc(w_high, 1)

            def tile_step(s, q, _=None):
                tokens, first, second, weighting = tile_stages(s)
                if tokens:
                    t, p = s + 1, 1 - q
                    act.wait_ge(fxT_full, t + 1)
                    nc.scalar.activation(fx_h[p][:], AB[p][:, 0:TILE], ACT.Copy).then_inc(fx_high, 1)
                if first:
                    t, p = s, q
                    e = expert_of(act, b1_at, s, HB)
                    for pair in range(2):
                        act.wait_ge(h_full, 2 * t + pair + 1)
                        for k in range(2):
                            b = 2 * pair + k
                            last = nc.scalar.activation(hf[p][:, b, :], S[2 * p + pair][:, k * TILE:(k + 1) * TILE], ACT.Gelu,
                                                        scale=inv_hscale[:, 0:1], bias=b1_flat[:, bass.ds(e + b, 1)])
                        last.then_inc(gelu_done, 1)
                if weighting:
                    t, p = s - 2, q
                    wait(act, y_sent[p], (t // 2) * 32 if isinstance(t, int) else (t - p) * 16)
                    act.wait_ge(y_full, t + 1)
                    for k in range(2):
                        last = nc.scalar.activation(yo[p][:, k, :], PT[p][:, k * P:(k + 1) * P], ACT.Copy,
                                                    scale=meta[:, tile_at(t), k, 0:1])
                    last.then_inc(y_ready, 1)

            act.wait_ge(table_ready, 2)
            act.wait_ge(small_in, 16 * (E + 3))
            tile_steps(act, tile_step)

        @block.vector
        def _(dve):
            chain = Chain(dve, dve_step)
            for c in range(CH):
                loaded = range(c, c + 1) if c < CH - 2 else range(c, CH) if c == CH - 2 else range(0)
                for n in loaded:
                    dve.wait_ge(x_in[n], 32)
                    last = row_statistics(n * CR, (n + 1) * CR)
                if loaded:
                    chain.link(last)
                    row_scales(chain, slice(loaded[0] * CR, (loaded[-1] + 1) * CR), 1e-6)
                k = chunk(c)
                for i in range(c * CR, (c + 1) * CR):
                    last = nc.vector.tensor_scalar(x1[:, i, :], xt[:, i, :], mean[:, i:i + 1], rstd[:, i:i + 1],
                                                   ALU.subtract, ALU.mult)
                chain.link(last)
                dve.wait_ge(lnw_in[c % 2], 32 * (c // 2 + 1))
                nc.vector.tensor_tensor(x1[:, k, :], x1[:, k, :], lnw_sb[:, c % 2], ALU.mult).then_inc(lnw_used, 1)
            chain.link(nc.vector.tensor_tensor(tmp_a[:], rstd[:], rstd[:], ALU.mult))
            chain.link(nc.vector.tensor_tensor(tmp_b[:], tmp_a[:], var[:], ALU.mult))
            nc.vector.tensor_reduce(gstat[:, 0:1], tmp_b[:], AX_X, ALU.add).then_inc(rowvar_ready, 1)
            dve.wait_ge(const_ready, 1)
            dve.wait_ge(w_in, 12 * 16)
            chain.link(nc.vector.tensor_copy(bg_f[0:1, :], bgrow[:]))
            chain.link(nc.vector.tensor_copy(bg_h[:], bg_f[:]))
            chain.link(nc.vector.tensor_tensor(bg_l[:], bg_f[:], bg_h[:], ALU.subtract))
            chain.link(nc.vector.tensor_copy(ones_r[:], ones[:]))
            dve.wait_ge(rowvar_summed, 1)
            chain.link(nc.vector.tensor_scalar(gstat[:, 1:2], B[:, 0:1], 1.0 / (P * HALF), 1e-5, ALU.mult, ALU.add))
            rsqrt(nc, chain, grstd[:], gstat[:, 1:2], gtmp[:, 0:1], gtmp2[:, 0:1])
            dve.wait_ge(lnw_used, CH)
            for c in range(CH):
                k = chunk(c)
                dve.wait_ge(lnb_in[c % 2], 32 * (c // 2 + 1))
                nc.vector.scalar_tensor_tensor(x1[:, k, :], x1[:, k, :], grstd[:, 0:1], lnb_at[c],
                                               ALU.mult, ALU.add).then_inc(x1_ready, 1)
            dve.wait_ge(x1_ready, CH)
            for k in range(CH, 2 * CH):
                half = x1[:, k * CR // 2:(k + 1) * CR // 2, :].rearrange("p r w -> p (r w)")
                chain.link(nc.vector.tensor_tensor_reduce(
                    dve_square_junk, half, half, scale=1.0, scalar=0.0, op0=ALU.mult, op1=ALU.add,
                    accum_out=xsq[:, k:k + 1]))
            dve.wait_ge(squares_ready, 1)
            nc.vector.tensor_reduce(sums[:, 3:4], xsq[:], AX_X, ALU.add).then_inc(sums_ready, 1)
            dve.wait_ge(squares_summed, 1)
            chain.link(nc.vector.tensor_copy(gstat[:, 0:4], B[:, 0:4]))
            chain.link(nc.vector.tensor_scalar(gstat[:, 4:7], gstat[:, 0:3], gstat[:, 3:4], 1e-30, ALU.mult, ALU.max))
            power_of_two(chain, scales[:, 0:3], gstat[:, 4:7], ebits[:, 0:3], ebits2[:, 0:3])
            chain.link(nc.vector.reciprocal(inv_scales[:, 0:3], scales[:, 0:3]))
            chain.link(nc.vector.tensor_scalar(bias_scale[:], scales[:, 0:1], scales[:, 1:2], float(D) ** 0.5, ALU.mult, ALU.mult))
            chain.link(nc.vector.tensor_scalar(logit_scale[:], inv_scales[:, 0:1], inv_scales[:, 1:2], -float(D) ** -0.5, ALU.mult, ALU.mult))
            dve.wait_ge(w_transposed, 1)
            for n in range(3):
                last = nc.vector.tensor_scalar(w4[:, n, :], PT[0][:, n * P:(n + 1) * P], scales[:, n:n + 1], None, ALU.mult)
            chain.link(nc.vector.tensor_copy(w4[:, 3, :], PT[0][:, 3 * P:4 * P]))
            chain.link(nc.vector.tensor_copy(w4h[:], w4[:]))
            for f in range(2):
                k = slice(f * C, (f + 1) * C)
                last = nc.vector.tensor_tensor(w4l[k, f], w4[k], w4h[k], ALU.subtract)
            chain.link(last)
            dve.wait_ge(wrep_transposed, 1)
            for f in range(2):
                last = nc.vector.tensor_scalar(wrepT[:, f * C:(f + 1) * C], PT[1][:, 0:C], inv_scales[:, 2:3], 0.5, ALU.mult, ALU.mult)
            chain.link(last)
            chain.link(nc.vector.tensor_copy(wrep_h[:], wrepT[:]))
            chain.link(nc.vector.tensor_tensor(wrep_l[:], wrepT[:], wrep_h[:], ALU.subtract))
            nc.vector.tensor_copy(turn[0][:], scales[:, 0:1]).then_inc(weights_ready, 1)

            def low_qk(u, p, n):
                dve.wait_ge(qk_high, 2 * u + n + 1)
                nc.vector.tensor_tensor(qk[n][1][p][:], A[:], qk[n][0][p][:], ALU.subtract).then_inc(qk_low, 1)
                if isinstance(u, int) and u == 0 and n == 1:
                    dve.wait_ge(bias_in, 2 * 2 * NH * 16)
                    chain.link(nc.vector.tensor_scalar(biasN[:], biasN[:], bias_scale[:, 0:1], None, ALU.mult))

            def low_v(u, p, half):
                dve.wait_ge(vg_high, 2 * u + half + 1)
                av = A[:].rearrange("p (r s c) -> p r s c", r=2, s=2)
                nc.vector.tensor_tensor(vl[p][:, 2 * half:2 * half + 2, :, 0:D],
                                        av[:, :, 0, :].rearrange("p r (h d) -> p r h d", d=D),
                                        vh[p][:, 2 * half:2 * half + 2, :, 0:D], ALU.subtract).then_inc(vg_low, 1)

            def low_p(u, p, i):
                dve.wait_ge(ph_ready, 4 * u + i + 1)
                nc.vector.tensor_tensor(pl[i % 2][:], PT[i % 2][:], ph[i % 2][:], ALU.subtract).then_inc(pl_ready, 1)

            def logits(u, p, h):
                if h % 2 == 0:
                    dve.wait_ge(s_full, 2 * u + h // 2 + 1)
                    if h == 0:
                        wait(dve, pt_full, 4 * (u - 1))
                    nc.vector.memset(turn[h // 2][:], 0.0)
                for i in range(R):
                    last = nc.vector.tensor_tensor_reduce(
                        out=L[p][:, h, i, :], in0=S[h][:, i * P:(i + 1) * P], in1=biasN[:, h, :],
                        scale=logit_scale[:, 0:1], scalar=BIG, op0=ALU.add, op1=ALU.min,
                        accum_out=lmin[p][:, h * R + i:h * R + i + 1])
                last.then_inc(logits_ready, 1)

            def normalise(u, p, half):
                dve.wait_ge(pv_done, 4 * u + 2 * half + 2)
                ov = B[:, 0:2 * NH * (D + 1)].rearrange("p (r h d) -> p r h d", r=2, h=NH)
                wait(dve, og_ready, 2 * u + half - 1)
                nc.vector.reciprocal(rden[half][:], ov[:, :, :, D]).then_inc(rden_ready, 1)
                dve.wait_ge(rden_ready, 2 * u + half + 1)
                nc.vector.tensor_tensor(on[half][:].rearrange("p r (h d) -> p r h d", d=D), ov[:, :, :, 0:D],
                                        rden[half][:].unsqueeze(3).broadcast_to([P, 2, NH, D]), ALU.mult).then_inc(norm_done, 1)

            def low_og(u, p):
                dve.wait_ge(ogt_high, u + 1)
                nc.vector.tensor_tensor(ogT_l[:], B[:], ogT_h[:], ALU.subtract).then_inc(ogt_low, 1)

            def residual(u, p):
                dve.wait_ge(oproj_done, u + 1)
                k = slice(p * C, (p + 1) * C)
                dst = xt[k, rows(u, p), :].rearrange("p r w -> p (r w)")
                nc.vector.scalar_tensor_tensor(dst, B[k, :], brep[k, 0:1], dst, ALU.add, ALU.add).then_inc(res_done, 1)

            def step(s, p):
                unit(s, p, 1, logits, 1)
                unit(s, p, 2, low_p, 0)
                unit(s, p, 2, low_p, 1)
                unit(s, p, 1, low_v, 1)
                unit(s, p, 3, low_og)
                unit(s, p, 1, logits, 2)
                unit(s, p, 0, low_qk, 0)
                unit(s, p, 3, residual)
                unit(s, p, 1, logits, 3)
                unit(s, p, 0, low_qk, 1)
                unit(s, p, 2, normalise, 0)
                unit(s, p, 2, low_p, 2)
                unit(s, p, 2, low_p, 3)
                unit(s, p, 0, logits, 0)
                unit(s, p, 2, normalise, 1)
                unit(s, p, 0, low_v, 0)

            def step_and_statistics(s, p):
                step(s, p)
                if isinstance(s, int) and UNITS <= s <= UNITS + 1:
                    complete = (s - 3 + 1) // 2 * R
                    dve.wait_ge(res_done, s - 2)
                    row_statistics(24 * (s - UNITS), min(24 * (s - UNITS + 1), complete))

            attention_steps(step_and_statistics, dve)
            row_statistics(48, HALF - R)
            dve.wait_ge(res_done, UNITS)
            chain.count = 0
            chain.sem = dve_step2

            chain.link(nc.vector.memset(pay[:, :, W + 2:ROW], 0.0))
            chain.link(row_statistics(HALF - R, HALF))
            row_scales(chain, slice(0, HALF), 1e-5)
            for i in range(HALF):
                last = nc.vector.tensor_scalar(pay[:, i, 0:W], xt[:, i, :], mean[:, i:i + 1], rstd[:, i:i + 1],
                                               ALU.subtract, ALU.mult)
                if i % R == R - 1:
                    last.then_inc(xn_ready, 1)
            dve.wait_ge(bgate_spread, 1)
            chain.link(nc.vector.tensor_copy(bgate_all[:], B[:, E:2 * E]))
            dve.wait_ge(lg_T, GROUPS)
            dve.wait_ge(const_ready, 1)
            rows_e = [P, HALF, E]
            spread = lambda v: v.unsqueeze(2).broadcast_to(rows_e)
            chain.link(nc.vector.tensor_tensor(lg[:], S[2][:].rearrange("p (i e) -> p i e", e=E),
                                                bgate_all[:].unsqueeze(1).broadcast_to(rows_e), ALU.add))
            for k in range(2):
                chain.link(nc.vector.tensor_reduce(top[k][:], lg[:], AX_X, ALU.max))
                chain.link(nc.vector.tensor_tensor(r_a[:], lg[:], spread(top[k][:]), ALU.is_equal))
                chain.link(nc.vector.tensor_tensor(r_b[:], r_a[:], order8[:].unsqueeze(1).broadcast_to(rows_e), ALU.mult))
                chain.link(nc.vector.tensor_reduce(key[:], r_b[:], AX_X, ALU.max))
                chain.link(nc.vector.tensor_tensor(oh[k][:], r_b[:], spread(key[:]), ALU.is_equal))
                if k == 0:
                    chain.link(nc.vector.scalar_tensor_tensor(lg[:], oh[0][:], -BIG, lg[:], ALU.mult, ALU.add))
            nc.vector.tensor_tensor(key[:], top[1][:], top[0][:], ALU.subtract).then_inc(gap_ready, 1)

            def route(k):
                src, dst, other = oh[k], r_b, picked
                step_rows = 1
                while step_rows < HALF:
                    nc.vector.tensor_copy(dst[:, 0:step_rows, :], src[:, 0:step_rows, :])
                    chain.link(nc.vector.tensor_tensor(dst[:, step_rows:, :], src[:, step_rows:, :], src[:, 0:HALF - step_rows, :], ALU.add))
                    src, dst, other = dst, other, dst
                    step_rows *= 2
                assert src is picked
                nc.vector.tensor_tensor(r_b[:], picked[:], oh[k][:], ALU.subtract).then_inc(totals_ready, 1)
                dve.wait_ge(totals_ready, k + 1)
                dve.wait_ge(totals_summed, 2 * k + 2)
                chain.link(nc.vector.tensor_copy(counts[:], B[:, 0:2 * E]))
                tf, tg, th = tiles_f
                chain.link(nc.vector.tensor_scalar(tiles_i[:], counts[:, E:2 * E], float(TILE - 1), None, ALU.add))
                chain.link(nc.vector.tensor_scalar(tiles_j[:], tiles_i[:], TILE.bit_length() - 1, None, ALU.arith_shift_right))
                chain.link(nc.vector.tensor_copy(tf[:], tiles_j[:]))
                a, b = tf, tg
                for d in (1, 2, 4):
                    nc.vector.tensor_copy(b[:, 0:d], a[:, 0:d])
                    chain.link(nc.vector.tensor_tensor(b[:, d:], a[:, d:], a[:, 0:E - d], ALU.add))
                    a, b = b, (th if a is tf else a)
                inclusive = a
                chain.link(nc.vector.tensor_tensor(first_row[:], inclusive[:], tf[:], ALU.subtract))
                chain.link(nc.vector.scalar_tensor_tensor(first_row2[:], first_row[:], float(TILE), counts[:, 0:E], ALU.mult, ALU.add))
                chain.link(nc.vector.tensor_tensor(r_b[:], r_b[:], first_row2[:].unsqueeze(1).broadcast_to(rows_e), ALU.add))
                chain.link(nc.vector.tensor_tensor(r_a[:], r_b[:], oh[k][:], ALU.mult))
                chain.link(nc.vector.tensor_reduce(posf[:], r_a[:], AX_X, ALU.add))
                chain.link(nc.vector.tensor_copy(pos[k][:], posf[:]))
                return inclusive

            def expert_table(k, inclusive):
                chain.link(nc.vector.memset(tile_expert[:], 0.0))
                for e in range(E - 1):
                    chain.link(nc.vector.tensor_scalar(tile_cmp[:], tile_no[:], inclusive[0:1, e:e + 1], None, ALU.is_ge))
                    chain.link(nc.vector.tensor_tensor(tile_expert[:], tile_expert[:], tile_cmp[:], ALU.add))
                mine = slice(k * SLOT_TILES, (k + 1) * SLOT_TILES)
                chain.link(nc.vector.tensor_scalar(w_at[:, mine], tile_expert[:], float(HID), None, ALU.mult))
                nc.vector.tensor_scalar(b1_at[:, mine], tile_expert[:], float(HB), None, ALU.mult).then_inc(table_ready, 1)
                dve.wait_ge(table_ready, k + 1)

            inclusive = route(0)
            dve.wait_ge(gate_exp, 1)
            chain.link(nc.vector.tensor_scalar(key[:], gate_e[:], 1.0, None, ALU.add))
            chain.link(nc.vector.reciprocal(weight[0][:], key[:]))
            chain.link(nc.vector.tensor_tensor(weight[1][:], gate_e[:], weight[0][:], ALU.mult))
            chain.link(nc.vector.tensor_copy(pay[:, :, W], weight[0][:]))
            nc.vector.tensor_copy(pay[:, :, W + 1], token_id[:]).then_inc(meta_ready, 1)
            expert_table(0, inclusive)
            expert_table(1, route(1))
            dve.wait_ge(wsq_summed, 1)
            chain.link(nc.vector.tensor_copy(gstat[:, 0:2], A[:, 0:2]))
            chain.link(nc.vector.tensor_scalar(gstat[:, 3:4], gstat[:, 0:1], float(4 * W), 1e-12, ALU.mult, ALU.add))
            chain.link(nc.vector.tensor_scalar(gstat[:, 4:6], gstat[:, 0:2], 1e-12, None, ALU.max))
            dve.wait_ge(small_in, 16 * (E + 3))
            chain.link(nc.vector.tensor_tensor(b1_sq[:], b1_sb[:].rearrange("p e b -> p (e b)"), b1_sb[:].rearrange("p e b -> p (e b)"), ALU.mult))
            nc.vector.tensor_reduce(b1_sum[:], b1_sq[:], AX_X, ALU.add).then_inc(b1_summing, 1)
            dve.wait_ge(b1_summed, 1)
            chain.link(nc.vector.scalar_tensor_tensor(gstat[:, 6:7], B[:, 0:1], 4.0, gstat[:, 3:4], ALU.mult, ALU.add))
            power_of_two(chain, hscale[:, 0:3], gstat[:, 4:7], ebits[:, 0:3], ebits2[:, 0:3])
            chain.link(nc.vector.reciprocal(inv_hscale[:, 0:3], hscale[:, 0:3]))
            nc.vector.tensor_scalar(y_scale[:], inv_hscale[:, 1:2], inv_hscale[:, 2:3], None, ALU.mult).then_inc(hscale_ready, 1)
            dve.wait_ge(hscale_ready, 1)
            chain.link(nc.vector.tensor_scalar(b2_row[:], b2_row[:], hscale[0:1, 1:2], hscale[0:1, 2:3], ALU.mult, ALU.mult))
            b2_e = b2_row[:].rearrange("o (e d) -> o e d", e=E)
            chain.link(nc.vector.tensor_copy(b2_parts[:, :, 0, :], b2_e))
            chain.link(nc.vector.tensor_tensor(b2_parts[:, :, 1, :], b2_e, b2_parts[:, :, 0, :], ALU.subtract))
            chain.link(nc.vector.tensor_copy(ones_x[:], ones[0:1, :]))
            for n in range(2):
                dve.wait_ge(w_high, n + 1)
                nc.vector.scalar_tensor_tensor(w_l[n][:].rearrange("p e b d -> p (e b d)"),
                                               w_raw[n][:].rearrange("p a r w -> p (a r w)"), hscale[:, n:n + 1],
                                               w_h[n][:].rearrange("p e b d -> p (e b d)"), ALU.mult, ALU.subtract).then_inc(w_split, 1)
            dve.wait_ge(scattered[0], 16 * HALF)
            nc.vector.tensor_copy(pay[:, :, W], weight[1][:]).then_inc(meta_ready, 1)

            def tile_step(s, q, _=None):
                tokens, first, second, weighting = tile_stages(s)
                if tokens:
                    t, p = s + 1, 1 - q
                    dve.wait_ge(fx_high, t + 1)
                    nc.vector.tensor_tensor(fx_l[p][:], AB[p][:, 0:TILE], fx_h[p][:], ALU.subtract).then_inc(fx_ready, 1)
                    nc.vector.tensor_copy(meta[:, tile_at(t), :, :], rows_in[p][:, :, W:W + 2].unsqueeze(1)).then_inc(meta_kept, 1)
                if weighting:
                    t, p = s - 2, q
                    wait(dve, y_sent[p], (t // 2) * 32 if isinstance(t, int) else (t - p) * 16)
                    dve.wait_ge(meta_kept, t + 1)
                    nc.vector.tensor_copy(yidx[p][:].unsqueeze(1), meta[:, tile_at(t), :, 1]).then_inc(yidx_ready, 1)
                if first:
                    t, p = s, q
                    for pair in range(2):
                        b = slice(2 * pair, 2 * pair + 2)
                        dve.wait_ge(gelu_done, 2 * t + pair + 1)
                        nc.vector.tensor_scalar(hh[p][:, b, :], hf[p][:, b, :], hscale[:, 2:3], None, ALU.mult).then_inc(hh_ready, 1)
                        dve.wait_ge(hh_ready, 2 * t + pair + 1)
                        nc.vector.scalar_tensor_tensor(hl[p][:, b, :], hf[p][:, b, :], hscale[:, 2:3], hh[p][:, b, :],
                                                       ALU.mult, ALU.subtract).then_inc(hl_ready, 1)

            dve.wait_ge(table_ready, 2)

            def add_first(g, j):
                if j == 0:
                    dve.wait_ge(y0_in, 32 * g + 32)
                k = bass.ds(g * CR + j * R, R)
                nc.vector.scalar_tensor_tensor(xt[:, k, :], shared[:, k, :], y_scale[:, 0:1], xt[:, k, :],
                                               ALU.mult, ALU.add).then_inc(y0_added, 1)

            tile_steps(dve, tile_step, add_first)

            dve.wait_ge(y0_added, HALF // R)
            for c in range(CH):
                dve.wait_ge(y_in[c], 32)
                nc.vector.scalar_tensor_tensor(xt[:, chunk(c), :], shared[:, chunk(c), :], y_scale[:, 0:1], xt[:, chunk(c), :],
                                               ALU.mult, ALU.add).then_inc(y_added, 1)

        @block.tensor
        def _(pe):
            pe.wait_ge(const_ready, 1)
            pe.wait_ge(w_in, 12 * 16)
            for n in range(4):
                last = nc.tensor.transpose(PT[0][:, n * P:(n + 1) * P], wraw[:, n].rearrange("o f c -> o (f c)"), identity[:])
            last.then_inc(w_transposed, 1)
            pe.wait_ge(wrep_reordered, 1)
            nc.tensor.transpose(PT[1][:, 0:C], wrep_ordered[:], identity[0:C, 0:C]).then_inc(wrep_transposed, 1)
            pe.wait_ge(rowvar_ready, 1)
            nc.tensor.matmul(B[:, 0:1], ones[:], gstat[:, 0:1], start=True, stop=True).then_inc(rowvar_summed, 1)
            pe.wait_ge(wb_in, 32)
            for n in range(HALF // R):
                if n % (CR // R) == 0:
                    pe.wait_ge(x1_ready, n // (CR // R) + 1)
                if n == HALF // R - 3:
                    pe.wait_ge(sums_ready, 1)
                    nc.tensor.matmul(B[:, 0:4], ones[:], sums[:, 0:4], start=True, stop=True).then_inc(squares_summed, 1)
                wait(pe, bias_copied, n - 3)
                nc.tensor.matmul(S[n % 4][0:2 * NH, :], wb_sb[:], x1[:, n * R:(n + 1) * R, :].rearrange("p r w -> p (r w)"),
                                 start=True, stop=True).then_inc(bias_done, 1)
            pe.wait_ge(weights_ready, 1)

            def project_qk(u, p, n):
                if n == 0:
                    wait(pe, vg_low, 2 * u)
                    pe.wait_ge(xs_ready, u + 1)
                else:
                    pe.wait_ge(qk_low, 2 * u + 1)
                nc.tensor.matmul(A[:], w4h[:, n, :], xs[p][:], start=True, stop=False)
                nc.tensor.matmul(A[:], w4l[:, p, n, :], xs[p][:], start=False, stop=True).then_inc(qk_full, 1)

            def project_vg(u, p, half):
                if half == 0:
                    pe.wait_ge(qk_low, 2 * u + 2)
                else:
                    pe.wait_ge(vg_low, 2 * u + 1)
                av = A[:].rearrange("p (r s c) -> p r s c", r=2, s=2)
                flags = dict(skip_group_check=True)
                for r in range(2):
                    i = 2 * half + r
                    xi = xs[p][:, i * P:(i + 1) * P]
                    nc.tensor.matmul(A[:, r * 256:(r + 1) * 256], xi, w4h[:, 2:4, :], start=r == 0, stop=False, **flags)
                    nc.tensor.matmul(A[:, r * 256:(r + 1) * 256], xi, w4l[:, p, 2:4, :], start=False, stop=False, **flags)
                for part in (bg_h, bg_l):
                    last = nc.tensor.matmul(av[:, :, 1, :], ones_r[:], part[:].unsqueeze(1).broadcast_to([P, 2, P]),
                                            start=False, stop=part is bg_l, **flags)
                last.then_inc(vg_full, 1)

            def scores(u, p, pair):
                if pair == 0:
                    pe.wait_ge(qk_low, 2 * u + 2)
                wait(pe, logits_ready, 4 * (u - 1) + 2 * pair + 2)
                (q_h, q_l), (k_h, k_l) = ([part[p] for part in qk[n]] for n in range(2))
                for i in range(R):
                    c = slice(i * P, (i + 1) * P)
                    for m, (a, b) in enumerate(((q_h, k_h), (q_h, k_l), (q_l, k_h))):
                        for h in (2 * pair, 2 * pair + 1):
                            d = slice(h * D, (h + 1) * D)
                            last = nc.tensor.matmul(S[h][:, c], a[d, c], b[d, c], start=m == 0, stop=m == 2)
                last.then_inc(s_full, 1)

            def transpose_p(u, p, i):
                if i == 0:
                    pe.wait_ge(exp_done, 4 * u + 4)
                wait(pe, pl_ready, 4 * u + i - 1)
                for h in range(NH):
                    last = nc.tensor.transpose(PT[i % 2][:, h * P:(h + 1) * P], L[p][:, h, i, :], identity[:])
                last.then_inc(pt_full, 1)

            def values(u, p, i):
                pe.wait_ge(pl_ready, 4 * u + i + 1)
                if i % 2 == 0:
                    pe.wait_ge(vg_low, 2 * u + i // 2 + 1)
                if i == 0:
                    wait(pe, res_done, u)
                if i == 2:
                    pe.wait_ge(norm_done, 2 * u + 1)
                for h in range(NH):
                    k = slice(h * P, (h + 1) * P)
                    o = ((i % 2) * NH + h) * (D + 1)
                    dst = B[:, o:o + D + 1]
                    nc.tensor.matmul(dst, ph[i % 2][:, k], vh[p][:, i, h, :], start=True, stop=False)
                    nc.tensor.matmul(dst, ph[i % 2][:, k], vl[p][:, i, h, :], start=False, stop=False)
                    last = nc.tensor.matmul(dst, pl[i % 2][:, k], vh[p][:, i, h, :], start=False, stop=True)
                last.then_inc(pv_done, 1)

            def transpose_og(u, p):
                pe.wait_ge(og_ready, 2 * u + 2)
                for i in range(R):
                    last = nc.tensor.transpose(B[:, i * P:(i + 1) * P], og[p][:, i, :], identity[:])
                last.then_inc(ogt_full, 1)

            def project_out(u, p):
                pe.wait_ge(ogt_low, u + 1)
                nc.tensor.matmul(B[:], wrep_h[:], ogT_h[:], start=True, stop=False)
                nc.tensor.matmul(B[:], wrep_h[:], ogT_l[:], start=False, stop=False)
                nc.tensor.matmul(B[:], wrep_l[:], ogT_h[:], start=False, stop=True).then_inc(oproj_done, 1)

            def step(s, p):
                unit(s, p, 0, project_qk, 0)
                unit(s, p, 2, transpose_p, 2)
                unit(s, p, 3, project_out)
                unit(s, p, 0, project_qk, 1)
                unit(s, p, 2, values, 0)
                unit(s, p, 2, transpose_p, 3)
                unit(s, p, 2, values, 1)
                unit(s, p, 0, scores, 0)
                unit(s, p, 2, values, 2)
                unit(s, p, 0, project_vg, 0)
                unit(s, p, 2, values, 3)
                unit(s, p, 1, transpose_p, 0)
                unit(s, p, 1, transpose_p, 1)
                unit(s, p, 0, project_vg, 1)
                unit(s, p, 2, transpose_og)
                unit(s, p, 0, scores, 1)

            attention_steps(step, pe)

            pe.wait_ge(res_done, UNITS)
            pe.wait_ge(small_in, 16 * (E + 3))
            nc.tensor.matmul(B[:, E:2 * E], ones[0:1, :], bgate_row[:], start=True, stop=True).then_inc(bgate_spread, 1)
            def transpose_rows(g, p):
                pe.wait_ge(staged, g + 1)
                wait(pe, xnT_ready, g - 1)
                for i in range(R):
                    last = nc.tensor.transpose(PT[p][:, i * P:(i + 1) * P], stage[p][:, i, :], identity[:])
                last.then_inc(stage_T, 1)

            def gate_logits(g, p):
                pe.wait_ge(xnT_ready, g + 1)
                wait(pe, lgT_ready, g - 1)
                nc.tensor.matmul(S[p][0:E, :], wg_sb[:], xnT[p][:], start=True, stop=True).then_inc(lg_full, 1)

            def transpose_logits(g, p):
                pe.wait_ge(lgT_ready, g + 1)
                for i in range(R):
                    last = nc.tensor.matmul(S[2][:, bass.ds(g * (R * E) + i * E, E)], lgT[p][:, i * P:(i + 1) * P],
                                            identity[0:E, 0:E], start=True, stop=True)
                last.then_inc(lg_T, 1)

            def step(s, p):
                group(s, p, 0, transpose_rows)
                group(s, p, 1, gate_logits)
                group(s, p, 2, transpose_logits)

            group_steps(pe, step)
            for k in range(2):
                pe.wait_ge(totals_ready, k + 1)
                nc.tensor.matmul(B[:, 0:E], before[:], picked[:, HALF - 1, :], start=True, stop=True).then_inc(totals_summed, 1)
                nc.tensor.matmul(B[:, E:2 * E], ones[:], picked[:, HALF - 1, :], start=True, stop=True).then_inc(totals_summed, 1)

            pe.wait_ge(wsq_ready, 1)
            nc.tensor.matmul(A[:, 0:2], ones[:], wsq[:], start=True, stop=True).then_inc(wsq_summed, 1)
            pe.wait_ge(b1_summing, 1)
            nc.tensor.matmul(B[:, 0:1], ones[:], b1_sum[:], start=True, stop=True).then_inc(b1_summed, 1)

            b2_flat = b2_parts[:].rearrange("o e b d -> o (e b d)")
            w1_h, w1_l, w2_h, w2_l = (w[:].rearrange("p e b d -> p (e b d)") for w in (w_h[0], w_l[0], w_h[1], w_l[1]))

            def tile_step(s, q, e_second=None):
                tokens, first, second, weighting = tile_stages(s)
                e_first = None
                if tokens:
                    t, p = s + 1, 1 - q
                    pe.wait_ge(rows_loaded[p], 16 * (t // 2 + 1) if isinstance(t, int) else (t - p) * 8 + 16)
                    for k in range(2):
                        last = nc.tensor.transpose(AB[p][:, k * P:(k + 1) * P], rows_in[p][:, k, 0:W], identity[:])
                    last.then_inc(fxT_full, 1)
                if first:
                    t, p = s, q
                    e_first = expert_of(pe, w_at, s, HID)
                    pe.wait_ge(fx_ready, t + 1)
                    for pair in range(2):
                        for k in range(2):
                            dst = S[2 * p + pair][:, k * TILE:(k + 1) * TILE]
                            block_at = bass.ds(e_first + (2 * pair + k) * P, P)
                            nc.tensor.matmul(dst, w1_h[:, block_at], fx_h[p][:], start=True, stop=False)
                            nc.tensor.matmul(dst, w1_h[:, block_at], fx_l[p][:], start=False, stop=False)
                            last = nc.tensor.matmul(dst, w1_l[:, block_at], fx_h[p][:], start=False, stop=True)
                        last.then_inc(h_full, 1)
                if second:
                    t, p = s - 1, 1 - q
                    if e_second is None:
                        e_second = expert_of(pe, w_at, s - 1, HID)
                    wait(pe, y_ready, t - 1)
                    for k in range(2):
                        nc.tensor.matmul(PT[p][:, 0:2 * P].rearrange("p (k d) -> p k d", k=2), ones_x[:],
                                         b2_flat[0:1, bass.ds(e_second + k * P, P)].unsqueeze(1).broadcast_to([1, 2, P]),
                                         start=k == 0, stop=False, skip_group_check=True)
                    pe.wait_ge(hl_ready, 2 * t + 2)
                    for b in range(HB):
                        block_at = bass.ds(e_second + b * P, P)
                        for h_part, w_part in ((hh, w2_h), (hl, w2_h), (hh, w2_l)):
                            for k in range(2):
                                last = nc.tensor.matmul(PT[p][:, k * P:(k + 1) * P], h_part[p][:, b, k * P:(k + 1) * P],
                                                        w_part[:, block_at], start=False,
                                                        stop=b == HB - 1 and w_part is w2_l, skip_group_check=True)
                    last.then_inc(y_full, 1)
                return e_first

            pe.wait_ge(table_ready, 2)
            pe.wait_ge(w_split, 2)
            tile_steps(pe, tile_step)


INPUTS = ["x", "L0_conv_ln_w", "L0_conv_ln_b", "L0_conv_wq", "L0_conv_wk", "L0_conv_wv", "L0_conv_wb", "L0_conv_wg_w",
          "L0_conv_wg_b", "L0_conv_wrep_w", "L0_conv_wrep_b", "L0_ffn_Wg", "L0_ffn_bg", "L0_ffn_W1", "L0_ffn_b1",
          "L0_ffn_W2", "L0_ffn_b2"]


def kernel(**inputs):
    import numpy as np
    import concourse.bacc as bacc
    from concourse.bass_utils import run_bass_kernel_spmd

    nc = bacc.Bacc("TRN2", target_bir_lowering=False, num_devices=1)
    arrays, args = {}, []
    for name in INPUTS:
        a = np.ascontiguousarray(inputs[name])
        arrays[f"in_{name}"] = a
        args.append(nc.dram_tensor(f"in_{name}", a.shape, mybir.dt.from_np(a.dtype), kind="ExternalInput").ap())
    out = nc.dram_tensor("out", list(inputs["x"].shape), F32, kind="ExternalOutput").ap()
    build(nc, *args, out)
    r = run_bass_kernel_spmd(nc, [arrays], core_ids=[0])
    return r.results[0]["out"]
```
